# Optimizing a Trainium2 kernel written in Bass

```python
import numpy as np
import jax
import jax.numpy as jnp

def _softmax(x, axis=-1):
    return jax.nn.softmax(x, axis=axis)

def _gelu(x):
    return jax.nn.gelu(x, approximate=True)

def _silu(x):
    return jax.nn.silu(x)

def _sigmoid(x):
    return jax.nn.sigmoid(x)

def _layernorm(x, axis=-1, eps=1e-05):
    m = jnp.mean(x, axis=axis, keepdims=True)
    v = jnp.var(x, axis=axis, keepdims=True)
    return (x - m) / jnp.sqrt(v + eps)

def _scatter_add(tgt, idx, src, axis=0):
    return tgt.at[idx].add(src)

def _segment_sum(src, seg, n):
    return jax.ops.segment_sum(src, seg, n)
kernel_name = 'mk_early_fusion_d2_tok_img768_r4_e4c958'

def setup_inputs(seed: int=0):
    np.random.seed(seed)
    _w = jnp.asarray

    def _rec_inputs():
        import jax
        import jax.numpy as jnp
        _rk = jax.random.key(seed)
        x = -0.000111679 + 0.999904 * jax.random.normal(jax.random.fold_in(_rk, 1), (16, 3, 96, 96), jnp.float32)
        txt = -1.55934e-10 + 0.999873 * jax.random.normal(jax.random.fold_in(_rk, 2), (16, 77, 192), jnp.float32)
        return (x, txt)
    x, txt = _rec_inputs()

    def _L0_tok_setup():
        import jax, jax.numpy as jnp
        import numpy as np
        PATCH = 10
        N_EMBD = 192
        EPS = 1e-05

        def _patchify(x, p):
            B, C, H, Wd = x.shape
            h_p, w_p = (H // p, Wd // p)
            x = x[:, :, :h_p * p, :w_p * p]
            x = x.reshape(B, C, h_p, p, w_p, p)
            x = x.transpose(0, 2, 4, 1, 3, 5)
            return x.reshape(B, h_p * w_p, C * p * p)
        key = jax.random.key(seed)
        k1, k2, k3 = jax.random.split(key, 3)
        B, C, H, W_img = (32, 3, 160, 160)
        x = jax.random.normal(k1, (B, C, H, W_img), dtype=jnp.float32)
        d_in = C * PATCH * PATCH
        W = jax.random.normal(k2, (N_EMBD, d_in), dtype=jnp.float32) / np.sqrt(d_in)
        b = jax.random.normal(k3, (N_EMBD,), dtype=jnp.float32) * 0.01
        cls = jnp.zeros((1, 1, N_EMBD), dtype=jnp.float32)
        gamma = jnp.ones((N_EMBD,), dtype=jnp.float32)
        beta = jnp.zeros((N_EMBD,), dtype=jnp.float32)
        return {'x': x, 'W': W, 'b': b, 'cls': cls, 'gamma': gamma, 'beta': beta}
    _L0_tok_all = _L0_tok_setup()
    _L0_tok_in = {k: v for k, v in _L0_tok_all.items() if k in ('W', 'b', 'cls', 'gamma', 'beta')}
    del _L0_tok_all

    def _L0_attn_setup():
        import jax, jax.numpy as jnp
        import numpy as np
        H = 192
        EPS = 1e-05

        def _layernorm(x, g, b):
            mu = jnp.mean(x, axis=-1, keepdims=True)
            var = jnp.var(x, axis=-1, keepdims=True)
            return (x - mu) * jax.lax.rsqrt(var + EPS) * g + b
        key = jax.random.key(seed)
        ks = jax.random.split(key, 12)
        B, T = (4, 512)
        s = 1.0 / np.sqrt(H)
        inp = {'hidden_states': jax.random.normal(ks[0], (B, T, H), dtype=jnp.float32), 'ln_gamma': jnp.ones((H,), jnp.float32), 'ln_beta': jnp.zeros((H,), jnp.float32), 'Wu_w': jax.random.normal(ks[1], (H, H), jnp.float32) * s, 'Wu_b': jnp.zeros((H,), jnp.float32), 'Wq_w': jax.random.normal(ks[2], (H, H), jnp.float32) * s, 'Wq_b': jnp.zeros((H,), jnp.float32), 'Wk_w': jax.random.normal(ks[3], (H, H), jnp.float32) * s, 'Wk_b': jnp.zeros((H,), jnp.float32), 'Wv_w': jax.random.normal(ks[4], (H, H), jnp.float32) * s, 'Wv_b': jnp.zeros((H,), jnp.float32), 'Wo_w': jax.random.normal(ks[5], (H, H), jnp.float32) * s, 'Wo_b': jnp.zeros((H,), jnp.float32)}
        return inp
    _L0_attn_all = _L0_attn_setup()
    _L0_attn_in = {k: v for k, v in _L0_attn_all.items() if k in ('ln_gamma', 'ln_beta', 'Wu_w', 'Wu_b', 'Wq_w', 'Wq_b', 'Wk_w', 'Wk_b', 'Wv_w', 'Wv_b', 'Wo_w', 'Wo_b')}
    del _L0_attn_all

    def _L0_ffn_setup():
        import jax, jax.numpy as jnp
        import numpy as np
        B, N, C, H, E = (8, 256, 192, 768, 4)
        key = jax.random.key(seed)
        ks = jax.random.split(key, 8)
        s_in = 1.0 / np.sqrt(C)
        s_h = 1.0 / np.sqrt(H)
        return {'x': jax.random.normal(ks[0], (B, N, C), dtype=jnp.float32), 'gate_w': jax.random.normal(ks[1], (C, E), dtype=jnp.float32) * 0.01, 'gate_b': jnp.zeros((E,), dtype=jnp.float32), 'gate_center': jnp.zeros((E,), dtype=jnp.float32), 'w1': jax.random.uniform(ks[2], (E, C, H), jnp.float32, -s_in, s_in), 'b1': jax.random.uniform(ks[3], (E, H), jnp.float32, -s_in, s_in), 'w2': jax.random.uniform(ks[4], (E, H, C), jnp.float32, -s_h, s_h), 'b2': jax.random.uniform(ks[5], (E, C), jnp.float32, -s_h, s_h)}
    _L0_ffn_all = _L0_ffn_setup()
    _L0_ffn_in = {k: v for k, v in _L0_ffn_all.items() if k in ('gate_w', 'gate_b', 'gate_center', 'w1', 'b1', 'w2', 'b2')}
    del _L0_ffn_all

    def _L1_attn_setup():
        import jax, jax.numpy as jnp
        import numpy as np
        B, T, C = (4, 512, 192)
        H, D = (12, 64)
        R = 64
        ROPE_THETA = 10000.0

        def _rope_cos_sin(t, d, dtype):
            inv_freq = 1.0 / ROPE_THETA ** (jnp.arange(0, d, 2, dtype=jnp.float32) / d)
            ang = jnp.arange(t, dtype=jnp.float32)[:, None] * inv_freq[None, :]
            ang = jnp.concatenate([ang, ang], axis=-1)
            return (jnp.cos(ang).astype(dtype), jnp.sin(ang).astype(dtype))

        def _apply_rope(q, cos, sin):
            d2 = q.shape[-1] // 2
            rot = jnp.concatenate([-q[..., d2:], q[..., :d2]], axis=-1)
            return q * cos + rot * sin
        key = jax.random.key(seed)
        ks = jax.random.split(key, 8)
        s = lambda fan_in: 1.0 / np.sqrt(fan_in)
        return {'x': jax.random.normal(ks[0], (B, T, C), jnp.float32), 'Wq': jax.random.normal(ks[1], (C, H * D), jnp.float32) * s(C), 'Wdown': jax.random.normal(ks[2], (C, R), jnp.float32) * s(C), 'ln_g': jnp.ones((R,), jnp.float32), 'ln_b': jnp.zeros((R,), jnp.float32), 'Wup': jax.random.normal(ks[3], (R, 2 * H * D), jnp.float32) * s(R), 'Wo': jax.random.normal(ks[4], (H * D, C), jnp.float32) * s(H * D), 'bo': jnp.zeros((C,), jnp.float32)}
    _L1_attn_all = _L1_attn_setup()
    _L1_attn_in = {k: v for k, v in _L1_attn_all.items() if k in ('Wq', 'Wdown', 'ln_g', 'ln_b', 'Wup', 'Wo', 'bo')}
    del _L1_attn_all

    def _L1_ffn_setup():
        import jax, jax.numpy as jnp
        import numpy as np
        E = 8
        TOP_K = 2
        CAP_RATIO = 1.2
        key = jax.random.key(seed)
        k1, k2, k3, k4 = jax.random.split(key, 4)
        B, L, D, H = (2, 512, 192, 512)
        x = jax.random.normal(k1, (B, L, D), dtype=jnp.float32)
        Wg = jax.random.normal(k2, (D, E), dtype=jnp.float32) * 0.02
        W1 = jax.random.normal(k3, (E, D, 2 * H), dtype=jnp.float32) * 0.02
        W2 = jax.random.normal(k4, (E, H, D), dtype=jnp.float32) * 0.02
        return {'x': x, 'Wg': Wg, 'W1': W1, 'W2': W2}
    _L1_ffn_all = _L1_ffn_setup()
    _L1_ffn_in = {k: v for k, v in _L1_ffn_all.items() if k in ('Wg', 'W1', 'W2')}
    del _L1_ffn_all
    return {'x': x, 'txt': txt, 'L0_tok_W': _L0_tok_in['W'], 'L0_tok_b': _L0_tok_in['b'], 'L0_tok_cls': _L0_tok_in['cls'], 'L0_tok_gamma': _L0_tok_in['gamma'], 'L0_tok_beta': _L0_tok_in['beta'], 'L0_attn_ln_gamma': _L0_attn_in['ln_gamma'], 'L0_attn_ln_beta': _L0_attn_in['ln_beta'], 'L0_attn_Wu_w': _L0_attn_in['Wu_w'], 'L0_attn_Wu_b': _L0_attn_in['Wu_b'], 'L0_attn_Wq_w': _L0_attn_in['Wq_w'], 'L0_attn_Wq_b': _L0_attn_in['Wq_b'], 'L0_attn_Wk_w': _L0_attn_in['Wk_w'], 'L0_attn_Wk_b': _L0_attn_in['Wk_b'], 'L0_attn_Wv_w': _L0_attn_in['Wv_w'], 'L0_attn_Wv_b': _L0_attn_in['Wv_b'], 'L0_attn_Wo_w': _L0_attn_in['Wo_w'], 'L0_attn_Wo_b': _L0_attn_in['Wo_b'], 'L0_ffn_gate_w': _L0_ffn_in['gate_w'], 'L0_ffn_gate_b': _L0_ffn_in['gate_b'], 'L0_ffn_gate_center': _L0_ffn_in['gate_center'], 'L0_ffn_w1': _L0_ffn_in['w1'], 'L0_ffn_b1': _L0_ffn_in['b1'], 'L0_ffn_w2': _L0_ffn_in['w2'], 'L0_ffn_b2': _L0_ffn_in['b2'], 'L1_attn_Wq': _L1_attn_in['Wq'], 'L1_attn_Wdown': _L1_attn_in['Wdown'], 'L1_attn_ln_g': _L1_attn_in['ln_g'], 'L1_attn_ln_b': _L1_attn_in['ln_b'], 'L1_attn_Wup': _L1_attn_in['Wup'], 'L1_attn_Wo': _L1_attn_in['Wo'], 'L1_attn_bo': _L1_attn_in['bo'], 'L1_ffn_Wg': _L1_ffn_in['Wg'], 'L1_ffn_W1': _L1_ffn_in['W1'], 'L1_ffn_W2': _L1_ffn_in['W2']}

def reference(x, txt, L0_tok_W, L0_tok_b, L0_tok_cls, L0_tok_gamma, L0_tok_beta, L0_attn_ln_gamma, L0_attn_ln_beta, L0_attn_Wu_w, L0_attn_Wu_b, L0_attn_Wq_w, L0_attn_Wq_b, L0_attn_Wk_w, L0_attn_Wk_b, L0_attn_Wv_w, L0_attn_Wv_b, L0_attn_Wo_w, L0_attn_Wo_b, L0_ffn_gate_w, L0_ffn_gate_b, L0_ffn_gate_center, L0_ffn_w1, L0_ffn_b1, L0_ffn_w2, L0_ffn_b2, L1_attn_Wq, L1_attn_Wdown, L1_attn_ln_g, L1_attn_ln_b, L1_attn_Wup, L1_attn_Wo, L1_attn_bo, L1_ffn_Wg, L1_ffn_W1, L1_ffn_W2):
    import jax
    import jax.numpy as jnp

    def _L0_tok_ref(x, W, b, cls, gamma, beta):
        import jax, jax.numpy as jnp
        import numpy as np
        PATCH = 10
        N_EMBD = 192
        EPS = 1e-05

        def _patchify(x, p):
            B, C, H, Wd = x.shape
            h_p, w_p = (H // p, Wd // p)
            x = x[:, :, :h_p * p, :w_p * p]
            x = x.reshape(B, C, h_p, p, w_p, p)
            x = x.transpose(0, 2, 4, 1, 3, 5)
            return x.reshape(B, h_p * w_p, C * p * p)
        B = x.shape[0]
        patches = _patchify(x, PATCH)
        tok = jnp.einsum('bnd,ed->bne', patches, W) + b
        cls_tok = jnp.broadcast_to(cls, (B, 1, N_EMBD))
        tok = jnp.concatenate([cls_tok, tok], axis=1)
        mean = tok.mean(-1, keepdims=True)
        var = tok.var(-1, keepdims=True)
        return (tok - mean) * jax.lax.rsqrt(var + EPS) * gamma + beta

    def _L0_attn_ref(hidden_states, ln_gamma, ln_beta, Wu_w, Wu_b, Wq_w, Wq_b, Wk_w, Wk_b, Wv_w, Wv_b, Wo_w, Wo_b):
        import jax, jax.numpy as jnp
        import numpy as np
        H = 192
        EPS = 1e-05

        def _layernorm(x, g, b):
            mu = jnp.mean(x, axis=-1, keepdims=True)
            var = jnp.var(x, axis=-1, keepdims=True)
            return (x - mu) * jax.lax.rsqrt(var + EPS) * g + b
        B, T, _ = hidden_states.shape
        x = _layernorm(hidden_states, ln_gamma, ln_beta)
        silu = jax.nn.silu
        U = silu(jnp.einsum('bth,dh->btd', x, Wu_w) + Wu_b)
        Q = silu(jnp.einsum('bth,dh->btd', x, Wq_w) + Wq_b)
        K = silu(jnp.einsum('bth,dh->btd', x, Wk_w) + Wk_b)
        V = silu(jnp.einsum('bth,dh->btd', x, Wv_w) + Wv_b)
        sim = jnp.einsum('bid,bjd->bij', Q, K) / jnp.sqrt(jnp.float32(T))
        A = jnp.square(jax.nn.relu(sim))
        AV = jnp.einsum('bij,bjd->bid', A, V)
        out = U * AV
        out = jnp.einsum('btd,hd->bth', out, Wo_w) + Wo_b
        return out

    def _L0_ffn_ref(x, gate_w, gate_b, gate_center, w1, b1, w2, b2):
        import jax, jax.numpy as jnp
        import numpy as np
        B, N, C, H, E = (8, 256, 192, 768, 4)
        b, n, c = x.shape
        scores = jnp.einsum('bnc,ce->bne', x, gate_w) + gate_b
        p_experts = jax.nn.softmax(scores - gate_center, axis=-1)
        expert = jnp.argmax(p_experts, axis=-1).reshape(-1)
        xt = x.reshape(-1, c)
        h = jax.nn.gelu(jnp.einsum('tc,ech->eth', xt, w1) + b1[:, None, :], approximate=False)
        out_all = jnp.einsum('eth,ehc->etc', h, w2) + b2[:, None, :]
        out = jnp.take_along_axis(out_all, expert[None, :, None], axis=0)[0]
        return out.reshape(b, n, c)

    def _L1_attn_ref(x, Wq, Wdown, ln_g, ln_b, Wup, Wo, bo):
        import jax, jax.numpy as jnp
        import numpy as np
        B, T, C = (4, 512, 192)
        H, D = (12, 64)
        R = 64
        ROPE_THETA = 10000.0

        def _rope_cos_sin(t, d, dtype):
            inv_freq = 1.0 / ROPE_THETA ** (jnp.arange(0, d, 2, dtype=jnp.float32) / d)
            ang = jnp.arange(t, dtype=jnp.float32)[:, None] * inv_freq[None, :]
            ang = jnp.concatenate([ang, ang], axis=-1)
            return (jnp.cos(ang).astype(dtype), jnp.sin(ang).astype(dtype))

        def _apply_rope(q, cos, sin):
            d2 = q.shape[-1] // 2
            rot = jnp.concatenate([-q[..., d2:], q[..., :d2]], axis=-1)
            return q * cos + rot * sin
        b, t, c = x.shape
        q = (x @ Wq).reshape(b, t, H, D).transpose(0, 2, 1, 3)
        ckv = x @ Wdown
        mu = jnp.mean(ckv, axis=-1, keepdims=True)
        var = jnp.var(ckv, axis=-1, keepdims=True)
        ckv = (ckv - mu) * jax.lax.rsqrt(var + 1e-05) * ln_g + ln_b
        kv = (ckv @ Wup).reshape(b, t, 2, H, D)
        k = kv[:, :, 0].transpose(0, 2, 1, 3)
        v = kv[:, :, 1].transpose(0, 2, 1, 3)
        cos, sin = _rope_cos_sin(t, D, x.dtype)
        q = _apply_rope(q, cos, sin)
        k = _apply_rope(k, cos, sin)
        wei = jnp.einsum('bhqd,bhkd->bhqk', q, k) * D ** (-0.5)
        causal = jnp.tril(jnp.ones((t, t), bool))
        wei = jnp.where(causal, wei, -jnp.inf)
        wei = jax.nn.softmax(wei, axis=-1)
        out = jnp.einsum('bhqk,bhkd->bhqd', wei, v)
        out = out.transpose(0, 2, 1, 3).reshape(b, t, H * D)
        return out @ Wo + bo

    def _L1_ffn_ref(x, Wg, W1, W2):
        import jax, jax.numpy as jnp
        import numpy as np
        E = 8
        TOP_K = 2
        CAP_RATIO = 1.2
        B, L, D = x.shape
        H = W2.shape[1]
        xf = x.reshape(-1, D)
        N = xf.shape[0]
        capacity = int(CAP_RATIO * N / E)
        logits = xf @ Wg
        scores, idx = jax.lax.top_k(logits, TOP_K)
        weights = jax.nn.softmax(scores, axis=-1)
        xpad = jnp.concatenate([xf, jnp.zeros((1, D), xf.dtype)], axis=0)
        wpad_zero = jnp.zeros((1,), weights.dtype)
        out = jnp.zeros((N, D), x.dtype)
        for k in range(TOP_K):
            ik = idx[:, k]
            onehot = ik[:, None] == jnp.arange(E)[None, :]
            pos = jnp.cumsum(onehot, axis=0) - 1
            posk = jnp.take_along_axis(pos, ik[:, None], axis=1)[:, 0]
            keep = posk < capacity
            buf = jnp.full((E, capacity), N, dtype=jnp.int32)
            buf = buf.at[ik, posk].set(jnp.arange(N, dtype=jnp.int32), mode='drop')
            xg = xpad[buf]
            h = jnp.einsum('ecd,edh->ech', xg, W1)
            act = h[..., :H] * jax.nn.silu(h[..., H:])
            ye = jnp.einsum('ech,ehd->ecd', act, W2)
            wk = jnp.where(keep, weights[:, k], 0.0)
            w_buf = jnp.concatenate([wk, wpad_zero])[buf]
            out = out.at[buf.reshape(-1)].add((w_buf[..., None] * ye).reshape(E * capacity, D), mode='drop')
        return out.reshape(B, L, D)
    h = _L0_tok_ref(x, L0_tok_W, L0_tok_b, L0_tok_cls, L0_tok_gamma, L0_tok_beta)
    h = jnp.concatenate([h, txt], axis=1)
    h = h + _L0_attn_ref(_layernorm(h, axis=-1), L0_attn_ln_gamma, L0_attn_ln_beta, L0_attn_Wu_w, L0_attn_Wu_b, L0_attn_Wq_w, L0_attn_Wq_b, L0_attn_Wk_w, L0_attn_Wk_b, L0_attn_Wv_w, L0_attn_Wv_b, L0_attn_Wo_w, L0_attn_Wo_b)
    h = h + _L0_ffn_ref(_layernorm(h, axis=-1), L0_ffn_gate_w, L0_ffn_gate_b, L0_ffn_gate_center, L0_ffn_w1, L0_ffn_b1, L0_ffn_w2, L0_ffn_b2)
    h = h + _L1_attn_ref(_layernorm(h, axis=-1), L1_attn_Wq, L1_attn_Wdown, L1_attn_ln_g, L1_attn_ln_b, L1_attn_Wup, L1_attn_Wo, L1_attn_bo)
    h = h + _L1_ffn_ref(_layernorm(h, axis=-1), L1_ffn_Wg, L1_ffn_W1, L1_ffn_W2)
    return h

_drawn_inputs = setup_inputs


def setup_inputs(seed=0):
    import zlib

    import numpy as np

    out = dict(_drawn_inputs(seed))
    spreads = {'L0_tok_cls': (0.0, 0.1),
     'L0_tok_gamma': (1.0, 0.2),
     'L0_tok_beta': (0.0, 0.1),
     'L0_attn_ln_gamma': (1.0, 0.2),
     'L0_attn_ln_beta': (0.0, 0.1),
     'L0_attn_Wu_b': (0.0, 0.1),
     'L0_attn_Wq_b': (0.0, 0.1),
     'L0_attn_Wk_b': (0.0, 0.1),
     'L0_attn_Wv_b': (0.0, 0.1),
     'L0_attn_Wo_b': (0.0, 0.8),
     'L0_ffn_gate_b': (0.0, 0.8),
     'L0_ffn_gate_center': (0.0, 0.8),
     'L1_attn_ln_g': (1.0, 0.6),
     'L1_attn_ln_b': (0.0, 0.8),
     'L1_attn_bo': (0.0, 0.8)}
    factors = {'L0_tok_b': 3.725,
     'L0_ffn_gate_w': 8.0,
     'L0_ffn_w1': 6.323,
     'L0_ffn_b1': 8.0,
     'L0_ffn_w2': 5.997,
     'L0_ffn_b2': 8.0,
     'L1_attn_Wq': 5.944,
     'L1_ffn_Wg': 8.0,
     'L1_ffn_W1': 8.0,
     'L1_ffn_W2': 8.0}
    for name, (base, spread) in spreads.items():
        noise = np.random.default_rng([zlib.crc32(name.encode()), seed]).standard_normal(out[name].shape)
        drawn = base * np.exp(spread * noise) if base else spread * noise
        out[name] = jnp.asarray(drawn.astype(out[name].dtype))
    for name, factor in factors.items():
        out[name] = (out[name] * factor).astype(out[name].dtype)
    return out
```

```python
from contextlib import ExitStack

import numpy as np

import concourse.bass as bass
from concourse import mybir

F32 = mybir.dt.float32
BF16 = mybir.dt.bfloat16
I32 = mybir.dt.int32
U32 = mybir.dt.uint32
ALU = mybir.AluOpType
ACT = mybir.ActivationFunctionType
AX = mybir.AxisListType

B = 16
PATCH = 10
GRID = 96 // PATCH
IMG = GRID * GRID + 1
TXT = 77
T = IMG + TXT
D = 192
N = B * T
EPS = 1e-5
HB = T // 2 + 1
SEQ = 2 * HB
TILES = -(-N // 128)
NP = TILES * 128
KP = 112
DC = D // 2

E0, H0 = 4, 768
TILES0 = (NP + E0 * 127) // 128
TILES0 += TILES0 % 2
FILL = 12
ROWS0 = -(-(E0 * NP + TILES0 * 128) // (FILL * 128)) * FILL * 128
E1, H1 = 8, 512
CAP = int(1.2 * N / E1)
CAPT = -(-CAP // 128)
CAPR = CAPT * 128
ROWS1 = E1 * 2 * CAPR
RW = D + 4
NOWHERE = 1 << 20

HEADS, HD, RANK = 12, 64, 64


START = 8


def primed_semaphores(nc, used):
    engines = [nc.sync, nc.scalar, nc.vector, nc.gpsimd, nc.tensor]

    def sem(name):
        s = nc.alloc_semaphore(name)
        engines[len(used) % len(engines)].sem_inc(s, START)
        used.append(s)
        return s

    return sem


def unprimed_semaphore(nc, used, name):
    s = nc.alloc_semaphore(name)
    used.append(s)
    return s


def clear_semaphores(nc, used):
    nc.clear_and_free_semaphores(used)
    used.clear()
    nc.all_engine_barrier()


def rows_of(dram, b):
    return dram[bass.ds(b * T, SEQ), :].rearrange("(t p) c -> p t c", p=HB)


def embed_patches(nc, used, w, dram, const):
    with ExitStack() as ctx:
        def sb(name, shape, dt=F32):
            return ctx.enter_context(nc.sbuf_tensor(name, shape, dt))

        sem = primed_semaphores(nc, used)

        bank = [ctx.enter_context(nc.psum_tensor(f"tok_bank{i}", [128, 512], F32)) for i in range(2)]
        zeros = sb("pad_zeros", [NP - N, D])
        tok_w = sb("tok_w", [KP, 3, D])
        gamma = sb("tok_gamma", [IMG, D])
        beta = sb("tok_beta", [IMG, D])
        minus_half = sb("tok_minus_half", [IMG, 1])
        patches = [sb(f"patches{i}", [KP, 3 * IMG]) for i in range(2)]
        stats = [sb(f"tok_stats{i}", [IMG, 6]) for i in range(2)]
        mv = [sb(f"tok_mv{i}", [IMG, 2]) for i in range(2)]
        ve = [sb(f"tok_ve{i}", [IMG, 1]) for i in range(2)]
        rstd = [sb(f"tok_rstd{i}", [IMG, 1]) for i in range(2)]
        y = [sb(f"tok_y{i}", [IMG, D]) for i in range(2)]

        weights_in = sem("tok_weights_in")
        patches_in = [sem(f"patches_in{i}") for i in range(2)]
        const_in = sem("const_in")
        fill_ready = sem("fill_ready")
        filled = sem("filled")
        tok_ps = sem("tok_ps")
        stats_done = sem("tok_stats_done")
        mv_done = sem("tok_mv_done")
        ve_done = sem("tok_ve_done")
        rstd_done = sem("tok_rstd_done")
        centred = sem("tok_centred")
        scaled = sem("tok_scaled")
        y_done = sem("tok_y_done")
        stored = [sem(f"tok_stored{i}") for i in range(2)]
        vector_step = sem("tok_vector_step")
        block = ctx.enter_context(nc.Block())

        @block.sync
        def _(sp):
            sp.dma_start(tok_w[:, :, :], w["tok_w"].rearrange("p (c n) -> p c n", c=3)).then_inc(weights_in, 16)
            sp.dma_start(gamma[:, :], w["tok_gamma"]).then_inc(weights_in, 16)
            sp.dma_start(beta[:, :], w["tok_beta"]).then_inc(weights_in, 16)
            with sp.Fori(0, B // 2) as i:
                for p in range(2):
                    b = 2 * i + p
                    sp.wait_ge(tok_ps, START + 2 * i)
                    sp.dma_start(patches[p][:, :], w["patches"][bass.ds(b, 1), :, :].rearrange("a p n -> (a p) n")
                                 ).then_inc(patches_in[p], 16)
                for p in range(2):
                    b = 2 * i + p
                    sp.wait_ge(y_done, START + b + 1)
                    sp.dma_start(dram["h0"][bass.ds(b * T, IMG), :], y[p][:, :]).then_inc(stored[p], 16)
            for p in range(2):
                sp.wait_ge(stored[p], START + 16 * (B // 2))
            sp.wait_ge(const_in, START + 16 * len(const))

        @block.scalar
        def _(act):
            for name, tile in const.items():
                act.dma_start(tile, w[name]).then_inc(const_in, 16)
            act.dma_start(dram["h0"][0:N, :].rearrange("(b t) c -> b t c", t=T)[:, IMG:T, :], w["txt"]
                          ).then_inc(filled, 16)
            act.wait_ge(fill_ready, START + 1)
            act.dma_start(dram["h0"][N:N + 1, :], zeros[0:1, :]).then_inc(filled, 16)
            act.dma_start(dram["h1"][N:NP, :], zeros[:, :]).then_inc(filled, 16)
            act.dma_start(dram["h3"][N:NP, :], zeros[:, :]).then_inc(filled, 16)
            act.wait_ge(filled, START + 16 * 4)

        @block.gpsimd
        def _(pool):
            pool.memset(zeros[:, :], 0.0).then_inc(fill_ready, 1)
            pool.memset(minus_half[:, :], -0.5).then_inc(fill_ready, 1)
            pool.wait_ge(fill_ready, START + 2)
            with pool.Fori(0, B // 2) as i:
                for p in range(2):
                    b = 2 * i + p
                    pool.wait_ge(ve_done, START + b + 1)
                    pool.tensor_tensor(rstd[p][:, :], ve[p][:, :], minus_half[:, :], ALU.pow).then_inc(rstd_done, 1)

        @block.tensor
        def _(pe):
            pe.wait_ge(weights_in, START + 48)
            with pe.Fori(0, B // 2) as i:
                for p in range(2):
                    pe.wait_ge(centred, START + 2 * i)
                    pe.wait_ge(patches_in[p], START + 16 * (i + 1))
                    for c in range(3):
                        mm = pe.matmul(bank[p][0:IMG, 0:D], patches[p][:, c * IMG:(c + 1) * IMG], tok_w[:, c, :],
                                       start=(c == 0), stop=(c == 2))
                    mm.then_inc(tok_ps, 1)

        @block.vector
        def _(dve):
            dve.wait_ge(weights_in, START + 48)
            with dve.Fori(0, B // 2) as i:
                for p in range(2):
                    dve.wait_ge(tok_ps, START + 2 * i + p + 1)
                    dve.bn_stats(stats[p][:, :], bank[p][0:IMG, 0:D]).then_inc(stats_done, 1)
                for p in range(2):
                    dve.wait_ge(stats_done, START + 2 * i + p + 1)
                    dve.sem_inc(vector_step, 1)
                    dve.bn_aggr(mv[p][:, :], stats[p][:, :]).then_inc(mv_done, 1)
                for p in range(2):
                    dve.wait_ge(mv_done, START + 2 * i + p + 1)
                    dve.tensor_scalar(ve[p][:, :], mv[p][:, 1:2], EPS, None, ALU.add).then_inc(ve_done, 1)
                for p in range(2):
                    dve.wait_ge(stored[p], START + 16 * i)
                    dve.wait_ge(rstd_done, START + 2 * i + p + 1)
                    dve.tensor_scalar(y[p][:, :], bank[p][0:IMG, 0:D], mv[p][:, 0:1], rstd[p][:, 0:1],
                                      ALU.subtract, ALU.mult).then_inc(centred, 1)
                for p in range(2):
                    dve.wait_ge(centred, START + 2 * i + p + 1)
                    dve.tensor_tensor(y[p][:, :], y[p][:, :], gamma[:, :], ALU.mult).then_inc(scaled, 1)
                for p in range(2):
                    dve.wait_ge(scaled, START + 2 * i + p + 1)
                    dve.tensor_tensor(y[p][:, :], y[p][:, :], beta[:, :], ALU.add).then_inc(y_done, 1)


def attend_squared(nc, used, w, dram, const):
    with ExitStack() as ctx:
        def sb(name, shape, dt=F32):
            return ctx.enter_context(nc.sbuf_tensor(name, shape, dt))

        sem = primed_semaphores(nc, used)

        bank = [ctx.enter_context(nc.psum_tensor(f"a_bank{i}", [128, 512], F32)) for i in range(8)]
        w_raw = sb("w_raw", [DC, 2, 4 * D])
        w_all = sb("w_all", [DC + 1, 2, 4 * D])
        b_all = sb("b_all", [1, 4 * D])
        ln_gb = sb("ln_gb", [DC, 2, 2])
        wo = sb("wo0", [DC + 1, 2, D])
        minus_half = sb("a_minus_half", [HB, 2])
        empty_rows = sb("empty_rows", [128, FILL, RW])
        zeros = sb("zeros", [128, 1920])
        h_norm = [sb(f"h_norm{i}", [HB, 2, D]) for i in range(2)]
        h_res = [sb(f"h_res{i}", [HB, 2, D]) for i in range(2)]
        stats = [sb(f"a_stats{i}", [HB, 2, 6]) for i in range(2)]
        mv = [sb(f"a_mv{i}", [HB, 2, 2]) for i in range(2)]
        ve = [sb(f"a_ve{i}", [HB, 2]) for i in range(2)]
        rstd = [sb(f"a_rstd{i}", [HB, 2]) for i in range(2)]
        z = [sb(f"a_z{i}", [HB, 2, D]) for i in range(2)]
        zT = [sb(f"a_zT{i}", [DC + 1, 2, SEQ]) for i in range(2)]
        uT = [sb(f"a_uT{i}", [DC, 2, SEQ]) for i in range(2)]
        qT = [sb(f"a_qT{i}", [DC, 2, SEQ]) for i in range(2)]
        kT = [sb(f"a_kT{i}", [DC, 2, SEQ]) for i in range(2)]
        v = [sb(f"a_v{i}", [HB, 2, D]) for i in range(2)]
        relu = [sb(f"a_relu{i}", [HB, 2, SEQ]) for i in range(2)]
        aT = [sb(f"a_aT{i}", [HB, 2, SEQ]) for i in range(2)]
        gT = [sb(f"a_gT{i}", [DC + 1, 2, SEQ]) for i in range(2)]
        h1 = [sb(f"a_h1_{i}", [HB, 2, D]) for i in range(2)]
        ident = const["ident"]
        U, Q, K, V = range(4)

        weights_in = sem("a_weights_in")
        norm_in = [sem(f"h_norm_in{i}") for i in range(2)]
        res_in = [sem(f"h_res_in{i}") for i in range(2)]
        gamma_done = sem("gamma_done")
        bias_ps = sem("bias_ps")
        w_ready = sem("a_w_ready")
        consts = sem("a_consts")
        fill_ready = sem("a_fill_ready")
        filled = sem("a_filled")
        stats_done = sem("a_stats_done")
        mv_done = sem("a_mv_done")
        ve_done = sem("a_ve_done")
        rstd_done = sem("a_rstd_done")
        z_done = sem("a_z_done")
        zT_ps = sem("a_zT_ps")
        zT_done = sem("a_zT_done")
        proj_ps = sem("a_proj_ps")
        silu_done = sem("a_silu_done")
        sim_ps = sem("a_sim_ps")
        relu_done = sem("a_relu_done")
        aT_done = sem("a_aT_done")
        av_ps = sem("a_av_ps")
        gT_done = sem("a_gT_done")
        wo_ps = sem("a_wo_ps")
        h1_done = sem("a_h1_done")
        stored = [sem(f"a_stored{i}") for i in range(2)]
        vector_step = sem("a_vector_step")
        block = ctx.enter_context(nc.Block())
        PAIRS = B // 2

        @block.sync
        def _(sp):
            sp.dma_start(w_raw[:, :, :], w["attn0_w"].rearrange("(c p) n -> p c n", c=2)).then_inc(weights_in, 16)
            sp.dma_start(b_all[:, :], w["attn0_b"]).then_inc(weights_in, 16)
            sp.dma_start(ln_gb[:, :, :], w["attn0_ln"].rearrange("(c p) n -> p c n", c=2)).then_inc(weights_in, 16)
            sp.dma_start(wo[0:DC, :, :], w["attn0_wo"].rearrange("(c p) n -> p c n", c=2)).then_inc(weights_in, 16)
            sp.dma_start(wo[DC:DC + 1, 0, :], w["attn0_bo"]).then_inc(weights_in, 16)

            def load(i):
                for p in range(2):
                    sp.wait_ge(z_done, START + 4 * i)
                    sp.dma_start(h_norm[p][:, :, :], rows_of(dram["h0"], 2 * i + p)).then_inc(norm_in[p], 16)
                for p in range(2):
                    sp.wait_ge(h1_done, START + 2 * i)
                    sp.dma_start(h_res[p][:, :, :], rows_of(dram["h0"], 2 * i + p)).then_inc(res_in[p], 16)

            def store(i):
                for p in range(2):
                    b = 2 * i + p
                    sp.wait_ge(h1_done, START + b + 1)
                    sp.dma_start(dram["h1"][bass.ds(b * T, HB), :], h1[p][:, 0, :]).then_inc(stored[p], 16)
                    sp.dma_start(dram["h1"][bass.ds(b * T + HB, T - HB), :], h1[p][0:T - HB, 1, :]
                                 ).then_inc(stored[p], 16)

            load(0)
            with sp.Fori(0, PAIRS - 1) as i:
                load(i + 1)
                store(i)
            store(PAIRS - 1)
            for p in range(2):
                sp.wait_ge(stored[p], START + 32 * PAIRS)

        @block.gpsimd
        def _(pool):
            pool.memset(minus_half[:, :], -0.5).then_inc(consts, 1)
            pool.memset(empty_rows[:, :, 0:D + 2], 0.0).then_inc(fill_ready, 1)
            pool.memset(empty_rows[:, :, D + 2:RW].bitcast(I32), NOWHERE).then_inc(fill_ready, 1)
            pool.memset(zeros[:, :], 0.0).then_inc(fill_ready, 1)
            pool.wait_ge(fill_ready, START + 3)
            for p in range(2):
                pool.memset(zT[p][DC:DC + 1, :, :], 1.0).then_inc(consts, 1)
                pool.memset(gT[p][DC:DC + 1, :, :], 1.0).then_inc(consts, 1)
            pool.wait_ge(consts, START + 5)

            def scales(i):
                for p in range(2):
                    pool.wait_ge(ve_done, START + 2 * i + p + 1)
                    pool.tensor_tensor(rstd[p][:, :], ve[p][:, :], minus_half[:, :], ALU.pow).then_inc(rstd_done, 1)

            def squares(i):
                for p in range(2):
                    b = 2 * i + p
                    pool.wait_ge(av_ps, START + 2 * i)
                    pool.wait_ge(relu_done, START + b + 1)
                    pool.tensor_tensor(aT[p][:, :, :], relu[p][:, :, :], relu[p][:, :, :], ALU.mult
                                       ).then_inc(aT_done, 1)

            scales(0)
            with pool.Fori(0, PAIRS - 1) as i:
                scales(i + 1)
                squares(i)
            squares(PAIRS - 1)

        @block.scalar
        def _(act):
            def copy_zT(i):
                for p in range(2):
                    act.wait_ge(proj_ps, START + 8 * i)
                    act.wait_ge(zT_ps, START + 2 * i + p + 1)
                    act.activation(zT[p][0:DC, :, :], bank[0][0:DC, 0:2 * SEQ].rearrange("p (c n) -> p c n", c=2),
                                   ACT.Copy).then_inc(zT_done, 1)

            def body(i):
                for p in range(2):
                    b = 2 * i + p
                    act.wait_ge(av_ps, START + 2 * i)
                    act.wait_ge(gT_done, START + 2 * i)
                    for n, (bk, tile) in enumerate(((1, qT), (2, kT), (3, v), (4, uT))):
                        act.wait_ge(proj_ps, START + 4 * b + n + 1)
                        rows, width = (HB, D) if tile is v else (DC, SEQ)
                        act.activation(tile[p][:, :, :],
                                       bank[bk][0:rows, 0:2 * width].rearrange("p (c n) -> p c n", c=2),
                                       ACT.Silu).then_inc(silu_done, 1)
                for p in range(2):
                    b = 2 * i + p
                    act.wait_ge(aT_done, START + 2 * i)
                    act.wait_ge(sim_ps, START + b + 1)
                    act.activation(relu[p][:, :, :], bank[5][0:HB, 0:2 * SEQ].rearrange("p (c n) -> p c n", c=2),
                                   ACT.Relu, scale=float(T) ** -0.5).then_inc(relu_done, 1)

            copy_zT(0)
            act.wait_ge(fill_ready, START + 3)
            n = 0
            for name, rows in (("slots0", ROWS0), ("slots1", ROWS1)):
                for r in range(0, rows, FILL * 128):
                    act.dma_start(dram[name][r:r + FILL * 128, :].rearrange("(p j) c -> p j c", j=FILL),
                                  empty_rows[:, :, :]).then_inc(filled, 16)
                    n += 1
            for r in range(0, 2 * NP, 1280):
                act.dma_start(dram["y1"][r:r + 1280, :].rearrange("(p j) c -> p (j c)", j=10),
                              zeros[:, :]).then_inc(filled, 16)
                n += 1
            with act.Fori(0, PAIRS - 1) as i:
                body(i)
                copy_zT(i + 1)
            body(PAIRS - 1)
            act.wait_ge(filled, START + 16 * n)

        @block.tensor
        def _(pe):
            pe.wait_ge(weights_in, START + 80)
            for half in range(2):
                for c in range(2):
                    mm = pe.matmul(bank[1 + half][0:1, 0:2 * D], ln_gb[:, c, 1:2],
                                   w_raw[:, c, half * 2 * D:(half + 1) * 2 * D], start=(c == 0), stop=(c == 1))
            mm.then_inc(bias_ps, 1)
            pe.wait_ge(w_ready, START + 2 + 2)
            pe.wait_ge(consts, START + 5)

            def transposes(i):
                for p in range(2):
                    b = 2 * i + p
                    pe.wait_ge(zT_done, START + b)
                    pe.wait_ge(z_done, START + 2 * b + 2)
                    for t in range(2):
                        for c in range(2):
                            mm = pe.transpose(bank[0][0:DC, c * SEQ + t * HB:c * SEQ + (t + 1) * HB],
                                              z[p][:, t, c * DC:(c + 1) * DC], ident[0:HB, 0:HB])
                    mm.then_inc(zT_ps, 1)

            def projections(i):
                for p in range(2):
                    b = 2 * i + p
                    pe.wait_ge(silu_done, START + 4 * b)
                    pe.wait_ge(zT_done, START + b + 1)
                    for bk, kind in ((1, Q), (2, K), (3, V), (4, U)):
                        for half in range(2):
                            for c in range(2):
                                rows = DC + 1 if c == 0 else DC
                                if kind == V:
                                    mm = pe.matmul(bank[bk][0:HB, half * D:(half + 1) * D],
                                                   zT[p][0:rows, c, half * HB:(half + 1) * HB],
                                                   w_all[0:rows, c, V * D:(V + 1) * D],
                                                   start=(c == 0), stop=(c == 1))
                                else:
                                    at = kind * D + half * DC
                                    mm = pe.matmul(bank[bk][0:DC, half * SEQ:(half + 1) * SEQ],
                                                   w_all[0:rows, c, at:at + DC], zT[p][0:rows, c, :],
                                                   start=(c == 0), stop=(c == 1))
                        mm.then_inc(proj_ps, 1)

            def scores(i):
                for p in range(2):
                    b = 2 * i + p
                    pe.wait_ge(relu_done, START + b)
                    pe.wait_ge(silu_done, START + 4 * b + 2)
                    for t in range(2):
                        for c in range(2):
                            mm = pe.matmul(bank[5][0:HB, t * SEQ:(t + 1) * SEQ], kT[p][:, c, t * HB:(t + 1) * HB],
                                           qT[p][:, c, :], start=(c == 0), stop=(c == 1))
                    mm.then_inc(sim_ps, 1)

            def values(i):
                for p in range(2):
                    b = 2 * i + p
                    pe.wait_ge(gT_done, START + b)
                    pe.wait_ge(silu_done, START + 4 * b + 3)
                    pe.wait_ge(aT_done, START + b + 1)
                    for c in range(2):
                        for t in range(2):
                            rows = HB if t == 0 else T - HB
                            mm = pe.matmul(bank[6][0:DC, c * SEQ:(c + 1) * SEQ],
                                           v[p][0:rows, t, c * DC:(c + 1) * DC], aT[p][0:rows, t, :],
                                           start=(t == 0), stop=(t == 1))
                    mm.then_inc(av_ps, 1)

            def outputs(i):
                for p in range(2):
                    b = 2 * i + p
                    pe.wait_ge(h1_done, START + b)
                    pe.wait_ge(gT_done, START + b + 1)
                    for t in range(2):
                        for c in range(2):
                            rows = DC + 1 if c == 0 else DC
                            mm = pe.matmul(bank[7][0:HB, t * D:(t + 1) * D], gT[p][0:rows, c, t * HB:(t + 1) * HB],
                                           wo[0:rows, c, :], start=(c == 0), stop=(c == 1))
                    mm.then_inc(wo_ps, 1)

            transposes(0)
            with pe.Fori(0, PAIRS - 1) as i:
                projections(i)
                scores(i)
                transposes(i + 1)
                values(i)
                outputs(i)
            projections(PAIRS - 1)
            scores(PAIRS - 1)
            values(PAIRS - 1)
            outputs(PAIRS - 1)

        @block.vector
        def _(dve):
            dve.wait_ge(weights_in, START + 80)
            for c in range(2):
                dve.tensor_scalar(w_all[0:DC, c, :], w_raw[:, c, :], ln_gb[:, c, 0:1], None, ALU.mult
                                  ).then_inc(w_ready, 1)
            dve.wait_ge(bias_ps, START + 1)
            for half in range(2):
                dve.tensor_tensor(w_all[DC:DC + 1, 0, half * 2 * D:(half + 1) * 2 * D], bank[1 + half][0:1, 0:2 * D],
                                  b_all[:, half * 2 * D:(half + 1) * 2 * D], ALU.add).then_inc(w_ready, 1)

            def normalise(i):
                for p in range(2):
                    dve.wait_ge(norm_in[p], START + 16 * (i + 1))
                    for t in range(2):
                        dve.bn_stats(stats[p][:, t, :], h_norm[p][:, t, :]).then_inc(stats_done, 1)
                for p in range(2):
                    b = 2 * i + p
                    dve.wait_ge(stats_done, START + 2 * b + 2)
                    dve.sem_inc(vector_step, 1)
                    for t in range(2):
                        dve.bn_aggr(mv[p][:, t, :], stats[p][:, t, :]).then_inc(mv_done, 1)
                for p in range(2):
                    b = 2 * i + p
                    dve.wait_ge(mv_done, START + 2 * b + 2)
                    dve.tensor_scalar(ve[p][:, :], mv[p][:, :, 1], 1.0 + EPS, EPS * EPS, ALU.mult, ALU.add
                                      ).then_inc(ve_done, 1)
                for p in range(2):
                    b = 2 * i + p
                    dve.wait_ge(zT_ps, START + 2 * i)
                    dve.wait_ge(rstd_done, START + b + 1)
                    for t in range(2):
                        dve.tensor_scalar(z[p][:, t, :], h_norm[p][:, t, :], mv[p][:, t, 0:1], rstd[p][:, t:t + 1],
                                          ALU.subtract, ALU.mult).then_inc(z_done, 1)

            def body(i):
                for p in range(2):
                    b = 2 * i + p
                    dve.wait_ge(wo_ps, START + 2 * i)
                    dve.wait_ge(silu_done, START + 4 * b + 4)
                    dve.wait_ge(av_ps, START + b + 1)
                    dve.tensor_tensor(gT[p][0:DC, :, :], bank[6][0:DC, 0:2 * SEQ].rearrange("p (c n) -> p c n", c=2),
                                      uT[p][:, :, :], ALU.mult).then_inc(gT_done, 1)
                for p in range(2):
                    b = 2 * i + p
                    dve.wait_ge(stored[p], START + 32 * i)
                    dve.wait_ge(res_in[p], START + 16 * (i + 1))
                    dve.wait_ge(wo_ps, START + b + 1)
                    dve.tensor_tensor(h1[p][:, :, :], bank[7][0:HB, 0:2 * D].rearrange("p (t n) -> p t n", t=2),
                                      h_res[p][:, :, :], ALU.add).then_inc(h1_done, 1)

            normalise(0)
            with dve.Fori(0, PAIRS - 1) as i:
                normalise(i + 1)
                body(i)
            body(PAIRS - 1)


def dispatch(nc, used, w, dram, const, layer):
    experts, top = (E0, 1) if layer == 0 else (E1, 2)
    region = NP if layer == 0 else CAPR
    h, slots = dram["h1" if layer == 0 else "h3"], dram[f"slots{layer}"]
    GT = 5
    ROUNDS = TILES // (2 * GT)
    M = top * experts
    with ExitStack() as ctx:
        def sb(name, shape, dt=F32):
            return ctx.enter_context(nc.sbuf_tensor(f"r{layer}_{name}", shape, dt))

        primed = primed_semaphores(nc, used)

        def sem(name):
            return primed(f"r{layer}_{name}")

        bank = [ctx.enter_context(nc.psum_tensor(f"r{layer}_bank{i}", [128, 512], F32)) for i in range(8)]
        gate = sb("gate", [DC + 1, 2, experts])
        centre = sb("centre", [DC + 1, experts])
        minus_half = sb("minus_half", [128, GT])
        hg = [sb(f"h{i}", [128, GT, D]) for i in range(2)]
        rows = [sb(f"rows{i}", [128, GT, RW]) for i in range(2)]
        stats = [sb(f"stats{i}", [128, GT, 6]) for i in range(2)]
        mv = [sb(f"mv{i}", [128, GT, 2]) for i in range(2)]
        ve = [sb(f"ve{i}", [128, GT]) for i in range(2)]
        rstd = [sb(f"rstd{i}", [128, GT]) for i in range(2)]
        zT = [sb(f"zT{i}", [DC + 1, GT, 2, 128]) for i in range(2)]
        logits = [sb(f"logits{i}", [128, GT, 8]) for i in range(2)]
        best = [sb(f"best{i}", [128, GT, 8]) for i in range(2)]
        best_at = [sb(f"best_at{i}", [128, GT, 8], U32) for i in range(2)]
        chosen = [sb(f"chosen{i}", [128, GT, top, experts], BF16) for i in range(2)]
        rank = [sb(f"rank{i}", [128, GT, M]) for i in range(2)]
        mine = [sb(f"mine{i}", [128, GT, M]) for i in range(2)]
        place = [sb(f"place{i}", [128, GT, top]) for i in range(2)]
        over = [sb(f"over{i}", [128, GT, top]) for i in range(2)]
        base = [sb(f"base{i}", [128, GT, top]) for i in range(2)]
        kept = [sb(f"kept{i}", [128, GT, top]) for i in range(2)]
        slot = [sb(f"slot{i}", [128, GT * top], I32) for i in range(2)]
        gap = [sb(f"gap{i}", [128, GT]) for i in range(2)]
        ex = [sb(f"ex{i}", [128, GT]) for i in range(2)]
        den = [sb(f"den{i}", [128, GT]) for i in range(2)]
        seen = sb("seen", [128, M])
        full = sb("full", [1, E0, TILES])
        in_use = sb("in_use", [1, E0])
        ends = sb("ends", [1, E0])
        past = sb("past", [1, TILES0, E0 - 1])
        expert_f = sb("expert_f", [1, TILES0])
        skipped = sb("skipped", [1, TILES0, E0 - 1])
        skip = sb("skip", [1, TILES0])
        own = sb("own", [1, TILES0])
        first = sb("first", [1, TILES0])
        expert_no, before, ones = const["expert_no"], const["before"], const["ones"]
        ident = const["ident"]

        gate_in = sem("gate_in")
        h_in = [sem(f"h_in{i}") for i in range(2)]
        consts = sem("consts")
        rowno = sem("rowno")
        gate_ready = sem("gate_ready")
        stats_done = sem("stats_done")
        mv_done = sem("mv_done")
        ve_done = sem("ve_done")
        rstd_done = sem("rstd_done")
        z_done = sem("z_done")
        zT_ps = sem("zT_ps")
        zT_done = sem("zT_done")
        logits_ps = sem("logits_ps")
        logits_done = sem("logits_done")
        best_done = sem("best_done")
        at_done = sem("at_done")
        chosen_done = sem("chosen_done")
        rank_ps = sem("rank_ps")
        rank_done = sem("rank_done")
        seen_done = sem("seen_done")
        base_done = sem("base_done")
        den_done = sem("den_done")
        first_done = sem("first_done")
        mine_done = sem("mine_done")
        place_done = sem("place_done")
        over_done = sem("over_done")
        kept_done = sem("kept_done")
        table = sem("table")
        gap_done = sem("gap_done")
        ex_done = sem("ex_done")
        weights_done = sem("weights_done")
        slot_done = sem("slot_done")
        rows_free = sem("rows_free")
        vector_step = sem("vector_step")
        scattered = [unprimed_semaphore(nc, used, f"r{layer}_scattered{i}") for i in range(2)]
        block = ctx.enter_context(nc.Block())

        @block.sync
        def _(sp):
            sp.dma_start(gate[0:DC, :, :], w[f"gate{layer}_w"].rearrange("(c p) n -> p c n", c=2)).then_inc(gate_in, 16)
            if layer == 0:
                sp.dma_start(gate[DC:DC + 1, 0, :], w["gate0_b"]).then_inc(gate_in, 16)
                sp.dma_start(centre[DC:DC + 1, :], w["gate0_centre"]).then_inc(gate_in, 16)
            with sp.Fori(0, ROUNDS) as i:
                for p in range(2):
                    g = 2 * i + p
                    sp.wait_ge(z_done, START + GT * (g - 1))
                    sp.dma_start(hg[p][:, :, :], h[bass.ds(g * GT * 128, GT * 128), :]
                                 .rearrange("(j p) c -> p j c", p=128)).then_inc(h_in[p], 16)

        @block.gpsimd
        def _(pool):
            pool.memset(minus_half[:, :], -0.5).then_inc(consts, 1)
            for p in range(2):
                pool.memset(rows[p][:, :, D:D + 2], 1.0).then_inc(rowno, 1)
                for k in range(2):
                    pool.iota(rows[p][:, :, D + 2 + k:D + 3 + k].bitcast(I32), pattern=[[128, GT], [0, 1]],
                              base=k * NP + p * GT * 128, channel_multiplier=1).then_inc(rowno, 1)
            pool.wait_ge(consts, START + 1)
            pool.wait_ge(rowno, START + 6)
            with pool.Fori(0, ROUNDS) as i:
                for p in range(2):
                    g = 2 * i + p
                    pool.wait_ge(ve_done, START + g + 1)
                    pool.tensor_tensor(rstd[p][:, :], ve[p][:, :], minus_half[:, :], ALU.pow).then_inc(rstd_done, 1)
                for p in range(2):
                    g = 2 * i + p
                    pool.wait_ge(z_done, START + GT * (g + 1))
                    if layer:
                        pool.wait_ge(weights_done, START + g + 1)
                    pool.wait_ge(slot_done, START + g + 1)
                    pool.sem_inc(vector_step, 1)
                    for j in range(GT):
                        for k in range(top):
                            pool.indirect_dma_start(
                                slots, bass.IndirectOffsetOnAxis(ap=slot[p][:, j * top + k:j * top + k + 1], axis=0),
                                rows[p][:, j, :], None, bounds_check=slots.shape[0] - 1, oob_is_err=False
                            ).then_inc(scattered[p], 16)
                for p in range(2):
                    pool.wait_ge(scattered[p], 16 * GT * top * (i + 1))
                    pool.sem_inc(rows_free, 1)

        @block.scalar
        def _(act):
            with act.Fori(0, ROUNDS) as i:
                for p in range(2):
                    g = 2 * i + p
                    act.wait_ge(logits_ps, START + g - 1)
                    for n in range(GT):
                        act.wait_ge(zT_ps, START + GT * g + n + 1)
                        act.activation(zT[p][0:DC, n, :, :],
                                       bank[n][0:DC, 0:256].rearrange("p (c n) -> p c n", c=2), ACT.Copy
                                       ).then_inc(zT_done, 1)
                if layer:
                    for p in range(2):
                        g = 2 * i + p
                        act.wait_ge(gap_done, START + g + 1)
                        act.activation(ex[p][:, :], gap[p][:, :], ACT.Exp).then_inc(ex_done, 1)

        @block.tensor
        def _(pe):
            pe.wait_ge(gate_ready, START + 3)
            with pe.Fori(0, ROUNDS) as i:
                for p in range(2):
                    g = 2 * i + p
                    for j in range(GT):
                        pe.wait_ge(zT_done, START + GT * (g - 1) + j + 1)
                        pe.wait_ge(z_done, START + GT * g + j + 1)
                        for c in range(2):
                            mm = pe.transpose(bank[j][0:DC, c * 128:(c + 1) * 128],
                                              rows[p][:, j, c * DC:(c + 1) * DC], ident)
                        mm.then_inc(zT_ps, 1)
                for p in range(2):
                    g = 2 * i + p
                    pe.wait_ge(logits_done, START + g)
                    for j in range(GT):
                        pe.wait_ge(zT_done, START + GT * g + j + 1)
                        for c in range(2):
                            k = DC + 1 if c == 0 and layer == 0 else DC
                            mm = pe.matmul(bank[5][:, 8 * j:8 * j + experts], zT[p][0:k, j, c, :], gate[0:k, c, :],
                                           start=(c == 0), stop=(c == 1))
                    mm.then_inc(logits_ps, 1)
                for p in range(2):
                    g = 2 * i + p
                    pe.wait_ge(seen_done, START + g)
                    pe.wait_ge(chosen_done, START + top * (g + 1))
                    for j in range(GT):
                        for earlier in range(j + 1):
                            pe.matmul(bank[6 + p][:, M * j:M * (j + 1)], before if earlier == j else ones,
                                      chosen[p][:, earlier, :, :].rearrange("p k e -> p (k e)"),
                                      start=(earlier == 0), stop=(earlier == j))
                    for j in range(GT):
                        mm = pe.matmul(bank[6 + p][:, 128:128 + M], ones, chosen[p][:, j, :, :].rearrange("p k e -> p (k e)"),
                                       start=(j == 0), stop=(j == GT - 1))
                    mm.then_inc(rank_ps, 1)

        @block.vector
        def _(dve):
            dve.memset(seen[:, :], 0.0).then_inc(seen_done, 1)
            for p in range(2):
                dve.memset(logits[p][:, :, :], -3e38).then_inc(consts, 1)
                dve.memset(zT[p][DC:DC + 1, :, :, :], 1.0).then_inc(gate_ready, 1)
            if layer == 0:
                dve.wait_ge(gate_in, START + 48)
                dve.tensor_tensor(gate[DC:DC + 1, 0, :], gate[DC:DC + 1, 0, :], centre[DC:DC + 1, :], ALU.subtract
                                  ).then_inc(gate_ready, 1)
            else:
                dve.wait_ge(gate_in, START + 16)
                dve.sem_inc(gate_ready, 1)
            dve.wait_ge(consts, START + 3)
            dve.wait_ge(seen_done, START + 1)
            dve.wait_ge(rowno, START + 6)
            numbers = expert_no[:, 0:experts].unsqueeze(1).broadcast_to([128, GT, experts])

            with dve.Fori(0, ROUNDS) as i:
                for p in range(2):
                    dve.wait_ge(h_in[p], START + 16 * (i + 1))
                    for j in range(GT):
                        dve.bn_stats(stats[p][:, j, :], hg[p][:, j, :]).then_inc(stats_done, 1)
                for p in range(2):
                    g = 2 * i + p
                    dve.wait_ge(stats_done, START + GT * (g + 1))
                    dve.sem_inc(vector_step, 1)
                    for j in range(GT):
                        dve.bn_aggr(mv[p][:, j, :], stats[p][:, j, :]).then_inc(mv_done, 1)
                for p in range(2):
                    g = 2 * i + p
                    dve.wait_ge(mv_done, START + GT * (g + 1))
                    dve.tensor_scalar(ve[p][:, :], mv[p][:, :, 1], EPS, None, ALU.add).then_inc(ve_done, 1)
                for p in range(2):
                    g = 2 * i + p
                    dve.wait_ge(rows_free, START + g - 1)
                    dve.wait_ge(rstd_done, START + g + 1)
                    for j in range(GT):
                        dve.tensor_scalar(rows[p][:, j, 0:D], hg[p][:, j, :], mv[p][:, j, 0:1], rstd[p][:, j:j + 1],
                                          ALU.subtract, ALU.mult).then_inc(z_done, 1)
                for p in range(2):
                    g = 2 * i + p
                    dve.wait_ge(logits_ps, START + g + 1)
                    dve.tensor_copy(logits[p][:, :, 0:experts],
                                    bank[5][:, 0:8 * GT].rearrange("p (j e) -> p j e", e=8)[:, :, 0:experts]
                                    ).then_inc(logits_done, 1)
                for p in range(2):
                    g = 2 * i + p
                    dve.wait_ge(logits_done, START + g + 1)
                    dve.sem_inc(vector_step, 1)
                    for j in range(GT):
                        dve.max(best[p][:, j, :], logits[p][:, j, :]).then_inc(best_done, 1)
                for p in range(2):
                    g = 2 * i + p
                    dve.wait_ge(best_done, START + GT * (g + 1))
                    dve.sem_inc(vector_step, 1)
                    for j in range(GT):
                        dve.max_index(best_at[p][:, j, :], best[p][:, j, :], logits[p][:, j, :]).then_inc(at_done, 1)
                for p in range(2):
                    g = 2 * i + p
                    dve.wait_ge(at_done, START + GT * (g + 1))
                    for k in range(top):
                        dve.tensor_tensor(chosen[p][:, :, k, :], numbers,
                                          best_at[p][:, :, k:k + 1].broadcast_to([128, GT, experts]),
                                          ALU.is_equal).then_inc(chosen_done, 1)
                for p in range(2):
                    for k in range(top):
                        dve.tensor_scalar(base[p][:, :, k], best_at[p][:, :, k], float(region * top),
                                          float(k * region), ALU.mult, ALU.add).then_inc(base_done, 1)
                if layer:
                    for p in range(2):
                        dve.tensor_tensor(gap[p][:, :], best[p][:, :, 1], best[p][:, :, 0], ALU.subtract
                                          ).then_inc(gap_done, 1)
                    for p in range(2):
                        g = 2 * i + p
                        dve.wait_ge(ex_done, START + g + 1)
                        dve.tensor_scalar(den[p][:, :], ex[p][:, :], 1.0, None, ALU.add).then_inc(den_done, 1)
                    for p in range(2):
                        g = 2 * i + p
                        dve.wait_ge(den_done, START + g + 1)
                        dve.reciprocal(rows[p][:, :, D], den[p][:, :]).then_inc(first_done, 1)
                    for p in range(2):
                        g = 2 * i + p
                        dve.wait_ge(first_done, START + g + 1)
                        dve.tensor_tensor(rows[p][:, :, D + 1], ex[p][:, :], rows[p][:, :, D], ALU.mult
                                          ).then_inc(weights_done, 1)
                for p in range(2):
                    g = 2 * i + p
                    dve.wait_ge(rank_ps, START + g + 1)
                    dve.wait_ge(seen_done, START + g + 1)
                    dve.tensor_tensor(rank[p][:, :, :], bank[6 + p][:, 0:M * GT].rearrange("p (j m) -> p j m", m=M),
                                      seen[:, :].unsqueeze(1).broadcast_to([128, GT, M]), ALU.add
                                      ).then_inc(rank_done, 1)
                    dve.wait_ge(rank_done, START + g + 1)
                    dve.tensor_tensor(seen[:, :], bank[6 + p][:, 128:128 + M], seen[:, :], ALU.add
                                      ).then_inc(seen_done, 1)
                for p in range(2):
                    dve.tensor_tensor(mine[p][:, :, :], rank[p][:, :, :],
                                      chosen[p][:, :, :, :].rearrange("p j k e -> p j (k e)"), ALU.mult
                                      ).then_inc(mine_done, 1)
                for p in range(2):
                    g = 2 * i + p
                    dve.wait_ge(mine_done, START + g + 1)
                    dve.tensor_reduce(place[p][:, :, :].rearrange("p j k -> p (j k)"),
                                      mine[p][:, :, :].rearrange("p j (k e) -> p (j k) e", k=top), AX.X, ALU.add
                                      ).then_inc(place_done, 1)
                for p in range(2):
                    g = 2 * i + p
                    dve.wait_ge(place_done, START + g + 1)
                    dve.tensor_scalar(over[p][:, :, :], place[p][:, :, :], float(CAP if layer else NP),
                                      float(NOWHERE), ALU.is_ge, ALU.mult).then_inc(over_done, 1)
                for p in range(2):
                    dve.tensor_tensor(kept[p][:, :, :], place[p][:, :, :], base[p][:, :, :], ALU.add
                                      ).then_inc(kept_done, 1)
                for p in range(2):
                    g = 2 * i + p
                    dve.wait_ge(rows_free, START + g - 1)
                    dve.wait_ge(over_done, START + g + 1)
                    dve.wait_ge(kept_done, START + g + 1)
                    dve.tensor_tensor(slot[p][:, :].rearrange("p (j k) -> p j k", k=top), kept[p][:, :, :],
                                      over[p][:, :, :], ALU.add).then_inc(slot_done, 1)
                for p in range(2):
                    g = 2 * i + p
                    dve.wait_ge(rows_free, START + g + 1)
                    dve.tensor_scalar(rows[p][:, :, D + 2:RW].bitcast(I32), rows[p][:, :, D + 2:RW].bitcast(I32),
                                      float(2 * GT * 128), None, ALU.add).then_inc(rowno, 1)
            if layer == 0:
                counted = seen[0:1, :]
                dve.wait_ge(seen_done, START + 2 * ROUNDS + 1)
                dve.tensor_tensor(full[:, :, :], counted.unsqueeze(2).broadcast_to([1, E0, TILES]),
                                  const["tile_rows"][:, 0:TILES].unsqueeze(1).broadcast_to([1, E0, TILES]), ALU.is_gt
                                  ).then_inc(table, 1)
                dve.wait_ge(table, START + 1)
                dve.tensor_reduce(in_use[:, :], full[:, :, :], AX.X, ALU.add).then_inc(table, 1)
                dve.wait_ge(table, START + 2)
                dve.tensor_copy(ends[:, 0:1], in_use[:, 0:1]).then_inc(table, 1)
                for e in range(1, E0):
                    dve.wait_ge(table, START + 2 + e)
                    dve.tensor_tensor(ends[:, e:e + 1], ends[:, e - 1:e], in_use[:, e:e + 1], ALU.add
                                      ).then_inc(table, 1)
                dve.wait_ge(table, START + 2 + E0)
                dve.tensor_tensor(past[:, :, :], const["tile_no"].unsqueeze(2).broadcast_to([1, TILES0, E0 - 1]),
                                  ends[:, 0:E0 - 1].unsqueeze(1).broadcast_to([1, TILES0, E0 - 1]), ALU.is_ge
                                  ).then_inc(table, 1)
                dve.wait_ge(table, START + 3 + E0)
                dve.tensor_reduce(expert_f[:, :], past[:, :, :], AX.X, ALU.add).then_inc(table, 1)
                dve.tensor_tensor(skipped[:, :, :], past[:, :, :],
                                  in_use[:, 0:E0 - 1].unsqueeze(1).broadcast_to([1, TILES0, E0 - 1]), ALU.mult
                                  ).then_inc(table, 1)
                dve.wait_ge(table, START + 5 + E0)
                dve.tensor_reduce(skip[:, :], skipped[:, :, :], AX.X, ALU.add).then_inc(table, 1)
                dve.wait_ge(table, START + 6 + E0)
                dve.tensor_tensor(own[:, :], const["tile_no"], skip[:, :], ALU.subtract).then_inc(table, 1)
                dve.tensor_scalar(first[:, :], expert_f[:, :], float(NP), None, ALU.mult).then_inc(table, 1)
                dve.wait_ge(table, START + 8 + E0)
                dve.scalar_tensor_tensor(const["tile_row"], own[:, :], 128.0, first[:, :], ALU.mult, ALU.add
                                         ).then_inc(table, 1)
                dve.tensor_scalar(const["tile_expert"], expert_f[:, :], 1.0, None, ALU.mult).then_inc(table, 1)


def experts_gelu(nc, used, w, dram, const):
    with ExitStack() as ctx:
        def sb(name, shape, dt=F32):
            return ctx.enter_context(nc.sbuf_tensor(f"e0_{name}", shape, dt))

        primed = primed_semaphores(nc, used)

        def sem(name):
            return primed(f"e0_{name}")

        bank = [ctx.enter_context(nc.psum_tensor(f"e0_bank{i}", [128, n, 512], F32))
                for i, n in enumerate((1, 2, 2, 2, 1))]
        T_PS, Y_PS = bank[0], bank[4]
        UP_PS, HT_PS = (bank[1], bank[2]), bank[3]
        HC = H0 // 128
        w1 = sb("w1", [DC + 1, 2, E0, H0])
        w2 = sb("w2", [128, HC, E0, D])
        x = [sb(f"x{i}", [128, RW]) for i in range(2)]
        to = [sb(f"to{i}", [128, 1], I32) for i in range(2)]
        b2 = [sb(f"b2_{i}", [128, D]) for i in range(2)]
        xT = [sb(f"xT{i}", [DC + 1, 2, 128]) for i in range(2)]
        hid = [sb(f"hid{i}", [128, H0]) for i in range(2)]
        hT = [sb(f"hT{i}", [128, HC, 128]) for i in range(2)]
        y = [sb(f"y{i}", [128, D]) for i in range(2)]
        ident = const["ident"]

        w_in = sem("w_in")
        x_in = [sem(f"x_in{i}") for i in range(2)]
        b2_in = [sem(f"b2_in{i}") for i in range(2)]
        consts = sem("consts")
        xT_ps = sem("xT_ps")
        xT_done = sem("xT_done")
        up_ps = sem("up_ps")
        hid_done = sem("hid_done")
        hT_ps = sem("hT_ps")
        hT_done = sem("hT_done")
        y_ps = sem("y_ps")
        y_done = sem("y_done")
        to_done = sem("to_done")
        y_free = sem("y_free")
        pool_step = sem("pool_step")
        scattered = [unprimed_semaphore(nc, used, f"e0_scattered{i}") for i in range(2)]
        PAIRS = TILES0 // 2
        block = ctx.enter_context(nc.Block())

        @block.sync
        def _(sp):
            for c in range(2):
                sp.dma_start(w1[0:DC, c, :, :], w["e0_w1"][c * DC:(c + 1) * DC, :]
                             .rearrange("p (e n) -> p e n", e=E0)).then_inc(w_in, 16)
            sp.dma_start(w1[DC:DC + 1, 0, :, :], w["e0_b1"].rearrange("p (e n) -> p e n", e=E0)).then_inc(w_in, 16)
            for e in range(E0):
                sp.dma_start(w2[:, :, e, :], w["e0_w2"][e].rearrange("(k p) n -> p k n", p=128)).then_inc(w_in, 16)
            with sp.Fori(0, PAIRS) as i:
                for p in range(2):
                    t = 2 * i + p
                    row = sp.value_load(const["tile_row"][0:1, bass.ds(t, 1)], min_val=0, max_val=ROWS0 - 128)
                    expert = sp.value_load(const["tile_expert"][0:1, bass.ds(t, 1)], min_val=0, max_val=E0 - 1)
                    sp.wait_ge(xT_ps, START + t - 1)
                    sp.wait_ge(to_done, START + t - 1)
                    sp.dma_start(x[p][:, :], dram["slots0"][bass.ds(row, 128), :]).then_inc(x_in[p], 16)
                    sp.wait_ge(y_done, START + t - 1)
                    sp.dma_start(b2[p][:, :], w["e0_b2"][bass.ds(expert, 1), :].broadcast_to([128, D])
                                 ).then_inc(b2_in[p], 16)

        @block.gpsimd
        def _(pool):
            with pool.Fori(0, PAIRS) as i:
                for p in range(2):
                    t = 2 * i + p
                    pool.wait_ge(to_done, START + t + 1)
                    pool.wait_ge(y_done, START + t + 1)
                    pool.sem_inc(pool_step, 1)
                    pool.indirect_dma_start(dram["y0"], bass.IndirectOffsetOnAxis(ap=to[p][:, 0:1], axis=0), y[p][:, :],
                                            None, bounds_check=NP - 1, oob_is_err=False).then_inc(scattered[p], 16)
                    pool.wait_ge(scattered[p], 16 * (i + 1))
                    pool.sem_inc(y_free, 1)

        @block.scalar
        def _(act):
            with act.Fori(0, PAIRS) as i:
                for p in range(2):
                    t = 2 * i + p
                    act.wait_ge(up_ps, START + t - 1)
                    act.wait_ge(xT_ps, START + t + 1)
                    act.activation(xT[p][0:DC, :, :], T_PS[0:DC, 0, 0:256].rearrange("p (c n) -> p c n", c=2), ACT.Copy
                                   ).then_inc(xT_done, 1)
                for p in range(2):
                    t = 2 * i + p
                    act.wait_ge(hT_ps, START + t - 1)
                    act.wait_ge(up_ps, START + t + 1)
                    act.activation(hid[p][:, :].rearrange("p (n f) -> p n f", n=2), UP_PS[p][:, :, 0:H0 // 2],
                                   ACT.Gelu).then_inc(hid_done, 1)

        @block.tensor
        def _(pe):
            pe.wait_ge(w_in, START + 16 * (3 + E0))
            pe.wait_ge(consts, START + 2)

            def transposes(i):
                for p in range(2):
                    t = 2 * i + p
                    pe.wait_ge(xT_done, START + t)
                    pe.wait_ge(x_in[p], START + 16 * (i + 1))
                    for c in range(2):
                        mm = pe.transpose(T_PS[0:DC, 0, c * 128:(c + 1) * 128], x[p][:, c * DC:(c + 1) * DC], ident)
                    mm.then_inc(xT_ps, 1)

            with pe.Fori(0, PAIRS) as i:
                transposes(i)
                for p in range(2):
                    t = 2 * i + p
                    expert = pe.value_load(const["tile_expert"][0:1, bass.ds(t, 1)], min_val=0, max_val=E0 - 1)
                    pe.wait_ge(hid_done, START + t - 1)
                    pe.wait_ge(xT_done, START + t + 1)
                    for half in range(2):
                        for c in range(2):
                            k = DC + 1 if c == 0 else DC
                            mm = pe.matmul(UP_PS[p][:, half, 0:H0 // 2], xT[p][0:k, c, :],
                                           w1[0:k, c, bass.ds(expert, 1), half * H0 // 2:(half + 1) * H0 // 2]
                                           .rearrange("p a n -> p (a n)"), start=(c == 0), stop=(c == 1))
                    mm.then_inc(up_ps, 1)
                for p in range(2):
                    t = 2 * i + p
                    expert = pe.value_load(const["tile_expert"][0:1, bass.ds(t, 1)], min_val=0, max_val=E0 - 1)
                    pe.wait_ge(hT_done, START + 2 * t)
                    pe.wait_ge(hid_done, START + t + 1)
                    for k in range(HC):
                        mm = pe.transpose(HT_PS[:, k // 3, k % 3 * 128:(k % 3 + 1) * 128],
                                          hid[p][:, k * 128:(k + 1) * 128], ident)
                    mm.then_inc(hT_ps, 1)
                    pe.wait_ge(y_done, START + t)
                    pe.wait_ge(hT_done, START + 2 * t + 2)
                    for k in range(HC):
                        mm = pe.matmul(Y_PS[:, 0, 0:D], hT[p][:, k, :],
                                       w2[:, k, bass.ds(expert, 1), :].rearrange("p a n -> p (a n)"),
                                       start=(k == 0), stop=(k == HC - 1))
                    mm.then_inc(y_ps, 1)

        @block.vector
        def _(dve):
            for p in range(2):
                dve.memset(xT[p][DC:DC + 1, :, :], 1.0).then_inc(consts, 1)
            with dve.Fori(0, PAIRS) as i:
                for p in range(2):
                    t = 2 * i + p
                    dve.wait_ge(y_free, START + t - 1)
                    dve.wait_ge(x_in[p], START + 16 * (i + 1))
                    dve.tensor_copy(to[p][:, :], x[p][:, D + 2:D + 3].bitcast(I32)).then_inc(to_done, 1)
                for p in range(2):
                    t = 2 * i + p
                    dve.wait_ge(y_ps, START + t - 1)
                    dve.wait_ge(hT_ps, START + t + 1)
                    for half in range(2):
                        dve.tensor_copy(hT[p][:, 3 * half:3 * half + 3, :],
                                        HT_PS[:, half, 0:384].rearrange("p (k n) -> p k n", k=3)).then_inc(hT_done, 1)
                    dve.wait_ge(b2_in[p], START + 16 * (i + 1))
                    dve.wait_ge(y_ps, START + t + 1)
                    dve.tensor_tensor(y[p][:, :], Y_PS[:, 0, 0:D], b2[p][:, :], ALU.add).then_inc(y_done, 1)


def attend_causal(nc, used, w, dram, const):
    PG = 2
    GROUPS = HEADS // (2 * PG)
    A, BT = slice(0, HB), slice(HB, SEQ)
    with ExitStack() as ctx:
        def sb(name, shape, dt=F32):
            return ctx.enter_context(nc.sbuf_tensor(f"c_{name}", shape, dt))

        primed = primed_semaphores(nc, used)

        def sem(name):
            return primed(f"c_{name}")

        def psum(name, banks):
            return ctx.enter_context(nc.psum_tensor(f"c_{name}", [128, banks, 512], F32))

        Q_PS, K_PS, V_PS = psum("q_ps", 1)[:, 0, :], psum("k_ps", 1)[:, 0, :], psum("v_ps", 1)[:, 0, :]
        S_PS, PT_PS, O_PS = psum("s_ps", 2), psum("pT_ps", 2), psum("o_ps", 1)[:, 0, :]
        wq = sb("wq", [DC, 2, HEADS * HD])
        wdown = sb("wdown", [DC, 2, RANK])
        up_raw = sb("up_raw", [RANK, 2 * HEADS * HD])
        wup = sb("wup", [RANK + 1, 2 * HEADS * HD])
        ln_gb = sb("ln_gb", [RANK, 2])
        wo = sb("wo", [128, HEADS // 2, D])
        bo = sb("bo", [HB, D])
        cos = sb("cos", [128, SEQ])
        sin = sb("sin", [128, SEQ])
        mask = sb("mask", [HB, 2 * HB + 2 * SEQ], BF16)
        ident_b = sb("ident_b", [HB, HB], BF16)
        minus_half = sb("minus_half", [HB, 2])
        h1 = sb("h1", [HB, 2, D])
        y0 = sb("y0", [HB, 2, D])
        h1_res = sb("h1_res", [HB, 2, D])
        y0_res = sb("y0_res", [HB, 2, D])
        h2 = sb("h2", [HB, 2, D])
        sum_res = sb("sum_res", [HB, 2, D])
        res = sb("res", [HB, 2, D])
        h3 = sb("h3", [HB, 2, D])
        stats = sb("stats", [HB, 2, 6])
        mv = sb("mv", [HB, 2, 2])
        ve = sb("ve", [HB, 2])
        rstd = sb("rstd", [HB, 2])
        z = sb("z", [HB, 2, D])
        zT = sb("zT", [DC, 2, SEQ])
        c_stats = sb("c_stats", [HB, 2, 6])
        c_mv = sb("c_mv", [HB, 2, 2])
        c_ve = sb("c_ve", [HB, 2])
        c_rstd = sb("c_rstd", [HB, 2])
        cz = sb("cz", [HB, 2, RANK])
        cT = sb("cT", [RANK + 1, SEQ])
        turn = {kind: [sb(f"{kind}_turn{i}", [128, PG, SEQ]) for i in range(2)] for kind in "qk"}
        qT = [sb(f"qT{g}", [128, PG, SEQ]) for g in range(GROUPS)]
        kT = [sb(f"kT{g}", [128, PG, SEQ]) for g in range(GROUPS)]
        v = [sb(f"v{g}", [HB, 2, 2 * PG * HD]) for g in range(GROUPS)]
        top = [sb(f"top{g}", [HB, 2 * 2 * PG]) for g in range(GROUPS)]
        minus_top = [sb(f"minus_top{g}", [HB, 2 * 2 * PG]) for g in range(GROUPS)]
        total = [sb(f"total{g}", [HB, 2 * 2 * PG]) for g in range(GROUPS)]
        share = [sb(f"share{g}", [HB, 2 * 2 * PG]) for g in range(GROUPS)]
        prob = [sb(f"prob{g}", [HB, 2, 480]) for g in range(GROUPS)]
        pT = [sb(f"pT{g}", [HB, 2, 480]) for g in range(GROUPS)]
        oT = sb("oT", [128, HEADS // 2, SEQ])
        ident = const["ident"]

        weights_in = sem("weights_in")
        h_in = sem("h_in")
        y_in = sem("y_in")
        hres_in = sem("hres_in")
        yres_in = sem("yres_in")
        consts = sem("consts")
        up_ready = sem("up_ready")
        upb_ps = sem("upb_ps")
        h2_done = sem("h2_done")
        stats_done = sem("stats_done")
        mv_done = sem("mv_done")
        ve_done = sem("ve_done")
        rstd_done = sem("rstd_done")
        z_done = sem("z_done")
        zT_ps = sem("zT_ps")
        zT_done = sem("zT_done")
        c_ps = sem("c_ps")
        c_stats_done = sem("c_stats_done")
        c_mv_done = sem("c_mv_done")
        c_ve_done = sem("c_ve_done")
        c_rstd_done = sem("c_rstd_done")
        cz_done = sem("cz_done")
        cT_ps = sem("cT_ps")
        cT_done = sem("cT_done")
        q_ps = sem("q_ps")
        k_ps = sem("k_ps")
        v_ps = sem("v_ps")
        q_turned = sem("q_turned")
        k_turned = sem("k_turned")
        q_done = sem("q_done")
        k_done = sem("k_done")
        v_done = sem("v_done")
        s_ps = sem("s_ps")
        top_done = sem("top_done")
        minus_done = sem("minus_done")
        exp_done = sem("exp_done")
        share_done = sem("share_done")
        prob_done = sem("prob_done")
        pT_ps = sem("pT_ps")
        pT_done = sem("pT_done")
        o_ps = sem("o_ps")
        o_done = sem("o_done")
        wo_ps = sem("wo_ps")
        sum_done = sem("sum_done")
        res_done = sem("res_done")
        h3_done = sem("h3_done")
        stored = sem("stored")
        step = sem("step")
        block = ctx.enter_context(nc.Block())
        W = HEADS * HD

        @block.sync
        def _(sp):
            for tile, src in ((wq, w["wq"].rearrange("(c p) n -> p c n", c=2)),
                              (wdown, w["wdown"].rearrange("(c p) n -> p c n", c=2)),
                              (wo, w["wo1"].rearrange("(k p) n -> p k n", p=128))):
                sp.dma_start(tile[:, :, :], src).then_inc(weights_in, 16)
            for tile, name in ((up_raw, "wup"), (ln_gb, "attn1_ln"), (bo, "bo"), (cos, "cos"), (sin, "sin"),
                               (mask, "mask"), (ident_b, "ident_b")):
                sp.dma_start(tile[:, :], w[name]).then_inc(weights_in, 16)

            def load(b):
                sp.wait_ge(h2_done, START + b)
                sp.dma_start(h1[:, :, :], rows_of(dram["h1"], b)).then_inc(h_in, 16)
                sp.dma_start(y0[:, :, :], rows_of(dram["y0"], b)).then_inc(y_in, 16)

            def residual(b):
                sp.wait_ge(sum_done, START + b)
                sp.dma_start(h1_res[:, :, :], rows_of(dram["h1"], b)).then_inc(hres_in, 16)
                sp.dma_start(y0_res[:, :, :], rows_of(dram["y0"], b)).then_inc(yres_in, 16)

            def store(b):
                sp.wait_ge(h3_done, START + b + 1)
                sp.dma_start(dram["h3"][bass.ds(b * T, HB), :], h3[:, 0, :]).then_inc(stored, 16)
                sp.dma_start(dram["h3"][bass.ds(b * T + HB, T - HB), :], h3[0:T - HB, 1, :]).then_inc(stored, 16)

            load(0)
            with sp.Fori(0, B - 1) as b:
                load(b + 1)
                residual(b)
                store(b)
            residual(B - 1)
            store(B - 1)
            sp.wait_ge(stored, START + 32 * B)

        @block.gpsimd
        def _(pool):
            pool.memset(minus_half[:, :], -0.5).then_inc(consts, 1)
            pool.wait_ge(consts, START + 2)
            pool.wait_ge(weights_in, START + 16 * 10)

            def scale_z(b):
                pool.wait_ge(ve_done, START + b + 1)
                pool.tensor_tensor(rstd[:, :], ve[:, :], minus_half[:, :], ALU.pow).then_inc(rstd_done, 1)

            def scale_c(b):
                pool.wait_ge(c_ve_done, START + b + 1)
                pool.tensor_tensor(c_rstd[:, :], c_ve[:, :], minus_half[:, :], ALU.pow).then_inc(c_rstd_done, 1)

            def rotate(G, g):
                for kind, turned, done, tiles in (("q", q_turned, q_done, qT), ("k", k_turned, k_done, kT)):
                    pool.wait_ge(s_ps, START + G - GROUPS + 1)
                    pool.wait_ge(turned, START + G + 1)
                    pool.tensor_tensor(tiles[g][:, :, :], turn[kind][0][:, :, :], turn[kind][1][:, :, :], ALU.add
                                       ).then_inc(done, 1)

            def normalise(G, g):
                pool.wait_ge(exp_done, START + 8 * (G + 1))
                pool.wait_ge(share_done, START + G + 1)
                for half, n in ((0, HB), (1, SEQ)):
                    cols = slice(0, 2 * HB) if half == 0 else slice(2 * HB, 480)
                    view = prob[g][:, :, cols].rearrange("p o (h n) -> p o h n", h=2)
                    pool.tensor_tensor(view, view, share[g][:, 4 * half:4 * half + 4]
                                       .rearrange("p (o h) -> p o h", o=2).unsqueeze(3).broadcast_to([HB, 2, 2, n]),
                                       ALU.mult).then_inc(prob_done, 1)

            def residual(b):
                pool.wait_ge(hres_in, START + 16 * (b + 1))
                pool.wait_ge(yres_in, START + 16 * (b + 1))
                pool.tensor_tensor(sum_res[:, :, :], h1_res[:, :, :], y0_res[:, :, :], ALU.add).then_inc(sum_done, 1)
                pool.wait_ge(h3_done, START + b)
                pool.wait_ge(sum_done, START + b + 1)
                pool.tensor_tensor(res[:, :, :], sum_res[:, :, :], bo[:, :].unsqueeze(1).broadcast_to([HB, 2, D]),
                                   ALU.add).then_inc(res_done, 1)

            def batch(b, last):
                rotate(3 * b + 1, 1)
                normalise(3 * b, 0)
                if not last:
                    scale_z(b + 1)
                rotate(3 * b + 2, 2)
                normalise(3 * b + 1, 1)
                residual(b)
                if not last:
                    scale_c(b + 1)
                    rotate(3 * b + 3, 0)
                normalise(3 * b + 2, 2)

            scale_z(0)
            scale_c(0)
            rotate(0, 0)
            with pool.Fori(0, B - 1) as b:
                batch(b, False)
            batch(B - 1, True)

        @block.scalar
        def _(act):
            def copy_zT(b):
                act.wait_ge(q_ps, START + 3 * b)
                act.wait_ge(zT_ps, START + b + 1)
                act.activation(zT[:, :, :], Q_PS[0:DC, 0:2 * SEQ].rearrange("p (c n) -> p c n", c=2), ACT.Copy
                               ).then_inc(zT_done, 1)

            def copy_cT(b):
                act.wait_ge(v_ps, START + 3 * b)
                act.wait_ge(cT_ps, START + b + 1)
                act.activation(cT[0:RANK, :], K_PS[0:RANK, 0:SEQ], ACT.Copy).then_inc(cT_done, 1)

            def copy_v(G, g):
                act.wait_ge(o_ps, START + G - GROUPS + 1)
                act.wait_ge(v_ps, START + G + 1)
                act.activation(v[g][:, :, :], V_PS[0:HB, :].rearrange("p (t n) -> p t n", t=2), ACT.Copy
                               ).then_inc(v_done, 1)

            def exps(G, g):
                act.wait_ge(pT_ps, START + G - GROUPS + 1)
                act.wait_ge(minus_done, START + G + 1)
                for tile, n in ((0, HB), (1, SEQ)):
                    for o in range(2):
                        for pr in range(PG):
                            at = 4 * tile + 2 * o + pr
                            cols = slice(tile * 2 * HB + pr * n, tile * 2 * HB + (pr + 1) * n)
                            act.activation(prob[g][:, o, cols], S_PS[0:HB, o, cols], ACT.Exp,
                                           bias=minus_top[g][:, at:at + 1], scale=HD ** -0.5,
                                           accum_out=total[g][:, at:at + 1]).then_inc(exp_done, 1)

            def copy_pT(G, g):
                act.wait_ge(o_ps, START + G - GROUPS + 1)
                act.wait_ge(pT_ps, START + G + 1)
                act.activation(pT[g][:, :, :], PT_PS[0:HB, :, 0:480], ACT.Copy).then_inc(pT_done, 1)

            def out_heads(b, g):
                act.wait_ge(wo_ps, START + b)
                act.wait_ge(o_ps, START + 3 * b + g + 1)
                act.activation(oT[:, PG * g:PG * (g + 1), :], O_PS[:, 0:2 * SEQ].rearrange("p (r n) -> p r n", r=PG),
                               ACT.Copy).then_inc(o_done, 1)

            def batch(b, last):
                exps(3 * b, 0)
                copy_v(3 * b + 1, 1)
                copy_pT(3 * b, 0)
                exps(3 * b + 1, 1)
                out_heads(b, 0)
                copy_v(3 * b + 2, 2)
                if not last:
                    copy_zT(b + 1)
                copy_pT(3 * b + 1, 1)
                exps(3 * b + 2, 2)
                out_heads(b, 1)
                if not last:
                    copy_cT(b + 1)
                    copy_v(3 * b + 3, 0)
                copy_pT(3 * b + 2, 2)
                out_heads(b, 2)

            copy_zT(0)
            copy_cT(0)
            copy_v(0, 0)
            with act.Fori(0, B - 1) as b:
                batch(b, False)
            batch(B - 1, True)

        @block.tensor
        def _(pe):
            pe.wait_ge(weights_in, START + 16 * 10)
            for n in range(3):
                mm = pe.matmul((Q_PS, K_PS, V_PS)[n][0:1, 0:512], ln_gb[:, 1:2], up_raw[:, 512 * n:512 * (n + 1)],
                               start=True, stop=True)
            mm.then_inc(upb_ps, 1)
            pe.wait_ge(up_ready, START + 4)
            pe.wait_ge(consts, START + 2)

            def transpose_z(b):
                pe.wait_ge(q_turned, START + 3 * b)
                pe.wait_ge(z_done, START + 2 * b + 2)
                for t in range(2):
                    for c in range(2):
                        mm = pe.transpose(Q_PS[0:DC, c * SEQ + t * HB:c * SEQ + (t + 1) * HB],
                                          z[:, t, c * DC:(c + 1) * DC], ident[0:HB, 0:HB])
                mm.then_inc(zT_ps, 1)

            def latent(b):
                pe.wait_ge(k_turned, START + 3 * b)
                pe.wait_ge(zT_done, START + b + 1)
                for t in range(2):
                    for c in range(2):
                        mm = pe.matmul(K_PS[0:HB, t * RANK:(t + 1) * RANK], zT[:, c, t * HB:(t + 1) * HB],
                                       wdown[:, c, :], start=(c == 0), stop=(c == 1))
                mm.then_inc(c_ps, 1)

            def transpose_c(b):
                pe.wait_ge(cz_done, START + 2 * b + 2)
                pe.sem_inc(step, 1)
                for t in range(2):
                    mm = pe.transpose(K_PS[0:RANK, t * HB:(t + 1) * HB], cz[:, t, :], ident[0:HB, 0:HB])
                mm.then_inc(cT_ps, 1)

            def project(b, g, G):
                pe.wait_ge(zT_done, START + b + 1)
                pe.wait_ge(q_turned, START + G)
                for pr in range(PG):
                    at = (PG * g + pr) * 128
                    for c in range(2):
                        mm = pe.matmul(Q_PS[:, pr * SEQ:(pr + 1) * SEQ], wq[:, c, at:at + 128], zT[:, c, :],
                                       start=(c == 0), stop=(c == 1))
                mm.then_inc(q_ps, 1)
                pe.wait_ge(cT_done, START + b + 1)
                pe.wait_ge(k_turned, START + G)
                for pr in range(PG):
                    at = (PG * g + pr) * 128
                    mm = pe.matmul(K_PS[:, pr * SEQ:(pr + 1) * SEQ], wup[:, at:at + 128], cT[:, :],
                                   start=True, stop=True)
                mm.then_inc(k_ps, 1)
                pe.wait_ge(v_done, START + G)
                for t in range(2):
                    mm = pe.matmul(V_PS[0:HB, t * 256:(t + 1) * 256], cT[:, t * HB:(t + 1) * HB],
                                   wup[:, W + g * 256:W + (g + 1) * 256], start=True, stop=True)
                mm.then_inc(v_ps, 1)

            def scores(G, g):
                pe.wait_ge(exp_done, START + 8 * G)
                pe.wait_ge(q_done, START + G + 1)
                pe.wait_ge(k_done, START + G + 1)
                for o in range(2):
                    pe.matmul(S_PS[0:HB, o, 0:480], ident_b[:, :], mask[:, :], start=True, stop=False)
                for pr in range(PG):
                    for o in range(2):
                        half = slice(o * HD, (o + 1) * HD)
                        pe.matmul(S_PS[0:HB, o, pr * HB:(pr + 1) * HB], qT[g][half, pr, A], kT[g][half, pr, A],
                                  start=False, stop=False)
                for pr in range(PG):
                    for o in range(2):
                        half = slice(o * HD, (o + 1) * HD)
                        at = 2 * HB + pr * SEQ
                        mm = pe.matmul(S_PS[0:HB, o, at:at + SEQ], qT[g][half, pr, BT], kT[g][half, pr, :],
                                       start=False, stop=(pr == PG - 1))
                mm.then_inc(s_ps, 1)

            def transpose_p(G, g):
                pe.wait_ge(pT_done, START + G)
                pe.wait_ge(prob_done, START + 2 * G + 2)
                for o in range(2):
                    for pr in range(PG):
                        for n, at in enumerate((pr * HB, 2 * HB + pr * SEQ, 2 * HB + pr * SEQ + HB)):
                            to = pr * 3 * HB + n * HB
                            mm = pe.transpose(PT_PS[0:HB, o, to:to + HB], prob[g][:, o, at:at + HB],
                                              ident[0:HB, 0:HB])
                mm.then_inc(pT_ps, 1)

            def values(b, G, g):
                pe.wait_ge(o_done, START + G)
                pe.wait_ge(h3_done, START + b)
                pe.wait_ge(v_done, START + G + 1)
                pe.wait_ge(pT_done, START + G + 1)
                for pr in range(PG):
                    for o in range(2):
                        out = O_PS[o * HD:(o + 1) * HD, pr * SEQ:(pr + 1) * SEQ]
                        cols = slice((2 * pr + o) * HD, (2 * pr + o + 1) * HD)
                        pe.matmul(out, v[g][:, 0, cols], pT[g][:, o, pr * 240:pr * 240 + SEQ], start=True, stop=False)
                        mm = pe.matmul(out[:, BT], v[g][:, 1, cols], pT[g][:, o, pr * 240 + SEQ:(pr + 1) * 240],
                                       start=False, stop=True)
                mm.then_inc(o_ps, 1)

            def output(b):
                pe.wait_ge(o_done, START + 3 * b + 3)
                for t in range(2):
                    for r in range(HEADS // 2):
                        mm = pe.matmul(O_PS[0:HB, t * D:(t + 1) * D], oT[:, r, t * HB:(t + 1) * HB], wo[:, r, :],
                                       start=(r == 0), stop=(r == HEADS // 2 - 1))
                mm.then_inc(wo_ps, 1)

            def batch(b, last):
                G = 3 * b
                project(b, 1, G + 1)
                transpose_p(G, 0)
                scores(G + 1, 1)
                values(b, G, 0)
                project(b, 2, G + 2)
                if not last:
                    transpose_z(b + 1)
                transpose_p(G + 1, 1)
                if not last:
                    latent(b + 1)
                scores(G + 2, 2)
                values(b, G + 1, 1)
                if not last:
                    transpose_c(b + 1)
                    project(b + 1, 0, G + 3)
                transpose_p(G + 2, 2)
                if not last:
                    scores(G + 3, 0)
                values(b, G + 2, 2)
                output(b)

            transpose_z(0)
            latent(0)
            transpose_c(0)
            project(0, 0, 0)
            scores(0, 0)
            with pe.Fori(0, B - 1) as b:
                batch(b, False)
            batch(B - 1, True)

        @block.vector
        def _(dve):
            dve.memset(cT[RANK:RANK + 1, :], 1.0).then_inc(consts, 1)
            dve.wait_ge(weights_in, START + 16 * 10)
            dve.tensor_scalar(wup[0:RANK, :], up_raw[:, :], ln_gb[:, 0:1], None, ALU.mult).then_inc(up_ready, 1)
            dve.wait_ge(upb_ps, START + 1)
            for n in range(3):
                dve.tensor_copy(wup[RANK:RANK + 1, 512 * n:512 * (n + 1)], (Q_PS, K_PS, V_PS)[n][0:1, 0:512]
                                ).then_inc(up_ready, 1)

            def normalise(b):
                dve.wait_ge(h_in, START + 16 * (b + 1))
                dve.wait_ge(y_in, START + 16 * (b + 1))
                dve.tensor_tensor(h2[:, :, :], h1[:, :, :], y0[:, :, :], ALU.add).then_inc(h2_done, 1)
                dve.wait_ge(h2_done, START + b + 1)
                for t in range(2):
                    dve.bn_stats(stats[:, t, :], h2[:, t, :]).then_inc(stats_done, 1)
                dve.wait_ge(stats_done, START + 2 * b + 2)
                dve.sem_inc(step, 1)
                for t in range(2):
                    dve.bn_aggr(mv[:, t, :], stats[:, t, :]).then_inc(mv_done, 1)
                dve.wait_ge(mv_done, START + 2 * b + 2)
                dve.tensor_scalar(ve[:, :], mv[:, :, 1], EPS, None, ALU.add).then_inc(ve_done, 1)
                dve.wait_ge(zT_ps, START + b)
                dve.wait_ge(rstd_done, START + b + 1)
                for t in range(2):
                    dve.tensor_scalar(z[:, t, :], h2[:, t, :], mv[:, t, 0:1], rstd[:, t:t + 1],
                                      ALU.subtract, ALU.mult).then_inc(z_done, 1)

            def normalise_latent(b):
                dve.wait_ge(c_ps, START + b + 1)
                for t in range(2):
                    dve.bn_stats(c_stats[:, t, :], K_PS[0:HB, t * RANK:(t + 1) * RANK]).then_inc(c_stats_done, 1)
                dve.wait_ge(c_stats_done, START + 2 * b + 2)
                dve.sem_inc(step, 1)
                for t in range(2):
                    dve.bn_aggr(c_mv[:, t, :], c_stats[:, t, :]).then_inc(c_mv_done, 1)
                dve.wait_ge(c_mv_done, START + 2 * b + 2)
                dve.tensor_scalar(c_ve[:, :], c_mv[:, :, 1], EPS, None, ALU.add).then_inc(c_ve_done, 1)
                dve.wait_ge(cT_ps, START + b)
                dve.wait_ge(c_rstd_done, START + b + 1)
                for t in range(2):
                    dve.tensor_scalar(cz[:, t, :], K_PS[0:HB, t * RANK:(t + 1) * RANK], c_mv[:, t, 0:1],
                                      c_rstd[:, t:t + 1], ALU.subtract, ALU.mult).then_inc(cz_done, 1)

            def rotate(G):
                for kind, ps, seen, done, turned in (("q", Q_PS, q_ps, q_done, q_turned),
                                                     ("k", K_PS, k_ps, k_done, k_turned)):
                    dve.wait_ge(done, START + G)
                    dve.wait_ge(seen, START + G + 1)
                    src = ps[:, 0:PG * SEQ].rearrange("p (r n) -> p r n", r=PG)
                    for quarter in range(4):
                        here = slice(32 * quarter, 32 * quarter + 32)
                        there = slice(32 * (quarter ^ 1), 32 * (quarter ^ 1) + 32)
                        dve.tensor_tensor(turn[kind][1][there, :, :], src[here],
                                          sin[here, :].unsqueeze(1).broadcast_to([32, PG, SEQ]), ALU.mult
                                          ).then_inc(step, 1)
                    dve.tensor_tensor(turn[kind][0][:, :, :], src,
                                      cos[:, :].unsqueeze(1).broadcast_to([128, PG, SEQ]), ALU.mult
                                      ).then_inc(turned, 1)

            def maxima(G, g):
                dve.wait_ge(s_ps, START + G + 1)
                for tile, cols in ((0, slice(0, 2 * HB)), (1, slice(2 * HB, 480))):
                    dve.tensor_reduce(top[g][:, 4 * tile:4 * tile + 4].rearrange("p (o h) -> p o h", o=2),
                                      S_PS[0:HB, :, cols].rearrange("p o (h n) -> p o h n", h=2), AX.X, ALU.max
                                      ).then_inc(top_done, 1)
                dve.wait_ge(top_done, START + 2 * G + 2)
                dve.tensor_scalar(minus_top[g][:, :], top[g][:, :], -HD ** -0.5, None, ALU.mult
                                  ).then_inc(minus_done, 1)

            def shares(G, g):
                dve.wait_ge(exp_done, START + 8 * (G + 1))
                dve.reciprocal(share[g][:, :], total[g][:, :]).then_inc(share_done, 1)

            def add(b):
                dve.wait_ge(stored, START + 32 * b)
                dve.wait_ge(res_done, START + b + 1)
                dve.wait_ge(wo_ps, START + b + 1)
                dve.tensor_tensor(h3[:, :, :], O_PS[0:HB, 0:2 * D].rearrange("p (t n) -> p t n", t=2), res[:, :, :],
                                  ALU.add).then_inc(h3_done, 1)

            def batch(b, last):
                G = 3 * b
                maxima(G, 0)
                rotate(G + 1)
                shares(G, 0)
                if not last:
                    normalise(b + 1)
                maxima(G + 1, 1)
                rotate(G + 2)
                shares(G + 1, 1)
                if not last:
                    normalise_latent(b + 1)
                maxima(G + 2, 2)
                if not last:
                    rotate(G + 3)
                shares(G + 2, 2)
                add(b)

            normalise(0)
            normalise_latent(0)
            rotate(0)
            with dve.Fori(0, B - 1) as b:
                batch(b, False)
            batch(B - 1, True)


def experts_swiglu(nc, used, w, dram, const):
    with ExitStack() as ctx:
        def sb(name, shape, dt=F32):
            return ctx.enter_context(nc.sbuf_tensor(f"e1_{name}", shape, dt))

        primed = primed_semaphores(nc, used)

        def sem(name):
            return primed(f"e1_{name}")

        bank = [ctx.enter_context(nc.psum_tensor(f"e1_bank{i}", [128, 512], F32)) for i in range(8)]
        T_PS, Y_PS = bank[0], bank[5]
        VALUE_PS, GATE_PS, AT_PS = (bank[1], bank[6]), (bank[2], bank[7]), (bank[3], bank[4])
        HC = H1 // 128
        w1 = sb("w1", [DC, 2, E1, 2 * H1])
        w2 = sb("w2", [128, HC, E1, D])
        x = [sb(f"x{i}", [128, RW]) for i in range(2)]
        to = [sb(f"to{i}", [128, 1], I32) for i in range(2)]
        scale = [sb(f"scale{i}", [128, 1]) for i in range(2)]
        xT = [sb(f"xT{i}", [DC, 2, 128]) for i in range(2)]
        silu = [sb(f"silu{i}", [128, H1]) for i in range(2)]
        act_ = [sb(f"act{i}", [128, H1]) for i in range(2)]
        aT = [sb(f"aT{i}", [128, HC, 128]) for i in range(2)]
        y = [sb(f"y{i}", [128, D]) for i in range(2)]
        ident = const["ident"]

        w_in = sem("w_in")
        x_in = [sem(f"x_in{i}") for i in range(2)]
        xT_ps = sem("xT_ps")
        xT_done = sem("xT_done")
        up_ps = sem("up_ps")
        silu_done = sem("silu_done")
        act_done = sem("act_done")
        aT_ps = sem("aT_ps")
        aT_done = sem("aT_done")
        y_ps = sem("y_ps")
        y_done = sem("y_done")
        to_done = sem("to_done")
        y_free = sem("y_free")
        step = sem("step")
        scattered = [unprimed_semaphore(nc, used, f"e1_scattered{i}") for i in range(2)]
        PER = 2 * CAPT
        block = ctx.enter_context(nc.Block())

        @block.sync
        def _(sp):
            for c in range(2):
                sp.dma_start(w1[:, c, :, :], w["e1_w1"][c * DC:(c + 1) * DC, :]
                             .rearrange("p (e n) -> p e n", e=E1)).then_inc(w_in, 16)
            for e in range(E1):
                sp.dma_start(w2[:, :, e, :], w["e1_w2"][e].rearrange("(k p) n -> p k n", p=128)).then_inc(w_in, 16)
            with sp.Fori(0, E1) as e:
                for n in range(PER):
                    p, t = n % 2, e * PER + n
                    sp.wait_ge(xT_ps, START + t - 1)
                    sp.wait_ge(to_done, START + t - 1)
                    sp.dma_start(x[p][:, :], dram["slots1"][bass.ds(t * 128, 128), :]).then_inc(x_in[p], 16)

        @block.gpsimd
        def _(pool):
            with pool.Fori(0, E1) as e:
                for n in range(PER):
                    p, t = n % 2, e * PER + n
                    pool.wait_ge(to_done, START + t + 1)
                    pool.wait_ge(y_done, START + t + 1)
                    pool.sem_inc(step, 1)
                    pool.indirect_dma_start(dram["y1"], bass.IndirectOffsetOnAxis(ap=to[p][:, 0:1], axis=0),
                                            y[p][:, :], None, bounds_check=2 * NP - 1, oob_is_err=False
                                            ).then_inc(scattered[p], 16)
                    pool.wait_ge(scattered[p], 16 * (e * CAPT + n // 2 + 1))
                    pool.sem_inc(y_free, 1)

        @block.scalar
        def _(act):
            def copy_xT(t, p):
                act.wait_ge(up_ps, START + t - 1)
                act.wait_ge(xT_ps, START + t + 1)
                act.activation(xT[p][:, :, :], T_PS[0:DC, 0:256].rearrange("p (c n) -> p c n", c=2), ACT.Copy
                               ).then_inc(xT_done, 1)

            def silus(t, p):
                act.wait_ge(act_done, START + t - 1)
                act.wait_ge(up_ps, START + t + 1)
                act.activation(silu[p][:, :], GATE_PS[p][:, :], ACT.Silu).then_inc(silu_done, 1)

            def copy_aT(t, p):
                act.wait_ge(y_ps, START + t - 1)
                act.wait_ge(aT_ps, START + t + 1)
                act.activation(aT[p][:, :, :], AT_PS[p][:, :].rearrange("p (k n) -> p k n", k=HC), ACT.Copy
                               ).then_inc(aT_done, 1)

            copy_xT(0, 0)
            with act.Fori(0, E1 - 1) as e:
                for n in range(PER):
                    t = e * PER + n
                    silus(t, n % 2)
                    copy_xT(t + 1, (n + 1) % 2)
                    copy_aT(t, n % 2)
            for n in range(PER):
                t = (E1 - 1) * PER + n
                silus(t, n % 2)
                if n < PER - 1:
                    copy_xT(t + 1, (n + 1) % 2)
                copy_aT(t, n % 2)

        @block.tensor
        def _(pe):
            pe.wait_ge(w_in, START + 16 * 10)

            def transposes(t, p, count):
                pe.wait_ge(xT_done, START + t)
                pe.wait_ge(x_in[p], START + 16 * count)
                for c in range(2):
                    mm = pe.transpose(T_PS[0:DC, c * 128:(c + 1) * 128], x[p][:, c * DC:(c + 1) * DC], ident)
                mm.then_inc(xT_ps, 1)

            def up(t, p, e):
                pe.wait_ge(act_done, START + t - 1)
                pe.wait_ge(xT_done, START + t + 1)
                for part, ps in enumerate((VALUE_PS[p], GATE_PS[p])):
                    for c in range(2):
                        mm = pe.matmul(ps[:, :], xT[p][:, c, :],
                                       w1[:, c, bass.ds(e, 1), part * H1:(part + 1) * H1]
                                       .rearrange("p a n -> p (a n)"), start=(c == 0), stop=(c == 1))
                mm.then_inc(up_ps, 1)

            def down(t, p, e):
                pe.wait_ge(y_done, START + t)
                pe.wait_ge(aT_done, START + t + 1)
                for k in range(HC):
                    mm = pe.matmul(Y_PS[:, 0:D], aT[p][:, k, :],
                                   w2[:, k, bass.ds(e, 1), :].rearrange("p a n -> p (a n)"),
                                   start=(k == 0), stop=(k == HC - 1))
                mm.then_inc(y_ps, 1)

            def turn(t, p):
                pe.wait_ge(aT_done, START + t - 1)
                pe.wait_ge(act_done, START + t + 1)
                for k in range(HC):
                    mm = pe.transpose(AT_PS[p][:, k * 128:(k + 1) * 128], act_[p][:, k * 128:(k + 1) * 128], ident)
                mm.then_inc(aT_ps, 1)

            def steps(e, last):
                for n in range(PER):
                    t = e * PER + n
                    more = not (last and n == PER - 1)
                    nxt = (n + 1) % 2
                    if more:
                        transposes(t + 1, nxt, e * CAPT + (n + 1) // 2 + 1)
                        up(t + 1, nxt, e if n < PER - 1 else e + 1)
                    turn(t, n % 2)
                    down(t, n % 2, e)

            transposes(0, 0, 1)
            up(0, 0, 0)
            with pe.Fori(0, E1 - 1) as e:
                steps(e, False)
            steps(E1 - 1, True)

        @block.vector
        def _(dve):
            def steps(e):
                for n in range(PER):
                    p, t, k = n % 2, e * PER + n, n // CAPT
                    dve.wait_ge(y_free, START + t - 1)
                    dve.wait_ge(x_in[p], START + 16 * (e * CAPT + n // 2 + 1))
                    dve.tensor_copy(scale[p][:, :], x[p][:, D + k:D + k + 1]).then_inc(step, 1)
                    dve.tensor_copy(to[p][:, :], x[p][:, D + 2 + k:D + 3 + k].bitcast(I32)).then_inc(to_done, 1)
                    dve.wait_ge(aT_ps, START + t - 1)
                    dve.wait_ge(silu_done, START + t + 1)
                    dve.tensor_tensor(act_[p][:, :], VALUE_PS[p][:, :], silu[p][:, :], ALU.mult).then_inc(act_done, 1)
                    dve.wait_ge(to_done, START + t + 1)
                    dve.wait_ge(y_ps, START + t + 1)
                    dve.tensor_scalar(y[p][:, :], Y_PS[:, 0:D], scale[p][:, 0:1], None, ALU.mult).then_inc(y_done, 1)

            with dve.Fori(0, E1) as e:
                steps(e)


def combine(nc, used, w, dram, const, out):
    CH = 4
    WIDTH = N * D // 128 // CH
    with ExitStack() as ctx:
        def flat(src):
            return src.rearrange("r c -> (r c)").rearrange("(p q n) -> q p n", p=128, q=CH)

        primed = primed_semaphores(nc, used)
        part = [[ctx.enter_context(nc.sbuf_tensor(f"s_{n}{i}", [128, WIDTH], F32)) for i in range(CH)]
                for n in ("h3", "first", "second")]
        loaded = [primed(f"s_loaded{i}") for i in range(CH)]
        summed = primed("s_summed")
        final = primed("s_final")
        stored = primed("s_stored")
        block = ctx.enter_context(nc.Block())

        @block.sync
        def _(sp):
            for i in range(CH):
                for tiles, src in zip(part, (dram["h3"][0:N, :], dram["y1"][0:N, :], dram["y1"][NP:NP + N, :])):
                    sp.dma_start(tiles[i][:, :], flat(src)[i]).then_inc(loaded[i], 16)
            for i in range(CH):
                sp.wait_ge(final, START + i + 1)
                sp.dma_start(flat(out.rearrange("b t c -> (b t) c"))[i], part[0][i][:, :]).then_inc(stored, 16)
            sp.wait_ge(stored, START + 16 * CH)

        @block.vector
        def _(dve):
            for i in range(CH):
                dve.wait_ge(loaded[i], START + 48)
                dve.tensor_tensor(part[1][i][:, :], part[1][i][:, :], part[2][i][:, :], ALU.add).then_inc(summed, 1)
                dve.wait_ge(summed, START + i + 1)
                dve.tensor_tensor(part[0][i][:, :], part[0][i][:, :], part[1][i][:, :], ALU.add).then_inc(final, 1)


def build(nc, w, out):
    with ExitStack() as ctx:
        def scratch(name, rows, width=D):
            return nc.dram_tensor(name, [rows, width], F32).ap()

        dram = {"h0": scratch("h0", N + 1), "h1": scratch("h1", NP), "h3": scratch("h3", NP),
                "slots0": scratch("slots0", ROWS0, RW), "slots1": scratch("slots1", ROWS1, RW),
                "y0": scratch("y0", NP), "y1": scratch("y1", 2 * NP)}
        const = {}
        for name, shape, dt in (("ident", [128, 128], F32), ("ones", [128, 128], BF16), ("before", [128, 128], BF16),
                                ("expert_no", [128, 8], F32), ("tile_rows", [1, TILES], F32),
                                ("tile_no", [1, TILES0], F32)):
            const[name] = ctx.enter_context(nc.sbuf_tensor(name, shape, dt))[:, :]
        made = {name: ctx.enter_context(nc.sbuf_tensor(name, [1, TILES0], I32))[:, :]
                for name in ("tile_row", "tile_expert")}
        used = []
        embed_patches(nc, used, w, dram, const)
        const.update(made)
        attend_squared(nc, used, w, dram, const)
        dispatch(nc, used, w, dram, const, 0)
        experts_gelu(nc, used, w, dram, const)
        clear_semaphores(nc, used)
        attend_causal(nc, used, w, dram, const)
        dispatch(nc, used, w, dram, const, 1)
        experts_swiglu(nc, used, w, dram, const)
        combine(nc, used, w, dram, const, out)


def _layouts(a):
    BF = mybir.dt.np(BF16)

    def f(name):
        return np.asarray(a[name])

    x = f("x")[:, :, :GRID * PATCH, :GRID * PATCH].reshape(B, 3, GRID, PATCH, GRID, PATCH)
    rows = np.zeros((B, 3 * KP, IMG), np.float32)
    rows[:, :300, 1:] = x.transpose(0, 1, 3, 5, 2, 4).reshape(B, 300, IMG - 1)
    rows[:, 300, 1:] = 1
    rows[:, 301, 0] = 1
    tok_w = np.zeros((3 * KP, D), np.float32)
    tok_w[:300] = f("L0_tok_W").T
    tok_w[300] = f("L0_tok_b")
    tok_w[301] = f("L0_tok_cls").reshape(-1)
    inv = np.float32(1) / np.float32(10000) ** (np.arange(0, HD, 2, dtype=np.float32) / np.float32(HD))
    angle = np.tile(inv[:, None] * np.arange(SEQ, dtype=np.float32)[None], (4, 1)).astype(np.float32)
    sign = np.tile(np.repeat(np.array([1, -1], np.float32), HD // 2), 2)[:, None]
    rows80 = np.arange(HB)[:, None]
    mask = np.concatenate([np.where(np.arange(HB)[None] <= rows80, 0, -1e30)] * 2
                          + [np.where(np.arange(SEQ)[None] <= rows80 + HB, 0, -1e30)] * 2, 1)
    out = {
        "patches": rows.reshape(B, 3, KP, IMG).transpose(0, 2, 1, 3).reshape(B, KP, 3 * IMG),
        "tok_w": tok_w.reshape(3, KP, D).transpose(1, 0, 2).reshape(KP, 3 * D),
        "tok_gamma": np.broadcast_to(f("L0_tok_gamma"), (IMG, D)),
        "tok_beta": np.broadcast_to(f("L0_tok_beta"), (IMG, D)),
        "txt": f("txt"),
        "ident": np.eye(128, dtype=np.float32),
        "attn0_w": np.concatenate([f(f"L0_attn_W{n}_w").T for n in "uqkv"], 1),
        "attn0_b": np.concatenate([f(f"L0_attn_W{n}_b") for n in "uqkv"])[None],
        "attn0_ln": np.stack([f("L0_attn_ln_gamma"), f("L0_attn_ln_beta")], 1),
        "attn0_wo": f("L0_attn_Wo_w").T,
        "attn0_bo": f("L0_attn_Wo_b")[None],
        "ones": np.ones((128, 128), BF),
        "before": np.triu(np.ones((128, 128), BF), 1),
        "expert_no": np.broadcast_to(np.arange(8, dtype=np.float32), (128, 8)),
        "tile_rows": np.arange(TILES, dtype=np.float32)[None] * 128,
        "tile_no": np.arange(TILES0, dtype=np.float32)[None],
        "gate0_w": f("L0_ffn_gate_w"),
        "gate0_b": f("L0_ffn_gate_b")[None],
        "gate0_centre": f("L0_ffn_gate_center")[None],
        "e0_w1": f("L0_ffn_w1").transpose(1, 0, 2).reshape(D, E0 * H0),
        "e0_b1": f("L0_ffn_b1").reshape(1, E0 * H0),
        "e0_w2": f("L0_ffn_w2"),
        "e0_b2": f("L0_ffn_b2"),
        "wq": f("L1_attn_Wq"),
        "wdown": f("L1_attn_Wdown"),
        "wup": f("L1_attn_Wup"),
        "attn1_ln": np.stack([f("L1_attn_ln_g"), f("L1_attn_ln_b")], 1),
        "wo1": f("L1_attn_Wo"),
        "bo": np.broadcast_to(f("L1_attn_bo"), (HB, D)),
        "cos": np.cos(angle),
        "sin": np.sin(angle) * sign,
        "mask": mask.astype(BF),
        "ident_b": np.eye(HB, dtype=BF),
        "gate1_w": f("L1_ffn_Wg"),
        "e1_w1": f("L1_ffn_W1").transpose(1, 0, 2).reshape(D, E1 * 2 * H1),
        "e1_w2": f("L1_ffn_W2"),
    }
    return {k: np.ascontiguousarray(v) for k, v in out.items()}


def kernel(**inputs):
    import concourse.bacc as _bacc
    from concourse.bass_utils import run_bass_kernel_spmd as _run

    nc = _bacc.Bacc("TRN2", target_bir_lowering=False, num_devices=1)
    arrays = {f"in_{k}": v for k, v in _layouts(inputs).items()}
    w = {k[3:]: nc.dram_tensor(k, v.shape, mybir.dt.from_np(v.dtype), kind="ExternalInput").ap()
         for k, v in arrays.items()}
    out = nc.dram_tensor("out_0", (B, T, D), F32, kind="ExternalOutput").ap()
    build(nc, w, out)
    r = _run(nc, [arrays], core_ids=[0])
    return r.results[0]["out_0"]
```

```python
from contextlib import ExitStack

import numpy as np

import concourse.bass as bass
from concourse import mybir

F32 = mybir.dt.float32
F32R = mybir.dt.float32r
BF16 = mybir.dt.bfloat16
I32 = mybir.dt.int32
U32 = mybir.dt.uint32
ALU = mybir.AluOpType
ACT = mybir.ActivationFunctionType
AX = mybir.AxisListType

B = 16
PATCH = 10
GRID = 96 // PATCH
IMG = GRID * GRID + 1
TXT = 77
T = IMG + TXT
D = 192
N = B * T
EPS = 1e-5
HB = T // 2 + 1
SEQ = 2 * HB
TILES = -(-N // 128)
NP = TILES * 128
KP = 112
DC = D // 2

E0, H0 = 4, 768
TILES0 = (NP + E0 * 127) // 128
TILES0 += TILES0 % 2
FILL = 13
ROWS0 = -(-(E0 * NP + TILES0 * 128) // (FILL * 128)) * FILL * 128
E1, H1 = 8, 512
CAP = int(1.2 * N / E1)
CAPT = -(-CAP // 128)
CAPR = CAPT * 128
ROWS1 = E1 * 2 * CAPR
RW = D + 4
NOWHERE = 1 << 20

HEADS, HD, RANK = 12, 64, 64


PARTS = ((0, 0), (0, 1), (1, 0))


START = 8


def primed_semaphores(nc, used):
    engines = [nc.sync, nc.scalar, nc.vector, nc.gpsimd, nc.tensor]

    def sem(name):
        s = nc.alloc_semaphore(name)
        engines[len(used) % len(engines)].sem_inc(s, START)
        used.append(s)
        return s

    return sem


def unprimed_semaphore(nc, used, name):
    s = nc.alloc_semaphore(name)
    used.append(s)
    return s


def clear_semaphores(nc, used):
    nc.clear_and_free_semaphores(used)
    used.clear()
    nc.all_engine_barrier()


def rows_of(dram, b):
    return dram[bass.ds(b * T, SEQ), :].rearrange("(t p) c -> p t c", p=HB)


def causal_weights(ctx, nc):
    def sb(name, shape, dt=F32):
        return ctx.enter_context(nc.sbuf_tensor(f"c_{name}", shape, dt))

    return {"wq": sb("wq", [DC, 2, HEADS * HD]),
            "wdown": sb("wdown", [DC, 2, RANK]),
            "wk": sb("wk", [DC, HEADS * HD]),
            "wvo": sb("wvo", [128, HEADS // 2, D]),
            "bias": sb("bias", [HB, D]),
            "cos": sb("cos", [128, SEQ]),
            "sin": sb("sin", [128, SEQ]),
            "mask": sb("mask", [HB, 2 * HB + 2 * SEQ], BF16),
            "ident_b": sb("ident_b", [HB, HB], BF16)}


def embed_patches(nc, used, w, dram, const, causal):
    R = 4
    PAIRS = HEADS // 2
    with ExitStack() as ctx:
        def sb(name, shape, dt=F32):
            return ctx.enter_context(nc.sbuf_tensor(name, shape, dt))

        sem = primed_semaphores(nc, used)

        bank = [ctx.enter_context(nc.psum_tensor(f"tok_bank{i}", [128, 512], F32)) for i in range(R)]
        zeros = sb("pad_zeros", [NP - N, D])
        tok_w = sb("tok_w", [KP, 3, D])
        gamma = sb("tok_gamma", [IMG, D])
        beta = sb("tok_beta", [IMG, D])
        minus_half = sb("tok_minus_half", [IMG, R])
        patches = [sb(f"patches{i}", [KP, 3 * IMG]) for i in range(R)]
        stats = sb("tok_stats", [IMG, R, 6])
        mv = sb("tok_mv", [IMG, R, 2])
        ve = sb("tok_ve", [IMG, R])
        rstd = sb("tok_rstd", [IMG, R])
        centred = sb("tok_centred", [IMG, R, D])
        scaled = sb("tok_scaled", [IMG, R, D])
        y = sb("tok_y", [IMG, R, D])

        prep_bank = [ctx.enter_context(nc.psum_tensor(f"prep_bank{i}", [128, 512], F32)) for i in range(4)]
        wq, wdown, wk, wvo = (causal[name] for name in ("wq", "wdown", "wk", "wvo"))
        up_k = sb("prep_up_k", [RANK, HEADS * HD])
        up_vT = sb("prep_up_vT", [128, PAIRS, RANK])
        latent_gb = sb("prep_latent_gb", [128, 2])
        latent_b = sb("prep_latent_b", [128, HB])
        wo = sb("prep_wo", [128, PAIRS, D])
        wvo_raw = sb("prep_wvo_raw", [128, PAIRS, D])
        bo = sb("prep_bo", [HB, D])

        prep_in = sem("prep_in")
        prep_step = sem("prep_step")
        wide_done = sem("prep_wide_done")
        bias_ps = sem("prep_bias_ps")
        wk_done = sem("prep_wk_done")
        wvo_ps = sem("prep_wvo_ps")
        raw_done = sem("prep_raw_done")
        wvo_done = sem("prep_wvo_done")
        out_bias_ps = sem("prep_out_bias_ps")
        bias_done = sem("prep_bias_done")
        PREP_LOADS = 11
        weights_in = sem("tok_weights_in")
        patches_in = [sem(f"patches_in{i}") for i in range(R)]
        const_in = sem("const_in")
        fill_ready = sem("fill_ready")
        filled = sem("filled")
        tok_ps = sem("tok_ps")
        stats_done = sem("tok_stats_done")
        mv_done = sem("tok_mv_done")
        ve_done = sem("tok_ve_done")
        rstd_done = sem("tok_rstd_done")
        centred_done = sem("tok_centred_done")
        scaled_done = sem("tok_scaled_done")
        y_done = sem("tok_y_done")
        stored = sem("tok_stored")
        vector_step = sem("tok_vector_step")
        block = ctx.enter_context(nc.Block())

        @block.sync
        def _(sp):
            sp.dma_start(tok_w[:, :, :], w["tok_w"].rearrange("p (c n) -> p c n", c=3)).then_inc(weights_in, 16)
            with sp.Fori(0, B // R) as i:
                for p in range(R):
                    sp.wait_ge(tok_ps, START + R * (i - 1) + p + 1)
                    sp.dma_start(patches[p][:, :], w["patches"][bass.ds(R * i + p, 1), :, :]
                                 .rearrange("a p n -> (a p) n")).then_inc(patches_in[p], 16)
            for tile, src in ((wdown, w["wdown"].rearrange("(c p) n -> p c n", c=2)),
                              (wq, w["wq"].rearrange("(c p) n -> p c n", c=2)),
                              (wo, w["wo1"].rearrange("(k p) n -> p k n", p=128)),
                              (up_vT, w["up_vT"].rearrange("(k p) n -> p k n", p=128))):
                sp.dma_start(tile[:, :, :], src).then_inc(prep_in, 16)
            for tile, name in ((up_k, "up_k"), (latent_gb, "attn1_ln"), (bo, "bo"), (causal["cos"], "cos"),
                               (causal["sin"], "sin"), (causal["mask"], "mask"), (causal["ident_b"], "ident_b")):
                sp.dma_start(tile[:, :], w[name]).then_inc(prep_in, 16)
            for name, tile in const.items():
                sp.dma_start(tile, w[name]).then_inc(const_in, 16)
            sp.wait_ge(const_in, START + 16 * len(const))

        @block.scalar
        def _(act):
            act.dma_start(gamma[:, :], w["tok_gamma"]).then_inc(weights_in, 16)
            act.dma_start(beta[:, :], w["tok_beta"]).then_inc(weights_in, 16)
            act.dma_start(dram["h0"][0:N, :].rearrange("(b t) c -> b t c", t=T)[:, IMG:T, :], w["txt"]
                          ).then_inc(filled, 16)
            act.wait_ge(fill_ready, START + 1)
            act.dma_start(dram["h0"][N:N + 1, :], zeros[0:1, :]).then_inc(filled, 16)
            act.dma_start(dram["h1"][N:NP, :], zeros[:, :]).then_inc(filled, 16)
            act.dma_start(dram["h3"][N:NP, :], zeros[:, :]).then_inc(filled, 16)
            with act.Fori(0, B // R) as i:
                act.wait_ge(y_done, START + i + 1)
                act.dma_start(dram["h0"][bass.ds(R * i * T, R * T), :].rearrange("(b t) c -> t b c", t=T)[0:IMG, :, :],
                              y[:, :, :]).then_inc(stored, 16)
            act.wait_ge(wvo_ps, START + 3)
            for i in range(3):
                act.activation(wvo_raw[:, 2 * i:2 * i + 2, :], prep_bank[i][:, 0:2 * D]
                               .rearrange("p (c n) -> p c n", c=2), ACT.Copy).then_inc(raw_done, 1)
            act.wait_ge(stored, START + 16 * (B // R))
            act.wait_ge(filled, START + 16 * 4)

        @block.gpsimd
        def _(pool):
            pool.memset(zeros[:, :], 0.0).then_inc(fill_ready, 1)
            pool.memset(minus_half[:, :], -0.5).then_inc(fill_ready, 1)
            pool.wait_ge(fill_ready, START + 2)
            with pool.Fori(0, B // R) as i:
                pool.wait_ge(ve_done, START + i + 1)
                pool.tensor_tensor(rstd[:, :], ve[:, :], minus_half[:, :], ALU.pow).then_inc(rstd_done, 1)

        @block.tensor
        def _(pe):
            pe.wait_ge(weights_in, START + 48)
            with pe.Fori(0, B // R) as i:
                for p in range(R):
                    pe.wait_ge(centred_done, START + R * (i - 1) + p + 1)
                    pe.wait_ge(patches_in[p], START + 16 * (i + 1))
                    for c in range(3):
                        mm = pe.matmul(bank[p][0:IMG, 0:D], patches[p][:, c * IMG:(c + 1) * IMG], tok_w[:, c, :],
                                       start=(c == 0), stop=(c == 2))
                    mm.then_inc(tok_ps, 1)
            pe.wait_ge(prep_in, START + 16 * PREP_LOADS)
            for i in range(3):
                for j in range(2):
                    for o in range(2):
                        half = slice(o * HD, (o + 1) * HD)
                        mm = pe.matmul(prep_bank[i][half, j * D:(j + 1) * D], up_vT[half, 2 * i + j, :],
                                       wo[half, 2 * i + j, :], start=True, stop=True)
                mm.then_inc(wvo_ps, 1)
            for i in range(2):
                pe.wait_ge(centred_done, START + B)
                mm = pe.matmul(bank[i][0:1, 0:2 * D], latent_gb[0:RANK, 1:2], up_k[:, 2 * D * i:2 * D * (i + 1)],
                               start=True, stop=True)
            mm.then_inc(bias_ps, 1)
            pe.wait_ge(raw_done, START + 3)
            pe.wait_ge(wide_done, START + 1)
            for k in range(PAIRS):
                mm = pe.matmul(prep_bank[3][0:HB, 0:D], latent_b[:, :], wvo_raw[:, k, :], start=(k == 0),
                               stop=(k == PAIRS - 1))
            mm.then_inc(out_bias_ps, 1)

        @block.vector
        def _(dve):
            dve.wait_ge(weights_in, START + 48)
            with dve.Fori(0, B // R) as i:
                for p in range(R):
                    dve.wait_ge(tok_ps, START + R * i + p + 1)
                    dve.bn_stats(stats[:, p, :], bank[p][0:IMG, 0:D]).then_inc(stats_done, 1)
                dve.wait_ge(stats_done, START + R * (i + 1))
                dve.sem_inc(vector_step, 1)
                for p in range(R):
                    dve.bn_aggr(mv[:, p, :], stats[:, p, :]).then_inc(mv_done, 1)
                dve.wait_ge(mv_done, START + R * (i + 1))
                dve.tensor_scalar(ve[:, :], mv[:, :, 1], EPS, None, ALU.add).then_inc(ve_done, 1)
                dve.wait_ge(rstd_done, START + i + 1)
                dve.wait_ge(scaled_done, START + i)
                for p in range(R):
                    dve.tensor_scalar(centred[:, p, :], bank[p][0:IMG, 0:D], mv[:, p, 0:1], rstd[:, p:p + 1],
                                      ALU.subtract, ALU.mult).then_inc(centred_done, 1)
                dve.wait_ge(centred_done, START + R * (i + 1))
                dve.wait_ge(y_done, START + i)
                dve.tensor_tensor(scaled[:, :, :], centred[:, :, :], gamma[:, :].unsqueeze(1).broadcast_to([IMG, R, D]),
                                  ALU.mult).then_inc(scaled_done, 1)
                dve.wait_ge(stored, START + 16 * i)
                dve.wait_ge(scaled_done, START + i + 1)
                dve.tensor_tensor(y[:, :, :], scaled[:, :, :], beta[:, :].unsqueeze(1).broadcast_to([IMG, R, D]),
                                  ALU.add).then_inc(y_done, 1)
            dve.memset(wk[RANK:DC, :], 0.0).then_inc(prep_step, 1)
            dve.memset(latent_b[:, :], 1.0).then_inc(prep_step, 1)
            dve.wait_ge(prep_step, START + 2)
            dve.wait_ge(prep_in, START + 16 * PREP_LOADS)
            dve.tensor_scalar(latent_b[:, :], latent_b[:, :], latent_gb[:, 1:2], None, ALU.mult).then_inc(wide_done, 1)
            dve.tensor_scalar(wk[0:RANK, :], up_k[:, :], latent_gb[0:RANK, 0:1], None, ALU.mult).then_inc(wk_done, 1)
            dve.wait_ge(bias_ps, START + 1)
            for i in range(2):
                dve.tensor_copy(wk[RANK:RANK + 1, 2 * D * i:2 * D * (i + 1)], bank[i][0:1, 0:2 * D]
                                ).then_inc(wk_done, 1)
            dve.wait_ge(raw_done, START + 3)
            for i in range(3):
                dve.tensor_scalar(wvo[:, 2 * i:2 * i + 2, :], wvo_raw[:, 2 * i:2 * i + 2, :], latent_gb[:, 0:1], None,
                                  ALU.mult).then_inc(wvo_done, 1)
            dve.wait_ge(out_bias_ps, START + 1)
            dve.tensor_tensor(causal["bias"][:, :], prep_bank[3][0:HB, 0:D], bo[:, :], ALU.add).then_inc(bias_done, 1)


def attend_squared(nc, used, w, dram, const):
    with ExitStack() as ctx:
        def sb(name, shape, dt=F32):
            return ctx.enter_context(nc.sbuf_tensor(name, shape, dt))

        sem = primed_semaphores(nc, used)

        bank = [ctx.enter_context(nc.psum_tensor(f"a_bank{i}", [128, 512], F32)) for i in range(8)]
        w_raw = sb("w_raw", [DC, 2, 4 * D])
        w_all = sb("w_all", [DC + 1, 2, 4 * D])
        b_all = sb("b_all", [1, 4 * D])
        ln_gb = sb("ln_gb", [DC, 2, 2])
        wo = sb("wo0", [DC + 1, 2, D])
        minus_half = sb("a_minus_half", [HB, 2])
        empty_rows = sb("empty_rows", [128, FILL, RW])
        h_norm = [sb(f"h_norm{i}", [HB, 2, D]) for i in range(2)]
        h_res = [sb(f"h_res{i}", [HB, 2, D]) for i in range(2)]
        stats = [sb(f"a_stats{i}", [HB, 2, 6]) for i in range(2)]
        mv = [sb(f"a_mv{i}", [HB, 2, 2]) for i in range(2)]
        ve = [sb(f"a_ve{i}", [HB, 2]) for i in range(2)]
        rstd = [sb(f"a_rstd{i}", [HB, 2]) for i in range(2)]
        z = [sb(f"a_z{i}", [HB, 2, D]) for i in range(2)]
        zT = [sb(f"a_zT{i}", [DC + 1, 2, SEQ]) for i in range(2)]
        uT = [sb(f"a_uT{i}", [DC, 2, SEQ]) for i in range(4)]
        qT = [sb(f"a_qT{i}", [DC, 2, SEQ]) for i in range(2)]
        kT = [sb(f"a_kT{i}", [DC, 2, SEQ]) for i in range(2)]
        v = [sb(f"a_v{i}", [HB, 2, D]) for i in range(4)]
        relu = [sb(f"a_relu{i}", [HB, 2, SEQ]) for i in range(2)]
        aT = [sb(f"a_aT{i}", [HB, 2, SEQ]) for i in range(2)]
        gT = [sb(f"a_gT{i}", [DC + 1, 2, SEQ]) for i in range(2)]
        h1 = [sb(f"a_h1_{i}", [HB, 2, D]) for i in range(2)]
        ident = const["ident"]
        U, Q, K, V = range(4)

        weights_in = sem("a_weights_in")
        norm_in = [sem(f"h_norm_in{i}") for i in range(2)]
        res_in = [sem(f"h_res_in{i}") for i in range(2)]
        gamma_done = sem("gamma_done")
        bias_ps = sem("bias_ps")
        w_ready = sem("a_w_ready")
        consts = sem("a_consts")
        fill_ready = sem("a_fill_ready")
        filled = sem("a_filled")
        stats_done = sem("a_stats_done")
        mv_done = sem("a_mv_done")
        ve_done = sem("a_ve_done")
        rstd_done = sem("a_rstd_done")
        z_done = sem("a_z_done")
        zT_ps = sem("a_zT_ps")
        zT_done = sem("a_zT_done")
        proj_ps = sem("a_proj_ps")
        silu_done = sem("a_silu_done")
        sim_ps = sem("a_sim_ps")
        relu_done = sem("a_relu_done")
        aT_done = sem("a_aT_done")
        av_ps = sem("a_av_ps")
        gT_done = sem("a_gT_done")
        wo_ps = sem("a_wo_ps")
        h1_done = sem("a_h1_done")
        stored = [sem(f"a_stored{i}") for i in range(2)]
        vector_step = sem("a_vector_step")
        block = ctx.enter_context(nc.Block())
        PAIRS = B // 2

        def run(engine, pair):
            for m in range(2):
                pair(m, m, m == 0, False)
            with engine.Fori(1, PAIRS // 2 - 1) as j:
                for m in range(2):
                    pair(2 * j + m, m, False, False)
            for m in range(2):
                pair(PAIRS - 2 + m, m, False, m == 1)

        @block.sync
        def _(sp):
            sp.dma_start(w_raw[:, :, :], w["attn0_w"].rearrange("(c p) n -> p c n", c=2)).then_inc(weights_in, 16)
            sp.dma_start(b_all[:, :], w["attn0_b"]).then_inc(weights_in, 16)
            sp.dma_start(ln_gb[:, :, :], w["attn0_ln"].rearrange("(c p) n -> p c n", c=2)).then_inc(weights_in, 16)
            sp.dma_start(wo[0:DC, :, :], w["attn0_wo"].rearrange("(c p) n -> p c n", c=2)).then_inc(weights_in, 16)
            sp.dma_start(wo[DC:DC + 1, 0, :], w["attn0_bo"]).then_inc(weights_in, 16)

            def load(i):
                for p in range(2):
                    sp.wait_ge(z_done, START + 4 * i)
                    sp.dma_start(h_norm[p][:, :, :], rows_of(dram["h0"], 2 * i + p)).then_inc(norm_in[p], 16)

            def load_residual(i):
                for p in range(2):
                    sp.wait_ge(h1_done, START + 2 * i)
                    sp.dma_start(h_res[p][:, :, :], rows_of(dram["h0"], 2 * i + p)).then_inc(res_in[p], 16)

            def store(i):
                for p in range(2):
                    b = 2 * i + p
                    sp.wait_ge(h1_done, START + b + 1)
                    sp.dma_start(dram["h1"][bass.ds(b * T, HB), :], h1[p][:, 0, :]).then_inc(stored[p], 16)
                    sp.dma_start(dram["h1"][bass.ds(b * T + HB, T - HB), :], h1[p][0:T - HB, 1, :]
                                 ).then_inc(stored[p], 16)

            load(0)
            load(1)
            load_residual(0)
            with sp.Fori(1, PAIRS - 1) as i:
                load(i + 1)
                store(i - 1)
                load_residual(i)
            store(PAIRS - 2)
            load_residual(PAIRS - 1)
            store(PAIRS - 1)
            for p in range(2):
                sp.wait_ge(stored[p], START + 32 * PAIRS)

        @block.gpsimd
        def _(pool):
            pool.memset(minus_half[:, :], -0.5).then_inc(consts, 1)
            pool.memset(empty_rows[:, :, 0:D + 2], 0.0).then_inc(fill_ready, 1)
            pool.memset(empty_rows[:, :, D + 2:RW].bitcast(I32), NOWHERE).then_inc(fill_ready, 1)
            pool.wait_ge(fill_ready, START + 2)
            for p in range(2):
                pool.memset(zT[p][DC:DC + 1, :, :], 1.0).then_inc(consts, 1)
                pool.memset(gT[p][DC:DC + 1, :, :], 1.0).then_inc(consts, 1)
            pool.wait_ge(consts, START + 5)

            def scales(i):
                for p in range(2):
                    pool.wait_ge(ve_done, START + 2 * i + p + 1)
                    pool.tensor_tensor(rstd[p][:, :], ve[p][:, :], minus_half[:, :], ALU.pow).then_inc(rstd_done, 1)

            def squares(i):
                for p in range(2):
                    b = 2 * i + p
                    pool.wait_ge(av_ps, START + 2 * i)
                    pool.wait_ge(relu_done, START + b + 1)
                    pool.tensor_tensor(aT[p][:, :, :], relu[p][:, :, :], relu[p][:, :, :], ALU.mult
                                       ).then_inc(aT_done, 1)

            scales(0)
            with pool.Fori(0, PAIRS - 1) as i:
                scales(i + 1)
                squares(i)
            squares(PAIRS - 1)

        @block.scalar
        def _(act):
            def copy_zT(b, p):
                act.wait_ge(proj_ps, START + 4 * (b - p))
                act.wait_ge(zT_ps, START + b + 1)
                act.activation(zT[p][0:DC, :, :], bank[0][0:DC, 0:2 * SEQ].rearrange("p (c n) -> p c n", c=2),
                               ACT.Copy).then_inc(zT_done, 1)

            def pair(i, m, first, last):
                for p in range(2):
                    b = 2 * i + p
                    act.wait_ge(sim_ps, START + 2 * i)
                    act.wait_ge(av_ps, START + 2 * (i - 1))
                    act.wait_ge(gT_done, START + 2 * (i - 1))
                    for n, (bk, tile) in enumerate(((1, qT[p]), (2, kT[p]), (3, v[2 * m + p]), (4, uT[2 * m + p]))):
                        act.wait_ge(proj_ps, START + 4 * b + n + 1)
                        rows, width = (HB, D) if n == 2 else (DC, SEQ)
                        act.activation(tile[:, :, :],
                                       bank[bk][0:rows, 0:2 * width].rearrange("p (c n) -> p c n", c=2),
                                       ACT.Silu).then_inc(silu_done, 1)
                for p in range(2):
                    b = 2 * i + p
                    act.wait_ge(aT_done, START + 2 * i)
                    act.wait_ge(sim_ps, START + b + 1)
                    act.activation(relu[p][:, :, :], bank[5][0:HB, 0:2 * SEQ].rearrange("p (c n) -> p c n", c=2),
                                   ACT.Relu, scale=float(T) ** -0.5).then_inc(relu_done, 1)
                    if not last:
                        copy_zT(b + 2, p)

            for p in range(2):
                copy_zT(p, p)
            act.wait_ge(fill_ready, START + 2)
            for r in range(0, ROWS0, FILL * 128):
                act.dma_start(dram["slots0"][r:r + FILL * 128, :].rearrange("(p j) c -> p j c", j=FILL),
                              empty_rows[:, :, :]).then_inc(filled, 16)
            run(act, pair)
            act.wait_ge(filled, START + 16 * (ROWS0 // (FILL * 128)))

        @block.tensor
        def _(pe):
            pe.wait_ge(weights_in, START + 80)
            for half in range(2):
                for c in range(2):
                    mm = pe.matmul(bank[1 + half][0:1, 0:2 * D], ln_gb[:, c, 1:2],
                                   w_raw[:, c, half * 2 * D:(half + 1) * 2 * D], start=(c == 0), stop=(c == 1))
            mm.then_inc(bias_ps, 1)
            pe.wait_ge(w_ready, START + 2 + 2)
            pe.wait_ge(consts, START + 5)

            def transposes(b, p):
                pe.wait_ge(zT_done, START + b)
                pe.wait_ge(z_done, START + 2 * b + 2)
                for t in range(2):
                    for c in range(2):
                        mm = pe.transpose(bank[0][0:DC, c * SEQ + t * HB:c * SEQ + (t + 1) * HB],
                                          z[p][:, t, c * DC:(c + 1) * DC], ident[0:HB, 0:HB])
                mm.then_inc(zT_ps, 1)

            def project(b, p, n):
                kind, bk = (Q, K, V, U)[n], n + 1
                pe.wait_ge(silu_done, START + 4 * (b - 1) + n + 1)
                pe.wait_ge(zT_done, START + b + 1)
                for half in range(2):
                    for c in range(2):
                        rows = DC + 1 if c == 0 else DC
                        if kind == V:
                            mm = pe.matmul(bank[bk][0:HB, half * D:(half + 1) * D],
                                           zT[p][0:rows, c, half * HB:(half + 1) * HB],
                                           w_all[0:rows, c, V * D:(V + 1) * D], start=(c == 0), stop=(c == 1))
                        else:
                            at = kind * D + half * DC
                            mm = pe.matmul(bank[bk][0:DC, half * SEQ:(half + 1) * SEQ],
                                           w_all[0:rows, c, at:at + DC], zT[p][0:rows, c, :],
                                           start=(c == 0), stop=(c == 1))
                mm.then_inc(proj_ps, 1)

            def scores(b, p):
                pe.wait_ge(relu_done, START + b)
                pe.wait_ge(silu_done, START + 4 * b + 2)
                for t in range(2):
                    for c in range(2):
                        mm = pe.matmul(bank[5][0:HB, t * SEQ:(t + 1) * SEQ], kT[p][:, c, t * HB:(t + 1) * HB],
                                       qT[p][:, c, :], start=(c == 0), stop=(c == 1))
                mm.then_inc(sim_ps, 1)

            def values(b, p, m):
                pe.wait_ge(gT_done, START + b)
                pe.wait_ge(silu_done, START + 4 * b + 3)
                pe.wait_ge(aT_done, START + b + 1)
                for c in range(2):
                    for t in range(2):
                        rows = HB if t == 0 else T - HB
                        mm = pe.matmul(bank[6][0:DC, c * SEQ:(c + 1) * SEQ],
                                       v[2 * m + p][0:rows, t, c * DC:(c + 1) * DC], aT[p][0:rows, t, :],
                                       start=(t == 0), stop=(t == 1))
                mm.then_inc(av_ps, 1)

            def outputs(b, p):
                pe.wait_ge(h1_done, START + b)
                pe.wait_ge(gT_done, START + b + 1)
                for t in range(2):
                    for c in range(2):
                        rows = DC + 1 if c == 0 else DC
                        mm = pe.matmul(bank[7][0:HB, t * D:(t + 1) * D], gT[p][0:rows, c, t * HB:(t + 1) * HB],
                                       wo[0:rows, c, :], start=(c == 0), stop=(c == 1))
                mm.then_inc(wo_ps, 1)

            def pair(i, m, first, last):
                for p in range(2):
                    b = 2 * i + p
                    for n in range(4):
                        project(b, p, n)
                        if p == 0 and n in (0, 2) and not first:
                            values(b - 2 + n // 2, n // 2, m ^ 1)
                        if (p, n) == (0, 3) and not first:
                            outputs(b - 2, 0)
                        if (p, n) == (1, 1) and not first:
                            outputs(b - 2, 1)
                for p in range(2):
                    scores(2 * i + p, p)
                    if not last:
                        transposes(2 * i + 2 + p, p)

            for p in range(2):
                transposes(p, p)
            run(pe, pair)
            for p in range(2):
                values(B - 2 + p, p, 1)
            for p in range(2):
                outputs(B - 2 + p, p)

        @block.vector
        def _(dve):
            dve.wait_ge(weights_in, START + 80)
            for c in range(2):
                dve.tensor_scalar(w_all[0:DC, c, :], w_raw[:, c, :], ln_gb[:, c, 0:1], None, ALU.mult
                                  ).then_inc(w_ready, 1)
            dve.wait_ge(bias_ps, START + 1)
            for half in range(2):
                dve.tensor_tensor(w_all[DC:DC + 1, 0, half * 2 * D:(half + 1) * 2 * D], bank[1 + half][0:1, 0:2 * D],
                                  b_all[:, half * 2 * D:(half + 1) * 2 * D], ALU.add).then_inc(w_ready, 1)

            def normalise(i):
                for p in range(2):
                    dve.wait_ge(norm_in[p], START + 16 * (i + 1))
                    for t in range(2):
                        dve.bn_stats(stats[p][:, t, :], h_norm[p][:, t, :]).then_inc(stats_done, 1)
                for p in range(2):
                    b = 2 * i + p
                    dve.wait_ge(stats_done, START + 2 * b + 2)
                    dve.sem_inc(vector_step, 1)
                    for t in range(2):
                        dve.bn_aggr(mv[p][:, t, :], stats[p][:, t, :]).then_inc(mv_done, 1)
                for p in range(2):
                    b = 2 * i + p
                    dve.wait_ge(mv_done, START + 2 * b + 2)
                    dve.tensor_scalar(ve[p][:, :], mv[p][:, :, 1], 1.0 + EPS, EPS * EPS, ALU.mult, ALU.add
                                      ).then_inc(ve_done, 1)
                for p in range(2):
                    b = 2 * i + p
                    dve.wait_ge(zT_ps, START + 2 * i)
                    dve.wait_ge(rstd_done, START + b + 1)
                    for t in range(2):
                        dve.tensor_scalar(z[p][:, t, :], h_norm[p][:, t, :], mv[p][:, t, 0:1], rstd[p][:, t:t + 1],
                                          ALU.subtract, ALU.mult).then_inc(z_done, 1)

            def gate_and_add(i, m):
                for p in range(2):
                    b = 2 * i + p
                    dve.wait_ge(wo_ps, START + 2 * i)
                    dve.wait_ge(silu_done, START + 4 * b + 4)
                    dve.wait_ge(av_ps, START + b + 1)
                    dve.tensor_tensor(gT[p][0:DC, :, :], bank[6][0:DC, 0:2 * SEQ].rearrange("p (c n) -> p c n", c=2),
                                      uT[2 * m + p][:, :, :], ALU.mult).then_inc(gT_done, 1)
                for p in range(2):
                    b = 2 * i + p
                    dve.wait_ge(stored[p], START + 32 * i)
                    dve.wait_ge(res_in[p], START + 16 * (i + 1))
                    dve.wait_ge(wo_ps, START + b + 1)
                    dve.tensor_tensor(h1[p][:, :, :], bank[7][0:HB, 0:2 * D].rearrange("p (t n) -> p t n", t=2),
                                      h_res[p][:, :, :], ALU.add).then_inc(h1_done, 1)

            def pair(i, m, first, last):
                if not first:
                    gate_and_add(i - 1, m ^ 1)
                if not last:
                    normalise(i + 1)

            normalise(0)
            run(dve, pair)
            gate_and_add(PAIRS - 1, 1)


def dispatch(nc, used, w, dram, const, layer, load_ahead):
    experts, top = (E0, 1) if layer == 0 else (E1, 2)
    region = NP if layer == 0 else CAPR
    h, slots = dram["h1" if layer == 0 else "h3"], dram[f"slots{layer}"]
    GT = 5
    GROUPS = TILES // GT
    M = top * experts
    with ExitStack() as ctx:
        def sb(name, shape, dt=F32):
            return ctx.enter_context(nc.sbuf_tensor(f"r{layer}_{name}", shape, dt))

        primed = primed_semaphores(nc, used)

        def sem(name):
            return primed(f"r{layer}_{name}")

        bank = [ctx.enter_context(nc.psum_tensor(f"r{layer}_bank{i}", [128, 512], F32)) for i in range(8)]
        gate = sb("gate", [DC + 1, 2, experts])
        centre = sb("centre", [DC + 1, experts])
        minus_half = sb("minus_half", [128, GT])
        hg = [sb(f"h{i}", [128, GT, D]) for i in range(GROUPS)]
        rows = [sb(f"rows{i}", [128, GT, RW]) for i in range(GROUPS)]
        stats = [sb(f"stats{i}", [128, GT, 6]) for i in range(GROUPS)]
        mv = [sb(f"mv{i}", [128, GT, 2]) for i in range(GROUPS)]
        ve = [sb(f"ve{i}", [128, GT]) for i in range(GROUPS)]
        rstd = [sb(f"rstd{i}", [128, GT]) for i in range(GROUPS)]
        zT = [sb(f"zT{i}", [DC + 1, GT, 2, 128]) for i in range(GROUPS)]
        logits = [sb(f"logits{i}", [128, GT, 8]) for i in range(GROUPS)]
        best = [sb(f"best{i}", [128, GT, 8]) for i in range(GROUPS)]
        best_at = [sb(f"best_at{i}", [128, GT, 8], U32) for i in range(GROUPS)]
        chosen = [sb(f"chosen{i}", [128, GT, top, experts], BF16) for i in range(GROUPS)]
        rank = [sb(f"rank{i}", [128, GT, M]) for i in range(GROUPS)]
        mine = [sb(f"mine{i}", [128, GT, M]) for i in range(GROUPS)]
        place = [sb(f"place{i}", [128, GT, top]) for i in range(GROUPS)]
        over = [sb(f"over{i}", [128, GT, top]) for i in range(GROUPS)]
        base = [sb(f"base{i}", [128, GT, top]) for i in range(GROUPS)]
        kept = [sb(f"kept{i}", [128, GT, top]) for i in range(GROUPS)]
        slot = [sb(f"slot{i}", [128, GT * top], I32) for i in range(GROUPS)]
        gap = [sb(f"gap{i}", [128, GT]) for i in range(GROUPS)]
        ex = [sb(f"ex{i}", [128, GT]) for i in range(GROUPS)]
        den = [sb(f"den{i}", [128, GT]) for i in range(GROUPS)]
        seen = sb("seen", [128, M])
        full = sb("full", [1, E0, TILES])
        in_use = sb("in_use", [1, E0])
        ends = sb("ends", [1, E0])
        past = sb("past", [1, TILES0, E0 - 1])
        expert_f = sb("expert_f", [1, TILES0])
        skipped = sb("skipped", [1, TILES0, E0 - 1])
        skip = sb("skip", [1, TILES0])
        own = sb("own", [1, TILES0])
        first = sb("first", [1, TILES0])
        expert_no, before, ones = const["expert_no"], const["before"], const["ones"]
        ident = const["ident"]

        gate_in = sem("gate_in")
        h_in = [sem(f"h_in{i}") for i in range(GROUPS)]
        consts = sem("consts")
        rowno = sem("rowno")
        gate_ready = sem("gate_ready")
        stats_done = sem("stats_done")
        mv_done = sem("mv_done")
        ve_done = sem("ve_done")
        rstd_done = sem("rstd_done")
        z_done = sem("z_done")
        zT_ps = sem("zT_ps")
        zT_done = sem("zT_done")
        logits_ps = sem("logits_ps")
        logits_done = sem("logits_done")
        best_done = sem("best_done")
        at_done = sem("at_done")
        chosen_done = sem("chosen_done")
        rank_ps = sem("rank_ps")
        rank_done = sem("rank_done")
        seen_done = sem("seen_done")
        base_done = sem("base_done")
        den_done = sem("den_done")
        first_done = sem("first_done")
        mine_done = sem("mine_done")
        place_done = sem("place_done")
        over_done = sem("over_done")
        kept_done = sem("kept_done")
        table = sem("table")
        gap_done = sem("gap_done")
        ex_done = sem("ex_done")
        weights_done = sem("weights_done")
        slot_done = sem("slot_done")
        scattered = unprimed_semaphore(nc, used, f"r{layer}_scattered")
        block = ctx.enter_context(nc.Block())

        @block.sync
        def _(sp):
            sp.dma_start(gate[0:DC, :, :], w[f"gate{layer}_w"].rearrange("(c p) n -> p c n", c=2)).then_inc(gate_in, 16)
            if layer == 0:
                sp.dma_start(gate[DC:DC + 1, 0, :], w["gate0_b"]).then_inc(gate_in, 16)
                sp.dma_start(centre[DC:DC + 1, :], w["gate0_centre"]).then_inc(gate_in, 16)
            for g in range(GROUPS):
                sp.dma_start(hg[g][:, :, :], h[g * GT * 128:(g + 1) * GT * 128, :]
                             .rearrange("(j p) c -> p j c", p=128)).then_inc(h_in[g], 16)
            load_ahead(sp)

        @block.gpsimd
        def _(pool):
            pool.memset(minus_half[:, :], -0.5).then_inc(consts, 1)
            for g in range(GROUPS):
                pool.memset(rows[g][:, :, D:D + 2], 1.0).then_inc(rowno, 1)
                for k in range(2):
                    pool.iota(rows[g][:, :, D + 2 + k:D + 3 + k].bitcast(I32), pattern=[[128, GT], [0, 1]],
                              base=k * NP + g * GT * 128, channel_multiplier=1).then_inc(rowno, 1)
            pool.wait_ge(consts, START + 1)
            pool.wait_ge(rowno, START + 3 * GROUPS)
            for g in range(GROUPS):
                pool.wait_ge(ve_done, START + g + 1)
                pool.tensor_tensor(rstd[g][:, :], ve[g][:, :], minus_half[:, :], ALU.pow).then_inc(rstd_done, 1)
            for g in range(GROUPS):
                pool.wait_ge(z_done, START + GT * (g + 1))
                if layer:
                    pool.wait_ge(weights_done, START + g + 1)
                pool.wait_ge(slot_done, START + g + 1)
                for j in range(GT):
                    for k in range(top):
                        pool.indirect_dma_start(
                            slots, bass.IndirectOffsetOnAxis(ap=slot[g][:, j * top + k:j * top + k + 1], axis=0),
                            rows[g][:, j, :], None, bounds_check=slots.shape[0] - 1, oob_is_err=False
                        ).then_inc(scattered, 16)
            pool.wait_ge(scattered, 16 * TILES * top)

        @block.scalar
        def _(act):
            def copy_zT(g):
                for n in range(GT):
                    act.wait_ge(zT_ps, START + GT * g + n + 1)
                    act.activation(zT[g][0:DC, n, :, :], bank[n][0:DC, 0:256].rearrange("p (c n) -> p c n", c=2),
                                   ACT.Copy).then_inc(zT_done, 1)

            def exps(g):
                act.wait_ge(gap_done, START + g + 1)
                act.activation(ex[g][:, :], gap[g][:, :], ACT.Exp).then_inc(ex_done, 1)

            copy_zT(0)
            copy_zT(1)
            for g in range(GROUPS):
                if layer:
                    exps(g)
                if g + 2 < GROUPS:
                    copy_zT(g + 2)

        @block.tensor
        def _(pe):
            pe.wait_ge(gate_ready, START + GROUPS + 1)

            def transposes(g):
                for j in range(GT):
                    pe.wait_ge(zT_done, START + GT * (g - 1) + j + 1)
                    pe.wait_ge(z_done, START + GT * g + j + 1)
                    for c in range(2):
                        mm = pe.transpose(bank[j][0:DC, c * 128:(c + 1) * 128],
                                          rows[g][:, j, c * DC:(c + 1) * DC], ident)
                    mm.then_inc(zT_ps, 1)

            def gates(g):
                pe.wait_ge(logits_done, START + g)
                pe.wait_ge(zT_done, START + GT * (g + 1))
                for j in range(GT):
                    for c in range(2):
                        k = DC + 1 if c == 0 and layer == 0 else DC
                        mm = pe.matmul(bank[5][:, 8 * j:8 * j + experts], zT[g][0:k, j, c, :], gate[0:k, c, :],
                                       start=(c == 0), stop=(c == 1))
                mm.then_inc(logits_ps, 1)

            def ranks(g):
                out = bank[6 + g % 2]
                pe.wait_ge(seen_done, START + g)
                pe.wait_ge(chosen_done, START + top * (g + 1))
                for j in range(GT):
                    for earlier in range(j + 1):
                        pe.matmul(out[:, M * j:M * (j + 1)], before if earlier == j else ones,
                                  chosen[g][:, earlier, :, :].rearrange("p k e -> p (k e)"),
                                  start=(earlier == 0), stop=(earlier == j))
                for j in range(GT):
                    mm = pe.matmul(out[:, 128:128 + M], ones, chosen[g][:, j, :, :].rearrange("p k e -> p (k e)"),
                                   start=(j == 0), stop=(j == GT - 1))
                mm.then_inc(rank_ps, 1)

            transposes(0)
            transposes(1)
            gates(0)
            gates(1)
            for g in range(GROUPS):
                ranks(g)
                if g + 2 < GROUPS:
                    transposes(g + 2)
                    gates(g + 2)

        @block.vector
        def _(dve):
            dve.memset(seen[:, :], 0.0).then_inc(seen_done, 1)
            for g in range(GROUPS):
                dve.memset(logits[g][:, :, :], -3e38).then_inc(consts, 1)
                dve.memset(zT[g][DC:DC + 1, :, :, :], 1.0).then_inc(gate_ready, 1)
            if layer == 0:
                dve.wait_ge(gate_in, START + 48)
                dve.tensor_tensor(gate[DC:DC + 1, 0, :], gate[DC:DC + 1, 0, :], centre[DC:DC + 1, :], ALU.subtract
                                  ).then_inc(gate_ready, 1)
            else:
                dve.wait_ge(gate_in, START + 16)
                dve.sem_inc(gate_ready, 1)
            dve.wait_ge(consts, START + GROUPS + 1)
            dve.wait_ge(seen_done, START + 1)
            dve.wait_ge(rowno, START + 3 * GROUPS)
            numbers = expert_no[:, 0:experts].unsqueeze(1).broadcast_to([128, GT, experts])

            def measure(g):
                dve.wait_ge(h_in[g], START + 16)
                for j in range(GT):
                    dve.bn_stats(stats[g][:, j, :], hg[g][:, j, :]).then_inc(stats_done, 1)
                dve.wait_ge(stats_done, START + GT * (g + 1))
                for j in range(GT):
                    dve.bn_aggr(mv[g][:, j, :], stats[g][:, j, :]).then_inc(mv_done, 1)
                dve.wait_ge(mv_done, START + GT * (g + 1))
                dve.tensor_scalar(ve[g][:, :], mv[g][:, :, 1], EPS, None, ALU.add).then_inc(ve_done, 1)

            def normalise(g):
                dve.wait_ge(rstd_done, START + g + 1)
                for j in range(GT):
                    dve.tensor_scalar(rows[g][:, j, 0:D], hg[g][:, j, :], mv[g][:, j, 0:1], rstd[g][:, j:j + 1],
                                      ALU.subtract, ALU.mult).then_inc(z_done, 1)

            def choose(g):
                dve.wait_ge(logits_ps, START + g + 1)
                dve.tensor_copy(logits[g][:, :, 0:experts],
                                bank[5][:, 0:8 * GT].rearrange("p (j e) -> p j e", e=8)[:, :, 0:experts]
                                ).then_inc(logits_done, 1)
                dve.wait_ge(logits_done, START + g + 1)
                for j in range(GT):
                    dve.max(best[g][:, j, :], logits[g][:, j, :]).then_inc(best_done, 1)
                dve.wait_ge(best_done, START + GT * (g + 1))
                for j in range(GT):
                    dve.max_index(best_at[g][:, j, :], best[g][:, j, :], logits[g][:, j, :]).then_inc(at_done, 1)
                dve.wait_ge(at_done, START + GT * (g + 1))
                for k in range(top):
                    dve.tensor_tensor(chosen[g][:, :, k, :], numbers,
                                      best_at[g][:, :, k:k + 1].broadcast_to([128, GT, experts]),
                                      ALU.is_equal).then_inc(chosen_done, 1)
                if layer:
                    dve.tensor_tensor(gap[g][:, :], best[g][:, :, 1], best[g][:, :, 0], ALU.subtract
                                      ).then_inc(gap_done, 1)
                for k in range(top):
                    dve.tensor_scalar(base[g][:, :, k], best_at[g][:, :, k], float(region * top),
                                      float(k * region), ALU.mult, ALU.add).then_inc(base_done, 1)

            def weights(g):
                dve.wait_ge(ex_done, START + g + 1)
                dve.tensor_scalar(den[g][:, :], ex[g][:, :], 1.0, None, ALU.add).then_inc(den_done, 1)
                dve.wait_ge(den_done, START + g + 1)
                dve.reciprocal(rows[g][:, :, D], den[g][:, :]).then_inc(first_done, 1)
                dve.wait_ge(first_done, START + g + 1)
                dve.tensor_tensor(rows[g][:, :, D + 1], ex[g][:, :], rows[g][:, :, D], ALU.mult
                                  ).then_inc(weights_done, 1)

            def slots_of(g):
                dve.wait_ge(rank_ps, START + g + 1)
                dve.wait_ge(seen_done, START + g + 1)
                out = bank[6 + g % 2]
                dve.tensor_tensor(rank[g][:, :, :], out[:, 0:M * GT].rearrange("p (j m) -> p j m", m=M),
                                  seen[:, :].unsqueeze(1).broadcast_to([128, GT, M]), ALU.add).then_inc(rank_done, 1)
                dve.wait_ge(rank_done, START + g + 1)
                dve.tensor_tensor(seen[:, :], out[:, 128:128 + M], seen[:, :], ALU.add).then_inc(seen_done, 1)
                dve.tensor_tensor(mine[g][:, :, :], rank[g][:, :, :],
                                  chosen[g][:, :, :, :].rearrange("p j k e -> p j (k e)"), ALU.mult
                                  ).then_inc(mine_done, 1)
                dve.wait_ge(mine_done, START + g + 1)
                dve.tensor_reduce(place[g][:, :, :].rearrange("p j k -> p (j k)"),
                                  mine[g][:, :, :].rearrange("p j (k e) -> p (j k) e", k=top), AX.X, ALU.add
                                  ).then_inc(place_done, 1)
                dve.wait_ge(place_done, START + g + 1)
                dve.tensor_scalar(over[g][:, :, :], place[g][:, :, :], float(CAP if layer else NP),
                                  float(NOWHERE), ALU.is_ge, ALU.mult).then_inc(over_done, 1)
                dve.wait_ge(base_done, START + top * (g + 1))
                dve.tensor_tensor(kept[g][:, :, :], place[g][:, :, :], base[g][:, :, :], ALU.add
                                  ).then_inc(kept_done, 1)
                dve.wait_ge(over_done, START + g + 1)
                dve.wait_ge(kept_done, START + g + 1)
                dve.tensor_tensor(slot[g][:, :].rearrange("p (j k) -> p j k", k=top), kept[g][:, :, :],
                                  over[g][:, :, :], ALU.add).then_inc(slot_done, 1)

            measure(0)
            measure(1)
            normalise(0)
            normalise(1)
            measure(2)
            measure(3)
            for g in range(GROUPS):
                choose(g)
                if g + 2 < GROUPS:
                    normalise(g + 2)
                if layer:
                    weights(g)
                slots_of(g)
            if layer == 0:
                counted = seen[0:1, :]
                dve.wait_ge(seen_done, START + GROUPS + 1)
                dve.tensor_tensor(full[:, :, :], counted.unsqueeze(2).broadcast_to([1, E0, TILES]),
                                  const["tile_rows"][:, 0:TILES].unsqueeze(1).broadcast_to([1, E0, TILES]), ALU.is_gt
                                  ).then_inc(table, 1)
                dve.wait_ge(table, START + 1)
                dve.tensor_reduce(in_use[:, :], full[:, :, :], AX.X, ALU.add).then_inc(table, 1)
                dve.wait_ge(table, START + 2)
                dve.tensor_copy(ends[:, 0:1], in_use[:, 0:1]).then_inc(table, 1)
                for e in range(1, E0):
                    dve.wait_ge(table, START + 2 + e)
                    dve.tensor_tensor(ends[:, e:e + 1], ends[:, e - 1:e], in_use[:, e:e + 1], ALU.add
                                      ).then_inc(table, 1)
                dve.wait_ge(table, START + 2 + E0)
                dve.tensor_tensor(past[:, :, :], const["tile_no"].unsqueeze(2).broadcast_to([1, TILES0, E0 - 1]),
                                  ends[:, 0:E0 - 1].unsqueeze(1).broadcast_to([1, TILES0, E0 - 1]), ALU.is_ge
                                  ).then_inc(table, 1)
                dve.wait_ge(table, START + 3 + E0)
                dve.tensor_reduce(expert_f[:, :], past[:, :, :], AX.X, ALU.add).then_inc(table, 1)
                dve.tensor_tensor(skipped[:, :, :], past[:, :, :],
                                  in_use[:, 0:E0 - 1].unsqueeze(1).broadcast_to([1, TILES0, E0 - 1]), ALU.mult
                                  ).then_inc(table, 1)
                dve.wait_ge(table, START + 5 + E0)
                dve.tensor_reduce(skip[:, :], skipped[:, :, :], AX.X, ALU.add).then_inc(table, 1)
                dve.wait_ge(table, START + 6 + E0)
                dve.tensor_tensor(own[:, :], const["tile_no"], skip[:, :], ALU.subtract).then_inc(table, 1)
                dve.tensor_scalar(first[:, :], expert_f[:, :], float(NP), None, ALU.mult).then_inc(table, 1)
                dve.wait_ge(table, START + 8 + E0)
                dve.scalar_tensor_tensor(const["tile_row"], own[:, :], 128.0, first[:, :], ALU.mult, ALU.add
                                         ).then_inc(table, 1)
                dve.tensor_scalar(const["tile_expert"], expert_f[:, :], 1.0, None, ALU.mult).then_inc(table, 1)


def gelu_weights(nc, used, ctx):
    sem = primed_semaphores(nc, used)
    return {"w1": ctx.enter_context(nc.sbuf_tensor("e0_w1", [DC + 1, 2, E0, H0], F32)),
            "w2": ctx.enter_context(nc.sbuf_tensor("e0_w2", [128, H0 // 128, E0, D], F32)),
            "in": sem("e0_w_in")}


def load_gelu(sp, w, weights):
    w1, w2, w_in = weights["w1"], weights["w2"], weights["in"]
    for c in range(2):
        sp.dma_start(w1[0:DC, c, :, :], w["e0_w1"][c * DC:(c + 1) * DC, :]
                     .rearrange("p (e n) -> p e n", e=E0)).then_inc(w_in, 16)
    sp.dma_start(w1[DC:DC + 1, 0, :, :], w["e0_b1"].rearrange("p (e n) -> p e n", e=E0)).then_inc(w_in, 16)
    for e in range(E0):
        sp.dma_start(w2[:, :, e, :], w["e0_w2"][e].rearrange("(k p) n -> p k n", p=128)).then_inc(w_in, 16)


def experts_gelu(nc, used, w, dram, const, weights):
    w1, w2, w_in = weights["w1"], weights["w2"], weights["in"]
    TURN, DOWN = 1, 2
    BODY = 4
    with ExitStack() as ctx:
        def sb(name, shape, dt=F32):
            return ctx.enter_context(nc.sbuf_tensor(f"e0_{name}", shape, dt))

        primed = primed_semaphores(nc, used)

        def sem(name):
            return primed(f"e0_{name}")

        bank = [ctx.enter_context(nc.psum_tensor(f"e0_bank{i}", [128, n, 512], F32))
                for i, n in enumerate((1, 2, 2, 2, 1))]
        T_PS, Y_PS = bank[0], bank[4]
        UP_PS, HT_PS = (bank[1], bank[2]), bank[3]
        HC = H0 // 128
        x = [sb(f"x{i}", [128, RW]) for i in range(BODY)]
        to = [sb(f"to{i}", [128, 1], I32) for i in range(BODY)]
        b2 = [sb(f"b2_{i}", [128, D]) for i in range(BODY)]
        xT = [sb(f"xT{i}", [DC + 1, 2, 128]) for i in range(2)]
        hid = [sb(f"hid{i}", [128, H0]) for i in range(2)]
        hT = [sb(f"hT{i}", [128, HC, 128]) for i in range(2)]
        y = [sb(f"y{i}", [128, D]) for i in range(2)]
        empty_rows = sb("empty_rows", [128, 2 * CAPT, RW])
        zeros = sb("zeros", [128, 2 * D * NP // 128 // 4])
        ident = const["ident"]

        x_in = [sem(f"x_in{i}") for i in range(BODY)]
        b2_in = [sem(f"b2_in{i}") for i in range(BODY)]
        consts = sem("consts")
        xT_ps = sem("xT_ps")
        xT_done = sem("xT_done")
        up_ps = sem("up_ps")
        hid_done = sem("hid_done")
        hT_ps = sem("hT_ps")
        hT_done = sem("hT_done")
        y_ps = sem("y_ps")
        y_done = sem("y_done")
        to_done = sem("to_done")
        y_free = sem("y_free")
        fill_ready = sem("fill_ready")
        filled = sem("filled")
        pool_step = sem("pool_step")
        scattered = [unprimed_semaphore(nc, used, f"e0_scattered{i}") for i in range(2)]
        block = ctx.enter_context(nc.Block())

        def run(engine, tile):
            for n in range(BODY):
                tile(0, n, True, False)
            with engine.Fori(1, TILES0 // BODY - 1) as i:
                for n in range(BODY):
                    tile(i, n, False, False)
            for n in range(BODY):
                tile(TILES0 // BODY - 1, n, False, n == BODY - 1)

        @block.sync
        def _(sp):
            with sp.Fori(0, TILES0 // BODY) as i:
                for n in range(BODY):
                    t = BODY * i + n
                    row = sp.value_load(const["tile_row"][0:1, bass.ds(t, 1)], min_val=0, max_val=ROWS0 - 128)
                    expert = sp.value_load(const["tile_expert"][0:1, bass.ds(t, 1)], min_val=0, max_val=E0 - 1)
                    sp.wait_ge(xT_ps, START + t - BODY + 1)
                    sp.wait_ge(to_done, START + t - BODY + 1)
                    sp.dma_start(x[n][:, :], dram["slots0"][bass.ds(row, 128), :]).then_inc(x_in[n], 16)
                    sp.wait_ge(y_done, START + t - BODY + 1)
                    sp.dma_start(b2[n][:, :], w["e0_b2"][bass.ds(expert, 1), :].broadcast_to([128, D])
                                 ).then_inc(b2_in[n], 16)

        @block.gpsimd
        def _(pool):
            pool.memset(empty_rows[:, :, 0:D + 2], 0.0).then_inc(fill_ready, 1)
            pool.memset(empty_rows[:, :, D + 2:RW].bitcast(I32), NOWHERE).then_inc(fill_ready, 1)
            pool.memset(zeros[:, :], 0.0).then_inc(fill_ready, 1)
            with pool.Fori(0, TILES0 // BODY) as i:
                for n in range(BODY):
                    t, p = BODY * i + n, n % 2
                    pool.wait_ge(to_done, START + t + 1)
                    pool.wait_ge(y_done, START + t + 1)
                    pool.sem_inc(pool_step, 1)
                    pool.indirect_dma_start(dram["y0"], bass.IndirectOffsetOnAxis(ap=to[n][:, 0:1], axis=0), y[p][:, :],
                                            None, bounds_check=NP - 1, oob_is_err=False).then_inc(scattered[p], 16)
                    pool.wait_ge(scattered[p], 16 * (BODY // 2 * i + n // 2 + 1))
                    pool.sem_inc(y_free, 1)

        @block.scalar
        def _(act):
            def units(t, p):
                act.wait_ge(hT_ps, START + t - 1)
                act.wait_ge(up_ps, START + t + 1)
                act.activation(hid[p][:, :].rearrange("p (n f) -> p n f", n=2), UP_PS[p][:, :, 0:H0 // 2],
                               ACT.Gelu).then_inc(hid_done, 1)

            for p in range(2):
                units(p, p)
            act.wait_ge(fill_ready, START + 3)
            for e in range(E1):
                rows = 2 * CAPR
                act.dma_start(dram["slots1"][e * rows:(e + 1) * rows, :].rearrange("(p j) c -> p j c", p=128),
                              empty_rows[:, :, :]).then_inc(filled, 16)
            for r in range(0, 2 * NP, NP // 2):
                act.dma_start(dram["y1"][r:r + NP // 2, :].rearrange("(p j) c -> p (j c)", p=128), zeros[:, :]
                              ).then_inc(filled, 16)
            with act.Fori(1, TILES0 // 2) as i:
                for p in range(2):
                    units(2 * i + p, p)
            act.wait_ge(filled, START + 16 * (E1 + 4))

        @block.tensor
        def _(pe):
            def transposes(t, n, loaded):
                pe.wait_ge(xT_done, START + t)
                pe.wait_ge(x_in[n], loaded)
                for c in range(2):
                    mm = pe.transpose(T_PS[0:DC, 0, c * 128:(c + 1) * 128], x[n][:, c * DC:(c + 1) * DC], ident)
                mm.then_inc(xT_ps, 1)

            def expert_of(t):
                return pe.value_load(const["tile_expert"][0:1, bass.ds(t, 1)], min_val=0, max_val=E0 - 1)

            def up(t, p):
                expert = expert_of(t)
                pe.wait_ge(hid_done, START + t - 1)
                pe.wait_ge(xT_done, START + t + 1)
                for half in range(2):
                    for c in range(2):
                        k = DC + 1 if c == 0 else DC
                        mm = pe.matmul(UP_PS[p][:, half, 0:H0 // 2], xT[p][0:k, c, :],
                                       w1[0:k, c, bass.ds(expert, 1), half * H0 // 2:(half + 1) * H0 // 2]
                                       .rearrange("p a n -> p (a n)"), start=(c == 0), stop=(c == 1))
                mm.then_inc(up_ps, 1)

            def turn(t, p):
                pe.wait_ge(hT_done, START + 2 * t)
                pe.wait_ge(hid_done, START + t + 1)
                for k in range(HC):
                    mm = pe.transpose(HT_PS[:, k // 3, k % 3 * 128:(k % 3 + 1) * 128],
                                      hid[p][:, k * 128:(k + 1) * 128], ident)
                mm.then_inc(hT_ps, 1)

            def down(t, p):
                expert = expert_of(t)
                pe.wait_ge(y_done, START + t)
                pe.wait_ge(hT_done, START + 2 * t + 2)
                for k in range(HC):
                    mm = pe.matmul(Y_PS[:, 0, 0:D], hT[p][:, k, :],
                                   w2[:, k, bass.ds(expert, 1), :].rearrange("p a n -> p (a n)"),
                                   start=(k == 0), stop=(k == HC - 1))
                mm.then_inc(y_ps, 1)

            def tile(i, n, first, last):
                t = BODY * i + n
                up(t, n % 2)
                if not last:
                    transposes(t + 1, (n + 1) % BODY, START + 16 * (i + (2 if n == BODY - 1 else 1)))
                if n >= TURN or not first:
                    turn(t - TURN, (n - TURN) % 2)
                if n >= DOWN or not first:
                    down(t - DOWN, n % 2)

            pe.wait_ge(consts, START + 2)
            transposes(0, 0, START + 16)
            pe.wait_ge(w_in, START + 16 * (3 + E0))
            run(pe, tile)
            turn(TILES0 - 1, 1)
            down(TILES0 - 2, 0)
            down(TILES0 - 1, 1)

        @block.vector
        def _(dve):
            for p in range(2):
                dve.memset(xT[p][DC:DC + 1, :, :], 1.0).then_inc(consts, 1)

            def copy_xT(t, p):
                dve.wait_ge(up_ps, START + t - 1)
                dve.wait_ge(xT_ps, START + t + 1)
                dve.tensor_copy(xT[p][0:DC, :, :], T_PS[0:DC, 0, 0:256].rearrange("p (c n) -> p c n", c=2)
                                ).then_inc(xT_done, 1)

            def copy_to(t, n):
                dve.wait_ge(y_free, START + t - BODY + 1)
                dve.tensor_copy(to[n][:, :], x[n][:, D + 2:D + 3].bitcast(I32)).then_inc(to_done, 1)

            def copy_hT(t, p):
                dve.wait_ge(y_ps, START + t - 1)
                dve.wait_ge(hT_ps, START + t + 1)
                for half in range(2):
                    dve.tensor_copy(hT[p][:, 3 * half:3 * half + 3, :],
                                    HT_PS[:, half, 0:384].rearrange("p (k n) -> p k n", k=3)).then_inc(hT_done, 1)

            def result(t, p, n, loaded):
                dve.wait_ge(y_free, START + t - 1)
                dve.wait_ge(b2_in[n], loaded)
                dve.wait_ge(y_ps, START + t + 1)
                dve.tensor_tensor(y[p][:, :], Y_PS[:, 0, 0:D], b2[n][:, :], ALU.add).then_inc(y_done, 1)

            def tile(i, n, first, last):
                t = BODY * i + n
                if not last:
                    copy_xT(t + 1, (n + 1) % 2)
                    copy_to(t + 1, (n + 1) % BODY)
                if n >= TURN or not first:
                    copy_hT(t - TURN, (n - TURN) % 2)
                if n >= DOWN or not first:
                    result(t - DOWN, n % 2, (n - DOWN) % BODY, START + 16 * (i + (1 if n >= DOWN else 0)))

            copy_xT(0, 0)
            copy_to(0, 0)
            run(dve, tile)
            copy_hT(TILES0 - 1, 1)
            result(TILES0 - 2, 0, BODY - 2, START + 16 * (TILES0 // BODY))
            result(TILES0 - 1, 1, BODY - 1, START + 16 * (TILES0 // BODY))


def attend_causal(nc, used, w, dram, const, causal):
    SCORE, SHARE, TURN, VALUE, OUT = 2, 3, 4, 5, 6
    PAIRS = HEADS // 2
    A, BT = slice(0, HB), slice(HB, SEQ)
    AK = slice(0, 2 * HB)
    BK = slice(2 * HB, 2 * HB + 2 * SEQ)
    KB = DC
    with ExitStack() as ctx:
        def sb(name, shape, dt=F32):
            return ctx.enter_context(nc.sbuf_tensor(f"c_{name}", shape, dt))

        primed = primed_semaphores(nc, used)

        def sem(name):
            return primed(f"c_{name}")

        def psum(name):
            return ctx.enter_context(nc.psum_tensor(f"c_{name}", [128, 512], F32))

        QK_PS = [psum(f"qk_ps{i}") for i in range(2)]
        S_PS = [psum(f"s_ps{i}") for i in range(2)]
        PT_PS = [psum(f"pT_ps{i}") for i in range(2)]
        X_PS, W_PS = psum("x_ps"), psum("w_ps")
        O_PS = X_PS[:, 0:SEQ]
        Z_PS = X_PS[:, SEQ:3 * SEQ]
        OUT_PS = W_PS[0:HB, 0:2 * D]
        wq, wk, wvo, wdown, bias, cos, sin, mask, ident_b = (
            causal[name] for name in ("wq", "wk", "wvo", "wdown", "bias", "cos", "sin", "mask", "ident_b"))
        minus_half = sb("minus_half", [HB, 2])
        h1 = sb("h1", [HB, 2, D])
        y0 = sb("y0", [HB, 2, D])
        h2 = [sb(f"h2_{i}", [HB, 2, D]) for i in range(2)]
        res = [sb(f"res{i}", [HB, 2, D]) for i in range(2)]
        h3 = sb("h3", [HB, 2, D])
        stats = sb("stats", [HB, 2, 6])
        mv = sb("mv", [HB, 2, 2])
        ve = sb("ve", [HB, 2])
        rstd = sb("rstd", [HB, 2])
        z = sb("z", [HB, 2, D])
        zT = [sb(f"zT{i}", [DC, 2, SEQ]) for i in range(2)]
        c = sb("c", [HB, 2, RANK])
        c_stats = sb("c_stats", [HB, 2, 6])
        c_mv = sb("c_mv", [HB, 2, 2])
        c_ve = sb("c_ve", [HB, 2])
        c_rstd = sb("c_rstd", [HB, 2])
        cz = sb("cz", [HB, 2, RANK])
        latent = [sb(f"latent{i}", [KB, 2, RANK]) for i in range(2)]
        cT = [sb(f"cT{i}", [KB, SEQ]) for i in range(2)]
        turn_cos = [sb(f"turn_cos{i}", [128, 2, SEQ]) for i in range(2)]
        turn_sin = [sb(f"turn_sin{i}", [128, 2, SEQ]) for i in range(2)]
        qT = [sb(f"qT{i}", [128, SEQ]) for i in range(3)]
        kT = [sb(f"kT{i}", [128, 2, SEQ]) for i in range(3)]
        top = [sb(f"top{i}", [HB, 4]) for i in range(3)]
        minus_top = [sb(f"minus_top{i}", [HB, 4]) for i in range(3)]
        total = [sb(f"total{i}", [HB, 4]) for i in range(3)]
        share = [sb(f"share{i}", [HB, 4]) for i in range(3)]
        prob = [sb(f"prob{i}", [HB, 2 * HB + 2 * SEQ]) for i in range(3)]
        pT = [sb(f"pT{i}", [KB, 2 * SEQ + 2 * HB]) for i in range(2)]
        oT = [sb(f"oT{i}", [128, SEQ]) for i in range(2)]
        ident = const["ident"]

        h_in = sem("h_in")
        y_in = sem("y_in")
        consts = sem("consts")
        cleared = sem("cleared")
        h2_done = sem("h2_done")
        stats_done = sem("stats_done")
        mv_done = sem("mv_done")
        ve_done = sem("ve_done")
        rstd_done = sem("rstd_done")
        z_done = sem("z_done")
        zT_ps = sem("zT_ps")
        zT_done = sem("zT_done")
        c_ps = sem("c_ps")
        c_done = sem("c_done")
        c_stats_done = sem("c_stats_done")
        c_mv_done = sem("c_mv_done")
        c_ve_done = sem("c_ve_done")
        c_rstd_done = sem("c_rstd_done")
        cz_done = sem("cz_done")
        latent_done = sem("latent_done")
        cT_ps = sem("cT_ps")
        cT_done = sem("cT_done")
        qk_ps = sem("qk_ps")
        turned = sem("turned")
        q_done = sem("q_done")
        k_done = sem("k_done")
        s_ps = sem("s_ps")
        top_done = sem("top_done")
        minus_done = sem("minus_done")
        exp_done = sem("exp_done")
        share_done = sem("share_done")
        prob_done = sem("prob_done")
        pT_ps = sem("pT_ps")
        pT_done = sem("pT_done")
        o_ps = sem("o_ps")
        oT_done = sem("oT_done")
        out_ps = sem("out_ps")
        res_done = sem("res_done")
        h3_done = sem("h3_done")
        stored = sem("stored")
        step = sem("step")
        block = ctx.enter_context(nc.Block())

        def done(i):
            return START + 1 + i

        def run(engine, sequence):
            for q in range(2):
                sequence(q, q, q == 0, False)
            with engine.Fori(1, B // 2 - 1) as i:
                for q in range(2):
                    sequence(2 * i + q, q, False, False)
            for q in range(2):
                sequence(B - 2 + q, q, False, q == 1)

        @block.sync
        def _(sp):
            def load(b):
                sp.wait_ge(h2_done, START + b)
                sp.dma_start(h1[:, :, :], rows_of(dram["h1"], b)).then_inc(h_in, 16)
                sp.dma_start(y0[:, :, :], rows_of(dram["y0"], b)).then_inc(y_in, 16)

            def store(b):
                sp.wait_ge(h3_done, done(b))
                sp.dma_start(dram["h3"][bass.ds(b * T, HB), :], h3[:, 0, :]).then_inc(stored, 16)
                sp.dma_start(dram["h3"][bass.ds(b * T + HB, T - HB), :], h3[0:T - HB, 1, :]).then_inc(stored, 16)

            for b in range(3):
                load(b)
            with sp.Fori(1, B - 2) as b:
                load(b + 2)
                store(b - 1)
            for b in range(B - 3, B):
                store(b)
            sp.wait_ge(stored, START + 32 * B)

        @block.gpsimd
        def _(pool):
            pool.memset(minus_half[:, :], -0.5).then_inc(consts, 1)
            for tile in [*kT, *latent]:
                pool.memset(tile[:, :, :], 0.0).then_inc(cleared, 1)
            for tile in pT:
                pool.memset(tile[:, :], 0.0).then_inc(cleared, 1)
            pool.wait_ge(consts, START + 3)
            pool.wait_ge(cleared, START + 7)

            def scale_z(b):
                pool.wait_ge(ve_done, done(b))
                pool.tensor_tensor(rstd[:, :], ve[:, :], minus_half[:, :], ALU.pow).then_inc(rstd_done, 1)

            def scale_c(b):
                pool.wait_ge(c_ve_done, done(b))
                pool.tensor_tensor(c_rstd[:, :], c_ve[:, :], minus_half[:, :], ALU.pow).then_inc(c_rstd_done, 1)

            def rotate_keys(s, n):
                pool.wait_ge(s_ps, done(s - 3))
                pool.wait_ge(turned, done(s))
                for quarter in range(4):
                    if quarter:
                        pool.wait_ge(k_done, START + 4 * s + quarter)
                    rows = slice(32 * quarter, 32 * quarter + 32)
                    pool.tensor_tensor(kT[n % 3][rows, quarter % 2, :], turn_cos[n % 2][rows, 1, :],
                                       turn_sin[n % 2][rows, 1, :], ALU.add).then_inc(k_done, 1)
                pool.wait_ge(k_done, START + 4 * s + 4)

            def normalise(s, n):
                pool.wait_ge(exp_done, START + 4 * s + 4)
                pool.wait_ge(share_done, done(s))
                for tile, cols in ((0, AK), (1, BK)):
                    view = prob[n % 3][:, cols].rearrange("p (o n) -> p o n", o=2)
                    pool.tensor_tensor(view, view, share[n % 3][:, 2 * tile:2 * tile + 2].unsqueeze(2)
                                       .broadcast_to([HB, 2, HB * (tile + 1)]), ALU.mult).then_inc(prob_done, 1)

            def sequence(b, q, first, last):
                for p in range(PAIRS):
                    s, n = PAIRS * b + p, PAIRS * q + p
                    if p >= SHARE or not first:
                        normalise(s - SHARE, n - SHARE)
                    if p >= SHARE or not first:
                        pool.wait_ge(prob_done, START + 2 * (s - SHARE) + 2)
                    if p == 1 and not last:
                        scale_z(b + 1)
                        pool.wait_ge(rstd_done, done(b + 1))
                    rotate_keys(s, n)
                    if p == 3 and not last:
                        scale_c(b + 1)

            scale_z(0)
            scale_c(0)
            run(pool, sequence)
            for p in range(SHARE):
                normalise(PAIRS * B + p - SHARE, p - SHARE)

        @block.scalar
        def _(act):
            def copy_zT(b, q):
                act.wait_ge(qk_ps, START + PAIRS * (b - 1))
                act.wait_ge(zT_ps, done(b))
                act.activation(zT[q][:, :, :], Z_PS[0:DC, :].rearrange("p (c n) -> p c n", c=2), ACT.Copy
                               ).then_inc(zT_done, 1)

            def copy_c(b):
                act.wait_ge(cz_done, START + 2 * b)
                act.wait_ge(c_ps, done(b))
                act.activation(c[:, :, :], Z_PS[0:HB, 0:2 * RANK].rearrange("p (t n) -> p t n", t=2), ACT.Copy
                               ).then_inc(c_done, 1)

            def copy_cT(b, q):
                act.wait_ge(qk_ps, START + PAIRS * (b - 1))
                act.wait_ge(cT_ps, done(b))
                act.activation(cT[q][0:RANK, :], Z_PS[0:RANK, 0:SEQ], ACT.Copy).then_inc(cT_done, 1)

            def keep_latent(b, q):
                act.wait_ge(o_ps, START + PAIRS * (b - 1))
                act.wait_ge(cz_done, START + 2 * b + 2)
                act.activation(latent[q][0:HB, :, :], cz[:, :, :], ACT.Copy).then_inc(latent_done, 1)

            def exps(s, n):
                act.wait_ge(pT_ps, done(s - 3))
                act.wait_ge(minus_done, done(s))
                for tile in range(2):
                    for o in range(2):
                        at, width = 2 * tile + o, HB * (tile + 1)
                        cols = slice(2 * HB * tile + o * width, 2 * HB * tile + (o + 1) * width)
                        act.activation(prob[n % 3][:, cols], S_PS[n % 2][0:HB, cols], ACT.Exp,
                                       bias=minus_top[n % 3][:, at:at + 1], scale=HD ** -0.5,
                                       accum_out=total[n % 3][:, at:at + 1]).then_inc(exp_done, 1)

            def copy_pT(s, n):
                act.wait_ge(o_ps, done(s - 2))
                act.wait_ge(pT_ps, done(s))
                act.activation(pT[n % 2][0:HB, :], PT_PS[n % 2][0:HB, 0:2 * SEQ + 2 * HB], ACT.Copy
                               ).then_inc(pT_done, 1)

            def copy_oT(s, n):
                act.wait_ge(out_ps, done(s - 2))
                act.wait_ge(o_ps, done(s))
                act.activation(oT[n % 2][:, :], O_PS, ACT.Copy).then_inc(oT_done, 1)

            def sequence(b, q, first, last):
                for p in range(PAIRS):
                    s, n = PAIRS * b + p, PAIRS * q + p
                    if p >= TURN or not first:
                        copy_pT(s - TURN, n - TURN)
                    if p >= VALUE or not first:
                        copy_oT(s - VALUE, n - VALUE)
                    if p == 2 and not last:
                        copy_zT(b + 1, q ^ 1)
                    if p == 3 and not last:
                        copy_c(b + 1)
                    if p == 5 and not last:
                        copy_cT(b + 1, q ^ 1)
                    if p == 1:
                        keep_latent(b, q)
                    if p >= SCORE or not first:
                        exps(s - SCORE, n - SCORE)

            copy_zT(0, 0)
            copy_c(0)
            copy_cT(0, 0)
            run(act, sequence)
            for p in range(VALUE):
                s, n = PAIRS * B + p, p
                if p < TURN:
                    copy_pT(s - TURN, n - TURN)
                copy_oT(s - VALUE, n - VALUE)
                if p < SCORE:
                    exps(s - SCORE, n - SCORE)

        @block.tensor
        def _(pe):
            pe.wait_ge(consts, START + 3)
            pe.wait_ge(cleared, START + 7)

            def transpose_z(b, values_out):
                pe.wait_ge(oT_done, values_out)
                pe.wait_ge(z_done, START + 2 * b + 2)
                for half in range(2):
                    for t in range(2):
                        mm = pe.transpose(Z_PS[0:DC, half * SEQ + t * HB:half * SEQ + (t + 1) * HB],
                                          z[:, t, half * DC:(half + 1) * DC], ident[0:HB, 0:HB])
                mm.then_inc(zT_ps, 1)

            def make_latent(b, q, values_out):
                pe.wait_ge(oT_done, values_out)
                pe.wait_ge(zT_done, done(b))
                for t in range(2):
                    for c in range(2):
                        mm = pe.matmul(Z_PS[0:HB, t * RANK:(t + 1) * RANK], zT[q][:, c, t * HB:(t + 1) * HB],
                                       wdown[:, c, :], start=(c == 0), stop=(c == 1))
                mm.then_inc(c_ps, 1)

            def transpose_c(b, values_out):
                pe.wait_ge(oT_done, values_out)
                pe.wait_ge(cz_done, START + 2 * b + 2)
                pe.sem_inc(step, 1)
                for t in range(2):
                    mm = pe.transpose(Z_PS[0:RANK, t * HB:(t + 1) * HB], cz[:, t, :], ident[0:HB, 0:HB])
                mm.then_inc(cT_ps, 1)

            def project(b, q, s, n, p):
                pe.wait_ge(turned, done(s - 2))
                pe.wait_ge(zT_done, done(b))
                for c in range(2):
                    pe.matmul(QK_PS[n % 2][:, 0:SEQ], wq[:, c, 128 * p:128 * (p + 1)], zT[q][:, c, :],
                              start=(c == 0), stop=(c == 1))
                pe.wait_ge(cT_done, done(b))
                pe.matmul(QK_PS[n % 2][:, SEQ:2 * SEQ], wk[:, 128 * p:128 * (p + 1)], cT[q][:, :],
                          start=True, stop=True).then_inc(qk_ps, 1)

            def scores(s, n):
                bank, keys = S_PS[n % 2][0:HB, :], kT[n % 3]
                pe.wait_ge(exp_done, START + 4 * (s - 1))
                pe.matmul(bank[:, 0:2 * HB + 2 * SEQ], ident_b[:, :], mask[:, :], start=True, stop=False)
                pe.wait_ge(q_done, done(s))
                pe.wait_ge(k_done, START + 4 * s + 4)
                pe.matmul(bank[:, AK].rearrange("p (o n) -> p o n", o=2), qT[n % 3][:, A], keys[:, :, A],
                          start=False, stop=False)
                pe.matmul(bank[:, BK].rearrange("p (o n) -> p o n", o=2), qT[n % 3][:, BT], keys[:, :, :],
                          start=False, stop=True).then_inc(s_ps, 1)

            def transpose_p(s, n):
                pe.wait_ge(pT_done, done(s - 2))
                pe.wait_ge(prob_done, START + 2 * s + 2)
                for o in range(2):
                    second = 2 * HB + o * SEQ
                    for src, to in ((o * HB, o * SEQ), (second, o * SEQ + HB), (second + HB, 2 * SEQ + o * HB)):
                        mm = pe.transpose(PT_PS[n % 2][0:HB, to:to + HB], prob[n % 3][:, src:src + HB],
                                          ident[0:HB, 0:HB])
                mm.then_inc(pT_ps, 1)

            def values(b, q, s, n):
                pe.wait_ge(oT_done, START + s)
                pe.wait_ge(latent_done, done(b))
                pe.wait_ge(pT_done, done(s))
                for o in range(2):
                    out = O_PS[o * RANK:(o + 1) * RANK, :]
                    pe.matmul(out, latent[q][:, 0, :], pT[n % 2][:, o * SEQ:(o + 1) * SEQ], start=True, stop=False)
                    mm = pe.matmul(out[:, BT], latent[q][:, 1, :],
                                   pT[n % 2][:, 2 * SEQ + o * HB:2 * SEQ + (o + 1) * HB], start=False, stop=True)
                mm.then_inc(o_ps, 1)

            def output(b, s, n, p):
                if p == 0:
                    pe.wait_ge(h3_done, START + b)
                pe.wait_ge(oT_done, done(s))
                for t in range(2):
                    mm = pe.matmul(OUT_PS[:, t * D:(t + 1) * D], oT[n % 2][:, t * HB:(t + 1) * HB], wvo[:, p, :],
                                   start=(p == 0 and t == 0), stop=(p == PAIRS - 1 and t == 1))
                mm.then_inc(out_ps, 1)

            def sequence(b, q, first, last):
                for p in range(PAIRS):
                    s, n = PAIRS * b + p, PAIRS * q + p
                    project(b, q, s, n, p)
                    if p >= SCORE or not first:
                        scores(s - SCORE, n - SCORE)
                    if not first:
                        output(b - 1, s - OUT, n - OUT, p)
                    if p >= TURN or not first:
                        transpose_p(s - TURN, n - TURN)
                    if p in (2, 3, 5) and not last:
                        values_out = START + max(s - VALUE, 0) if first else START + s - VALUE
                        if p == 2:
                            transpose_z(b + 1, values_out)
                        if p == 3:
                            make_latent(b + 1, q ^ 1, values_out)
                        if p == 5:
                            transpose_c(b + 1, values_out)
                    if p == 4 and not last:
                        pe.wait_ge(c_done, done(b + 1))
                    if p == 0:
                        pe.wait_ge(cT_done, done(b))
                    if p >= VALUE:
                        values(b, q, s - VALUE, n - VALUE)
                    elif not first:
                        values(b - 1, q ^ 1, s - VALUE, n - VALUE)

            transpose_z(0, START)
            make_latent(0, 0, START)
            transpose_c(0, START)
            run(pe, sequence)
            for p in range(OUT):
                s, n = PAIRS * B + p, p
                output(B - 1, s - OUT, n - OUT, p)
                if p < SCORE:
                    scores(s - SCORE, n - SCORE)
                if p < TURN:
                    transpose_p(s - TURN, n - TURN)
                if p < VALUE:
                    values(B - 1, 1, s - VALUE, n - VALUE)

        @block.vector
        def _(dve):
            for i in range(2):
                dve.memset(cT[i][RANK:KB, :], 0.0).then_inc(step, 1)
            dve.wait_ge(step, START + 2)
            for i in range(2):
                dve.memset(cT[i][RANK:RANK + 1, :], 1.0).then_inc(consts, 1)

            def measure(b, q):
                dve.wait_ge(h_in, START + 16 * (b + 1))
                dve.wait_ge(y_in, START + 16 * (b + 1))
                dve.wait_ge(res_done, START + b - 1)
                dve.tensor_tensor(h2[q][:, :, :], h1[:, :, :], y0[:, :, :], ALU.add).then_inc(h2_done, 1)
                dve.wait_ge(h2_done, done(b))
                for t in range(2):
                    dve.bn_stats(stats[:, t, :], h2[q][:, t, :]).then_inc(stats_done, 1)
                dve.wait_ge(stats_done, START + 2 * b + 2)
                dve.sem_inc(step, 1)
                for t in range(2):
                    dve.bn_aggr(mv[:, t, :], stats[:, t, :]).then_inc(mv_done, 1)
                dve.wait_ge(mv_done, START + 2 * b + 2)
                dve.tensor_scalar(ve[:, :], mv[:, :, 1], EPS, None, ALU.add).then_inc(ve_done, 1)

            def normalise(b, q):
                dve.wait_ge(zT_ps, START + b)
                dve.wait_ge(rstd_done, done(b))
                for t in range(2):
                    dve.tensor_scalar(z[:, t, :], h2[q][:, t, :], mv[:, t, 0:1], rstd[:, t:t + 1],
                                      ALU.subtract, ALU.mult).then_inc(z_done, 1)

            def measure_latent(b):
                dve.wait_ge(c_done, done(b))
                for t in range(2):
                    dve.bn_stats(c_stats[:, t, :], c[:, t, :]).then_inc(c_stats_done, 1)
                dve.wait_ge(c_stats_done, START + 2 * b + 2)
                dve.sem_inc(step, 1)
                for t in range(2):
                    dve.bn_aggr(c_mv[:, t, :], c_stats[:, t, :]).then_inc(c_mv_done, 1)
                dve.wait_ge(c_mv_done, START + 2 * b + 2)
                dve.tensor_scalar(c_ve[:, :], c_mv[:, :, 1], EPS, None, ALU.add).then_inc(c_ve_done, 1)

            def normalise_latent(b):
                dve.wait_ge(cT_ps, START + b)
                dve.wait_ge(latent_done, START + b)
                dve.wait_ge(c_rstd_done, done(b))
                for t in range(2):
                    dve.tensor_scalar(cz[:, t, :], c[:, t, :], c_mv[:, t, 0:1],
                                      c_rstd[:, t:t + 1], ALU.subtract, ALU.mult).then_inc(cz_done, 1)

            def residual(b, q):
                dve.wait_ge(h3_done, START + b - 1)
                dve.tensor_tensor(res[q][:, :, :], h2[q][:, :, :], bias[:, :].unsqueeze(1).broadcast_to([HB, 2, D]),
                                  ALU.add).then_inc(res_done, 1)

            def turn(s, n):
                dve.wait_ge(q_done, done(s - 2))
                dve.wait_ge(k_done, START + 4 * (s - 1))
                dve.wait_ge(qk_ps, done(s))
                src = QK_PS[n % 2][:, 0:2 * SEQ].rearrange("p (r n) -> p r n", r=2)
                for half in range(2):
                    here, there = slice(64 * half, 64 * half + 64), slice(64 - 64 * half, 128 - 64 * half)
                    dve.tensor_tensor(turn_sin[n % 2][there, :, :], src[here],
                                      sin[here, :].unsqueeze(1).broadcast_to([64, 2, SEQ]), ALU.mult
                                      ).then_inc(step, 1)
                dve.tensor_tensor(turn_cos[n % 2][:, :, :], src, cos[:, :].unsqueeze(1).broadcast_to([128, 2, SEQ]),
                                  ALU.mult).then_inc(turned, 1)

            def rotate_queries(s, n):
                dve.wait_ge(s_ps, done(s - 3))
                dve.wait_ge(turned, done(s))
                dve.tensor_tensor(qT[n % 3][:, :], turn_cos[n % 2][:, 0, :], turn_sin[n % 2][:, 0, :], ALU.add
                                  ).then_inc(q_done, 1)

            def maxima(s, n):
                dve.wait_ge(s_ps, done(s))
                for tile, cols in ((0, AK), (1, BK)):
                    dve.tensor_reduce(top[n % 3][:, 2 * tile:2 * tile + 2],
                                      S_PS[n % 2][0:HB, cols].rearrange("p (o n) -> p o n", o=2), AX.X, ALU.max
                                      ).then_inc(top_done, 1)
                dve.wait_ge(top_done, START + 2 * s + 2)
                dve.tensor_scalar(minus_top[n % 3][:, :], top[n % 3][:, :], -HD ** -0.5, None, ALU.mult
                                  ).then_inc(minus_done, 1)

            def shares(s, n):
                dve.wait_ge(exp_done, START + 4 * s + 4)
                dve.reciprocal(share[n % 3][:, :], total[n % 3][:, :]).then_inc(share_done, 1)

            def add(b, q):
                dve.wait_ge(stored, START + 32 * b)
                dve.wait_ge(res_done, done(b))
                dve.wait_ge(out_ps, START + PAIRS * (b + 1))
                dve.tensor_tensor(h3[:, :, :], OUT_PS.rearrange("p (t n) -> p t n", t=2), res[q][:, :, :],
                                  ALU.add).then_inc(h3_done, 1)

            def sequence(b, q, first, last):
                for p in range(PAIRS):
                    s, n = PAIRS * b + p, PAIRS * q + p
                    if p == 4 and not last:
                        measure_latent(b + 1)
                    turn(s, n)
                    if p >= SHARE or not first:
                        shares(s - SHARE, n - SHARE)
                    if p >= SCORE or not first:
                        maxima(s - SCORE, n - SCORE)
                    rotate_queries(s, n)
                    if p == 0 and not last:
                        measure(b + 1, q ^ 1)
                    if p == 1 and not last:
                        normalise(b + 1, q ^ 1)
                    if p == 3:
                        residual(b, q)
                    if p == 4 and not last:
                        normalise_latent(b + 1)
                    if p == 5 and not first:
                        add(b - 1, q ^ 1)

            measure(0, 0)
            normalise(0, 0)
            measure_latent(0)
            normalise_latent(0)
            run(dve, sequence)
            for p in range(SHARE):
                s, n = PAIRS * B + p, p
                shares(s - SHARE, n - SHARE)
                if p < SCORE:
                    maxima(s - SCORE, n - SCORE)
            add(B - 1, 1)


def swiglu_weights(nc, used, ctx):
    sem = primed_semaphores(nc, used)
    return {"w1": [ctx.enter_context(nc.sbuf_tensor(f"e1_w1_{i}", [DC, 2, 2 * H1], F32)) for i in range(2)],
            "w2": [ctx.enter_context(nc.sbuf_tensor(f"e1_w2_{i}", [128, H1 // 128, D], F32)) for i in range(2)],
            "in": [sem(f"e1_w_in{i}") for i in range(2)]}


def load_swiglu(sp, w, weights, e, j):
    sp.dma_start(weights["w1"][j][:, :, :], w["e1_w1"][bass.ds(e * D, D), :].rearrange("(c p) n -> p c n", c=2)
                 ).then_inc(weights["in"][j], 16)
    sp.dma_start(weights["w2"][j][:, :, :], w["e1_w2"][bass.ds(e * H1, H1), :].rearrange("(k p) n -> p k n", p=128)
                 ).then_inc(weights["in"][j], 16)


def experts_swiglu(nc, used, w, dram, const, weights):
    w1, w2, w_in = weights["w1"], weights["w2"], weights["in"]
    UNITS = 2 * E1
    BODY = 4
    HC = H1 // 128
    with ExitStack() as ctx:
        def sb(name, shape, dt=F32):
            return ctx.enter_context(nc.sbuf_tensor(f"e1_{name}", shape, dt))

        primed = primed_semaphores(nc, used)

        def sem(name):
            return primed(f"e1_{name}")

        bank = [ctx.enter_context(nc.psum_tensor(f"e1_bank{i}", [128, 512], F32)) for i in range(8)]
        T_PS, VALUE_PS, GATE_PS, Y_PS = bank[0:2], bank[2:4], bank[4:6], bank[6:8]

        def parts(name, shape):
            return [[sb(f"{name}_{part}{i}", shape, F32R) for part in ("high", "low")] for i in range(2)]

        w1_parts, w2_parts = parts("w1", [DC, 2, 2 * H1]), parts("w2", [128, HC, D])
        x = [sb(f"x{i}", [128, CAPT, RW]) for i in range(BODY)]
        xT = parts("xT", [DC, 2, CAPR])
        silu = [sb(f"silu{i}", [128, CAPR]) for i in range(2)]
        product = [sb(f"product{i}", [128, CAPR]) for i in range(2)]
        gated = parts("gated", [128, HC, CAPR])
        y = [sb(f"y{i}", [128, CAPT, D]) for i in range(2)]
        ident = const["ident"]

        x_in = [sem(f"x_in{i}") for i in range(BODY)]
        xT_ps = sem("xT_ps")
        w_high = sem("w_high")
        w_low = sem("w_low")
        xT_high = sem("xT_high")
        xT_low = sem("xT_low")
        up_ps = sem("up_ps")
        silu_done = sem("silu_done")
        product_done = sem("product_done")
        gated_high = sem("gated_high")
        gated_low = sem("gated_low")
        y_ps = sem("y_ps")
        y_done = sem("y_done")
        x_free = sem("x_free")
        step = sem("step")
        scattered = [unprimed_semaphore(nc, used, f"e1_scattered{i}") for i in range(2)]
        block = ctx.enter_context(nc.Block())

        def pieces(j):
            for c in range(2):
                yield w1[j][:, c, :], [part[:, c, :] for part in w1_parts[j]]
            yield w2[j][:, :, :], [part[:, :, :] for part in w2_parts[j]]

        def run(engine, unit):
            for n in range(BODY):
                unit(0, n, n == 0, False)
            with engine.Fori(1, UNITS // BODY - 1) as i:
                for n in range(BODY):
                    unit(i, n, False, False)
            for n in range(BODY):
                unit(UNITS // BODY - 1, n, False, n == BODY - 1)

        @block.sync
        def _(sp):
            def load_x(u, n):
                sp.wait_ge(x_free, START + u - BODY + 1)
                sp.dma_start(x[n][:, :, :], dram["slots1"][bass.ds(u * CAPR, CAPR), :]
                             .rearrange("(t p) c -> p t c", p=128)).then_inc(x_in[n], 16)

            def load_weights(e, j):
                sp.wait_ge(w_low, START + 3 * (e - 1))
                load_swiglu(sp, w, weights, e, j)

            for n in range(BODY):
                load_x(n, n)
            with sp.Fori(1, UNITS // BODY) as i:
                for j in range(2):
                    load_weights(2 * i + j, j)
                    for n in (2 * j, 2 * j + 1):
                        load_x(BODY * i + n, n)

        @block.gpsimd
        def _(pool):
            with pool.Fori(0, UNITS // BODY) as i:
                for n in range(BODY):
                    u, k = BODY * i + n, n % 2
                    for t in range(CAPT):
                        pool.wait_ge(y_done, START + CAPT * u + t + 1)
                        pool.sem_inc(step, 1)
                        pool.indirect_dma_start(
                            dram["y1"], bass.IndirectOffsetOnAxis(ap=x[n][:, t, D + 2 + k:D + 3 + k].bitcast(I32), axis=0),
                            y[n % 2][:, t, :], None, bounds_check=2 * NP - 1, oob_is_err=False
                        ).then_inc(scattered[n % 2], 16)
                    if n:
                        pool.wait_ge(scattered[(n - 1) % 2], 16 * CAPT * (2 * i + (n - 1) // 2 + 1))
                        pool.sem_inc(x_free, 1)
                pool.wait_ge(scattered[1], 16 * CAPT * (2 * i + 2))
                pool.sem_inc(x_free, 1)

        @block.scalar
        def _(act):
            def high_xT(u, n):
                act.wait_ge(up_ps, START + HC * (u - 1))
                for c in range(2):
                    act.wait_ge(xT_ps, START + 2 * u + c + 1)
                    act.activation(xT[n % 2][0][:, c, :], T_PS[c][0:DC, 0:CAPR], ACT.Copy).then_inc(xT_high, 1)

            def high_weights(e, j, loaded, piece):
                act.wait_ge(y_ps, START + CAPT * 2 * (e - 1))
                act.wait_ge(w_in[j], loaded)
                whole, (high, low) = list(pieces(j))[piece]
                act.activation(high, whole, ACT.Copy).then_inc(w_high, 1)

            def high_gated(u, n, k):
                act.wait_ge(y_ps, START + CAPT * (u - 1))
                act.wait_ge(product_done, START + HC * u + k + 1)
                act.activation(gated[n % 2][0][:, k, :], product[k % 2][:, :], ACT.Copy).then_inc(gated_high, 1)

            def unit(i, n, first, last):
                u = BODY * i + n
                for k in range(HC):
                    act.wait_ge(product_done, START + HC * u + k - 1)
                    act.wait_ge(up_ps, START + HC * u + k + 1)
                    act.activation(silu[k % 2][:, :], GATE_PS[k % 2][:, 0:CAPR], ACT.Silu).then_inc(silu_done, 1)
                    if k:
                        high_gated(u, n, k - 1)
                    if n % 2 and k < 3 and not last:
                        high_weights(2 * i + (n + 1) // 2, (n + 1) // 2 % 2, START + 32 * (i + 1 + n // 3), k)
                    if k == HC - 2 and not last:
                        high_xT(u + 1, n + 1)
                high_gated(u, n, HC - 1)

            for piece in range(3):
                high_weights(0, 0, START + 32, piece)
            high_xT(0, 0)
            run(act, unit)

        @block.tensor
        def _(pe):
            def transposes(u, n, in_):
                pe.wait_ge(x_in[n % BODY], in_)
                for c in range(2):
                    pe.wait_ge(xT_low, START + 2 * u + c - 1)
                    for t in range(CAPT):
                        mm = pe.transpose(T_PS[c][0:DC, t * 128:(t + 1) * 128], x[n % BODY][:, t, c * DC:(c + 1) * DC],
                                          ident)
                    mm.then_inc(xT_ps, 1)

            def up(u, n, k):
                pe.wait_ge(product_done, START + HC * u + k - 1)
                pe.wait_ge(xT_low, START + 2 * u + 2)
                for part, ps in enumerate((GATE_PS, VALUE_PS)):
                    at = H1 * (1 - part) + 128 * k
                    for c in range(2):
                        for a, b in PARTS:
                            mm = pe.matmul(ps[k % 2][:, 0:CAPR], w1_parts[n // 2][a][:, c, at:at + 128],
                                           xT[n % 2][b][:, c, :], start=(c == 0 and (a, b) == PARTS[0]),
                                           stop=(c == 1 and (a, b) == PARTS[-1]))
                mm.then_inc(up_ps, 1)

            def down(u, n, t):
                pe.wait_ge(y_done, START + CAPT * u + t - 1)
                pe.wait_ge(gated_low, START + HC * (u + 1))
                bank_ = Y_PS[(CAPT * n + t) % 2]
                for k in range(HC):
                    for a, b in PARTS:
                        mm = pe.matmul(bank_[:, 0:D], gated[n % 2][a][:, k, t * 128:(t + 1) * 128],
                                       w2_parts[n // 2][b][:, k, :], start=(k == 0 and (a, b) == PARTS[0]),
                                       stop=(k == HC - 1 and (a, b) == PARTS[-1]))
                mm.then_inc(y_ps, 1)

            def unit(i, n, first, last):
                u = BODY * i + n
                if n % 2 == 0:
                    pe.wait_ge(w_low, START + 3 * (2 * i + n // 2 + 1))
                for k in range(HC):
                    up(u, n, k)
                    if k == HC - 2 and not last:
                        transposes(u + 1, n + 1, START + 16 * (i + (2 if n == BODY - 1 else 1)))
                    if k and not first:
                        down(u - 1, (n - 1) % BODY, k - 1)

            transposes(0, 0, START + 16)
            run(pe, unit)
            for t in range(CAPT):
                down(UNITS - 1, BODY - 1, t)

        @block.vector
        def _(dve):
            def scale_y(u, n, t):
                dve.wait_ge(x_free, START + u - 1)
                dve.wait_ge(y_ps, START + CAPT * u + t + 1)
                dve.tensor_scalar(y[n % 2][:, t, :], Y_PS[(CAPT * n + t) % 2][:, 0:D],
                                  x[n][:, t, D + n % 2:D + n % 2 + 1], None, ALU.mult).then_inc(y_done, 1)

            def low_xT(u, n):
                dve.wait_ge(up_ps, START + HC * (u - 1))
                for c in range(2):
                    high, low = xT[n % 2]
                    dve.wait_ge(xT_high, START + 2 * u + c + 1)
                    dve.tensor_tensor(low[:, c, :], T_PS[c][0:DC, 0:CAPR], high[:, c, :].bitcast(F32), ALU.subtract
                                      ).then_inc(xT_low, 1)

            def low_weights(e, j, piece):
                whole, (high, low) = list(pieces(j))[piece]
                dve.wait_ge(y_ps, START + CAPT * 2 * (e - 1))
                dve.wait_ge(w_high, START + 3 * e + piece + 1)
                dve.tensor_tensor(low, whole, high.bitcast(F32), ALU.subtract).then_inc(w_low, 1)

            def low_gated(u, n, k):
                high, low = gated[n % 2]
                dve.wait_ge(y_ps, START + CAPT * (u - 1))
                dve.wait_ge(gated_high, START + HC * u + k + 1)
                dve.tensor_tensor(low[:, k, :], product[k % 2][:, :], high[:, k, :].bitcast(F32), ALU.subtract
                                  ).then_inc(gated_low, 1)

            def unit(i, n, first, last):
                u = BODY * i + n
                for k in range(HC):
                    dve.wait_ge(gated_low, START + HC * u + k - 1)
                    dve.wait_ge(gated_high, START + HC * u + k - 1)
                    dve.wait_ge(silu_done, START + HC * u + k + 1)
                    dve.tensor_tensor(product[k % 2][:, :], VALUE_PS[k % 2][:, 0:CAPR], silu[k % 2][:, :], ALU.mult
                                      ).then_inc(product_done, 1)
                    if k:
                        low_gated(u, n, k - 1)
                    if k and not first:
                        scale_y(u - 1, (n - 1) % BODY, k - 1)
                    if n % 2 and k < 3 and not last:
                        low_weights(2 * i + (n + 1) // 2, (n + 1) // 2 % 2, k)
                    if k == HC - 2 and not last:
                        low_xT(u + 1, n + 1)
                low_gated(u, n, HC - 1)

            for piece in range(3):
                low_weights(0, 0, piece)
            low_xT(0, 0)
            run(dve, unit)
            for t in range(CAPT):
                scale_y(UNITS - 1, BODY - 1, t)


def combine(nc, used, w, dram, const, out):
    CH = 4
    WIDTH = N * D // 128 // CH
    with ExitStack() as ctx:
        def flat(src):
            return src.rearrange("r c -> (r c)").rearrange("(p q n) -> q p n", p=128, q=CH)

        primed = primed_semaphores(nc, used)
        part = [[ctx.enter_context(nc.sbuf_tensor(f"s_{n}{i}", [128, WIDTH], F32)) for i in range(CH)]
                for n in ("h3", "first", "second")]
        loaded = [primed(f"s_loaded{i}") for i in range(CH)]
        summed = primed("s_summed")
        final = primed("s_final")
        stored = primed("s_stored")
        block = ctx.enter_context(nc.Block())

        @block.sync
        def _(sp):
            for i in range(CH):
                for tiles, src in zip(part, (dram["h3"][0:N, :], dram["y1"][0:N, :], dram["y1"][NP:NP + N, :])):
                    sp.dma_start(tiles[i][:, :], flat(src)[i]).then_inc(loaded[i], 16)
            for i in range(CH):
                sp.wait_ge(final, START + i + 1)
                sp.dma_start(flat(out.rearrange("b t c -> (b t) c"))[i], part[0][i][:, :]).then_inc(stored, 16)
            sp.wait_ge(stored, START + 16 * CH)

        @block.vector
        def _(dve):
            for i in range(CH):
                dve.wait_ge(loaded[i], START + 48)
                dve.tensor_tensor(part[1][i][:, :], part[1][i][:, :], part[2][i][:, :], ALU.add).then_inc(summed, 1)
                dve.wait_ge(summed, START + i + 1)
                dve.tensor_tensor(part[0][i][:, :], part[0][i][:, :], part[1][i][:, :], ALU.add).then_inc(final, 1)


def build(nc, w, out):
    with ExitStack() as ctx:
        def scratch(name, rows, width=D):
            return nc.dram_tensor(name, [rows, width], F32).ap()

        dram = {"h0": scratch("h0", N + 1), "h1": scratch("h1", NP), "h3": scratch("h3", NP),
                "slots0": scratch("slots0", ROWS0, RW), "slots1": scratch("slots1", ROWS1, RW),
                "y0": scratch("y0", NP), "y1": scratch("y1", 2 * NP)}
        const = {}
        for name, shape, dt in (("ident", [128, 128], F32), ("ones", [128, 128], BF16), ("before", [128, 128], BF16),
                                ("expert_no", [128, 8], F32), ("tile_rows", [1, TILES], F32),
                                ("tile_no", [1, TILES0], F32)):
            const[name] = ctx.enter_context(nc.sbuf_tensor(name, shape, dt))[:, :]
        made = {name: ctx.enter_context(nc.sbuf_tensor(name, [1, TILES0], I32))[:, :]
                for name in ("tile_row", "tile_expert")}
        used = []
        causal = causal_weights(ctx, nc)
        embed_patches(nc, used, w, dram, const, causal)
        const.update(made)
        attend_squared(nc, used, w, dram, const)
        with ExitStack() as layer:
            weights = gelu_weights(nc, used, layer)
            dispatch(nc, used, w, dram, const, 0, lambda sp: load_gelu(sp, w, weights))
            experts_gelu(nc, used, w, dram, const, weights)
        clear_semaphores(nc, used)
        attend_causal(nc, used, w, dram, const, causal)
        weights = swiglu_weights(nc, used, ctx)
        dispatch(nc, used, w, dram, const, 1, lambda sp: [load_swiglu(sp, w, weights, e, e) for e in range(2)])
        experts_swiglu(nc, used, w, dram, const, weights)
        combine(nc, used, w, dram, const, out)


def _layouts(a):
    BF = mybir.dt.np(BF16)

    def f(name):
        return np.asarray(a[name])

    x = f("x")[:, :, :GRID * PATCH, :GRID * PATCH].reshape(B, 3, GRID, PATCH, GRID, PATCH)
    rows = np.zeros((B, 3 * KP, IMG), np.float32)
    rows[:, :300, 1:] = x.transpose(0, 1, 3, 5, 2, 4).reshape(B, 300, IMG - 1)
    rows[:, 300, 1:] = 1
    rows[:, 301, 0] = 1
    tok_w = np.zeros((3 * KP, D), np.float32)
    tok_w[:300] = f("L0_tok_W").T
    tok_w[300] = f("L0_tok_b")
    tok_w[301] = f("L0_tok_cls").reshape(-1)

    def halves_first(m):
        return m.reshape(-1, HEADS // 2, 2, 2, HD // 2).swapaxes(2, 3).reshape(m.shape)

    inv = np.float32(1) / np.float32(10000) ** (np.arange(0, HD, 2, dtype=np.float32) / np.float32(HD))
    angle = np.tile(inv[:, None] * np.arange(SEQ, dtype=np.float32)[None], (4, 1)).astype(np.float32)
    sign = np.repeat(np.array([1, -1], np.float32), HD)[:, None]
    rows80 = np.arange(HB)[:, None]
    mask = np.concatenate([np.where(np.arange(HB)[None] <= rows80, 0, -1e30)] * 2
                          + [np.where(np.arange(SEQ)[None] <= rows80 + HB, 0, -1e30)] * 2, 1)
    out = {
        "patches": rows.reshape(B, 3, KP, IMG).transpose(0, 2, 1, 3).reshape(B, KP, 3 * IMG),
        "tok_w": tok_w.reshape(3, KP, D).transpose(1, 0, 2).reshape(KP, 3 * D),
        "tok_gamma": np.broadcast_to(f("L0_tok_gamma"), (IMG, D)),
        "tok_beta": np.broadcast_to(f("L0_tok_beta"), (IMG, D)),
        "txt": f("txt"),
        "ident": np.eye(128, dtype=np.float32),
        "attn0_w": np.concatenate([f(f"L0_attn_W{n}_w").T for n in "uqkv"], 1),
        "attn0_b": np.concatenate([f(f"L0_attn_W{n}_b") for n in "uqkv"])[None],
        "attn0_ln": np.stack([f("L0_attn_ln_gamma"), f("L0_attn_ln_beta")], 1),
        "attn0_wo": f("L0_attn_Wo_w").T,
        "attn0_bo": f("L0_attn_Wo_b")[None],
        "ones": np.ones((128, 128), BF),
        "before": np.triu(np.ones((128, 128), BF), 1),
        "expert_no": np.broadcast_to(np.arange(8, dtype=np.float32), (128, 8)),
        "tile_rows": np.arange(TILES, dtype=np.float32)[None] * 128,
        "tile_no": np.arange(TILES0, dtype=np.float32)[None],
        "gate0_w": f("L0_ffn_gate_w"),
        "gate0_b": f("L0_ffn_gate_b")[None],
        "gate0_centre": f("L0_ffn_gate_center")[None],
        "e0_w1": f("L0_ffn_w1").transpose(1, 0, 2).reshape(D, E0 * H0),
        "e0_b1": f("L0_ffn_b1").reshape(1, E0 * H0),
        "e0_w2": f("L0_ffn_w2"),
        "e0_b2": f("L0_ffn_b2"),
        "wq": halves_first(f("L1_attn_Wq")),
        "wdown": f("L1_attn_Wdown"),
        "up_k": halves_first(f("L1_attn_Wup")[:, :HEADS * HD]),
        "up_vT": f("L1_attn_Wup")[:, HEADS * HD:].T,
        "attn1_ln": np.tile(np.stack([f("L1_attn_ln_g"), f("L1_attn_ln_b")], 1), (2, 1)),
        "wo1": f("L1_attn_Wo"),
        "bo": np.broadcast_to(f("L1_attn_bo"), (HB, D)),
        "cos": np.cos(angle),
        "sin": np.sin(angle) * sign,
        "mask": mask.astype(BF),
        "ident_b": np.eye(HB, dtype=BF),
        "gate1_w": f("L1_ffn_Wg"),
        "e1_w1": f("L1_ffn_W1").reshape(E1 * D, 2 * H1),
        "e1_w2": f("L1_ffn_W2").reshape(E1 * H1, D),
    }
    return {k: np.ascontiguousarray(v) for k, v in out.items()}


def kernel(**inputs):
    import concourse.bacc as _bacc
    from concourse.bass_utils import run_bass_kernel_spmd as _run

    nc = _bacc.Bacc("TRN2", target_bir_lowering=False, num_devices=1)
    arrays = {f"in_{k}": v for k, v in _layouts(inputs).items()}
    w = {k[3:]: nc.dram_tensor(k, v.shape, mybir.dt.from_np(v.dtype), kind="ExternalInput").ap()
         for k, v in arrays.items()}
    out = nc.dram_tensor("out_0", (B, T, D), F32, kind="ExternalOutput").ap()
    build(nc, w, out)
    r = _run(nc, [arrays], core_ids=[0])
    return r.results[0]["out_0"]
```

```python
from contextlib import ExitStack

import numpy as np

import concourse.bass as bass
from concourse import mybir

F32 = mybir.dt.float32
F32R = mybir.dt.float32r
BF16 = mybir.dt.bfloat16
I32 = mybir.dt.int32
U32 = mybir.dt.uint32
ALU = mybir.AluOpType
ACT = mybir.ActivationFunctionType
AX = mybir.AxisListType

B = 16
PATCH = 10
GRID = 96 // PATCH
IMG = GRID * GRID + 1
TXT = 77
T = IMG + TXT
D = 192
N = B * T
EPS = 1e-5
HB = T // 2 + 1
SEQ = 2 * HB
TILES = -(-N // 128)
NP = TILES * 128
KP = 112
DC = D // 2

E0, H0 = 4, 768
TILES0 = (NP + E0 * 127) // 128
TILES0 += TILES0 % 2
FILL = 13
ROWS0 = -(-(E0 * NP + TILES0 * 128) // (FILL * 128)) * FILL * 128
E1, H1 = 8, 512
CAP = int(1.2 * N / E1)
CAPT = -(-CAP // 128)
CAPR = CAPT * 128
ROWS1 = E1 * 2 * CAPR
RW = D + 4
NOWHERE = 1 << 20

HEADS, HD, RANK = 12, 64, 64


PARTS = ((0, 0), (0, 1), (1, 0))


START = 8


def primed_semaphores(nc, used):
    engines = [nc.sync, nc.scalar, nc.vector, nc.gpsimd, nc.tensor]

    def sem(name):
        s = nc.alloc_semaphore(name)
        engines[len(used) % len(engines)].sem_inc(s, START)
        used.append(s)
        return s

    return sem


def unprimed_semaphore(nc, used, name):
    s = nc.alloc_semaphore(name)
    used.append(s)
    return s


def clear_semaphores(nc, used):
    nc.clear_and_free_semaphores(used)
    used.clear()
    nc.all_engine_barrier()


def rows_of(dram, b):
    return dram[bass.ds(b * T, SEQ), :].rearrange("(t p) c -> p t c", p=HB)


def causal_weights(ctx, nc):
    def sb(name, shape, dt=F32):
        return ctx.enter_context(nc.sbuf_tensor(f"c_{name}", shape, dt))

    return {"wq": sb("wq", [DC, 2, HEADS * HD]),
            "wdown": sb("wdown", [DC, 2, RANK]),
            "wk": sb("wk", [DC, HEADS * HD]),
            "wvo": sb("wvo", [128, HEADS // 2, D]),
            "bias": sb("bias", [HB, D]),
            "cos": sb("cos", [128, SEQ]),
            "sin": sb("sin", [128, SEQ]),
            "mask": sb("mask", [HB, 2 * HB + 2 * SEQ], BF16),
            "ident_b": sb("ident_b", [HB, HB], BF16)}


def embed_patches(nc, used, w, dram, const, causal):
    R = 4
    ROUNDS = B // R
    PAIRS = HEADS // 2
    with ExitStack() as ctx:
        def sb(name, shape, dt=F32):
            return ctx.enter_context(nc.sbuf_tensor(name, shape, dt))

        sem = primed_semaphores(nc, used)

        bank = [ctx.enter_context(nc.psum_tensor(f"tok_bank{i}", [128, 512], F32)) for i in range(2 * R)]
        zeros = sb("pad_zeros", [NP - N, D])
        tok_w = sb("tok_w", [KP, 3, D])
        gamma = sb("tok_gamma", [IMG, D])
        beta = sb("tok_beta", [IMG, D])
        minus_half = sb("tok_minus_half", [IMG, R])
        patches = [sb(f"patches{i}", [KP, 3 * IMG]) for i in range(2 * R)]
        stats = [sb(f"tok_stats{i}", [IMG, R, 6]) for i in range(2)]
        mv = [sb(f"tok_mv{i}", [IMG, R, 2]) for i in range(2)]
        ve = [sb(f"tok_ve{i}", [IMG, R]) for i in range(2)]
        rstd = [sb(f"tok_rstd{i}", [IMG, R]) for i in range(2)]
        centred = sb("tok_centred", [IMG, R, D])
        scaled = sb("tok_scaled", [IMG, R, D])
        y = sb("tok_y", [IMG, R, D])

        wq, wdown, wk, wvo = (causal[name] for name in ("wq", "wdown", "wk", "wvo"))
        up_k = sb("prep_up_k", [RANK, HEADS * HD])
        up_vT = sb("prep_up_vT", [128, PAIRS, RANK])
        latent_gb = sb("prep_latent_gb", [128, 2])
        latent_b = sb("prep_latent_b", [128, HB])
        wo = sb("prep_wo", [128, PAIRS, D])
        wvo_raw = sb("prep_wvo_raw", [128, PAIRS, D])
        bo = sb("prep_bo", [HB, D])

        prep_in = sem("prep_in")
        prep_step = sem("prep_step")
        wide_done = sem("prep_wide_done")
        bias_ps = sem("prep_bias_ps")
        wk_done = sem("prep_wk_done")
        wvo_ps = sem("prep_wvo_ps")
        raw_done = sem("prep_raw_done")
        wvo_done = sem("prep_wvo_done")
        out_bias_ps = sem("prep_out_bias_ps")
        bias_done = sem("prep_bias_done")
        PREP_LOADS = 11
        weights_in = sem("tok_weights_in")
        patches_in = [sem(f"patches_in{i}") for i in range(2 * R)]
        const_in = sem("const_in")
        fill_ready = sem("fill_ready")
        filled = sem("filled")
        tok_ps = sem("tok_ps")
        stats_done = sem("tok_stats_done")
        mv_done = sem("tok_mv_done")
        ve_done = sem("tok_ve_done")
        rstd_done = sem("tok_rstd_done")
        centred_done = sem("tok_centred_done")
        scaled_done = sem("tok_scaled_done")
        y_done = sem("tok_y_done")
        stored = sem("tok_stored")
        vector_step = sem("tok_vector_step")
        block = ctx.enter_context(nc.Block())

        @block.sync
        def _(sp):
            sp.dma_start(tok_w[:, :, :], w["tok_w"].rearrange("p (c n) -> p c n", c=3)).then_inc(weights_in, 16)
            with sp.Fori(0, ROUNDS // 2) as i:
                for p in range(2 * R):
                    sp.wait_ge(tok_ps, START + 2 * R * (i - 1) + p + 1)
                    sp.dma_start(patches[p][:, :], w["patches"][bass.ds(2 * R * i + p, 1), :, :]
                                 .rearrange("a p n -> (a p) n")).then_inc(patches_in[p], 16)
            for tile, src in ((wdown, w["wdown"].rearrange("(c p) n -> p c n", c=2)),
                              (wq, w["wq"].rearrange("(c p) n -> p c n", c=2)),
                              (wo, w["wo1"].rearrange("(k p) n -> p k n", p=128)),
                              (up_vT, w["up_vT"].rearrange("(k p) n -> p k n", p=128))):
                sp.dma_start(tile[:, :, :], src).then_inc(prep_in, 16)
            for tile, name in ((up_k, "up_k"), (latent_gb, "attn1_ln"), (bo, "bo"), (causal["cos"], "cos"),
                               (causal["sin"], "sin"), (causal["mask"], "mask"), (causal["ident_b"], "ident_b")):
                sp.dma_start(tile[:, :], w[name]).then_inc(prep_in, 16)
            for name, tile in const.items():
                sp.dma_start(tile, w[name]).then_inc(const_in, 16)
            sp.wait_ge(const_in, START + 16 * len(const))

        @block.scalar
        def _(act):
            act.dma_start(gamma[:, :], w["tok_gamma"]).then_inc(weights_in, 16)
            act.dma_start(beta[:, :], w["tok_beta"]).then_inc(weights_in, 16)
            act.dma_start(dram["h0"][0:N, :].rearrange("(b t) c -> b t c", t=T)[:, IMG:T, :], w["txt"]
                          ).then_inc(filled, 16)
            act.wait_ge(fill_ready, START + 1)
            act.dma_start(dram["h0"][N:N + 1, :], zeros[0:1, :]).then_inc(filled, 16)
            act.dma_start(dram["h1"][N:NP, :], zeros[:, :]).then_inc(filled, 16)
            act.dma_start(dram["h3"][N:NP, :], zeros[:, :]).then_inc(filled, 16)

            def store(i):
                act.wait_ge(y_done, START + i + 1)
                act.dma_start(dram["h0"][bass.ds(R * i * T, R * T), :].rearrange("(b t) c -> t b c", t=T)[0:IMG, :, :],
                              y[:, :, :]).then_inc(stored, 16)

            with act.Fori(0, ROUNDS - 1) as i:
                store(i)
            act.wait_ge(wvo_ps, START + 3)
            for i in range(3):
                act.activation(wvo_raw[:, 2 * i:2 * i + 2, :], bank[i][:, 0:2 * D]
                               .rearrange("p (c n) -> p c n", c=2), ACT.Copy).then_inc(raw_done, 1)
            store(ROUNDS - 1)
            act.wait_ge(stored, START + 16 * (B // R))
            act.wait_ge(filled, START + 16 * 4)

        @block.gpsimd
        def _(pool):
            pool.memset(zeros[:, :], 0.0).then_inc(fill_ready, 1)
            pool.memset(minus_half[:, :], -0.5).then_inc(fill_ready, 1)
            pool.wait_ge(fill_ready, START + 2)
            with pool.Fori(0, ROUNDS // 2) as i:
                for q in range(2):
                    pool.wait_ge(ve_done, START + 2 * i + q + 1)
                    pool.tensor_tensor(rstd[q][:, :], ve[q][:, :], minus_half[:, :], ALU.pow).then_inc(rstd_done, 1)

        @block.tensor
        def _(pe):
            pe.wait_ge(weights_in, START + 48)
            with pe.Fori(0, ROUNDS // 2) as i:
                for p in range(2 * R):
                    pe.wait_ge(centred_done, START + 2 * R * (i - 1) + p + 1)
                    pe.wait_ge(patches_in[p], START + 16 * (i + 1))
                    for c in range(3):
                        mm = pe.matmul(bank[p][0:IMG, 0:D], patches[p][:, c * IMG:(c + 1) * IMG], tok_w[:, c, :],
                                       start=(c == 0), stop=(c == 2))
                    mm.then_inc(tok_ps, 1)
            pe.wait_ge(prep_in, START + 16 * PREP_LOADS)
            pe.wait_ge(centred_done, START + R * (ROUNDS - 1))
            for i in range(3):
                for j in range(2):
                    for o in range(2):
                        half = slice(o * HD, (o + 1) * HD)
                        mm = pe.matmul(bank[i][half, j * D:(j + 1) * D], up_vT[half, 2 * i + j, :],
                                       wo[half, 2 * i + j, :], start=True, stop=True)
                mm.then_inc(wvo_ps, 1)
            for i in range(2):
                pe.wait_ge(centred_done, START + B)
                mm = pe.matmul(bank[R + i][0:1, 0:2 * D], latent_gb[0:RANK, 1:2], up_k[:, 2 * D * i:2 * D * (i + 1)],
                               start=True, stop=True)
            mm.then_inc(bias_ps, 1)
            pe.wait_ge(raw_done, START + 3)
            pe.wait_ge(wide_done, START + 1)
            for k in range(PAIRS):
                mm = pe.matmul(bank[3][0:HB, 0:D], latent_b[:, :], wvo_raw[:, k, :], start=(k == 0),
                               stop=(k == PAIRS - 1))
            mm.then_inc(out_bias_ps, 1)

        @block.vector
        def _(dve):
            dve.memset(wk[RANK:DC, :], 0.0).then_inc(prep_step, 1)
            dve.memset(latent_b[:, :], 1.0).then_inc(prep_step, 1)
            dve.wait_ge(weights_in, START + 48)

            def measure(i, q):
                for p in range(R):
                    dve.wait_ge(tok_ps, START + R * i + p + 1)
                    dve.bn_stats(stats[q][:, p, :], bank[R * q + p][0:IMG, 0:D]).then_inc(stats_done, 1)
                dve.wait_ge(stats_done, START + R * (i + 1))
                dve.sem_inc(vector_step, 1)
                for p in range(R):
                    dve.bn_aggr(mv[q][:, p, :], stats[q][:, p, :]).then_inc(mv_done, 1)
                dve.wait_ge(mv_done, START + R * (i + 1))
                dve.tensor_scalar(ve[q][:, :], mv[q][:, :, 1], EPS, None, ALU.add).then_inc(ve_done, 1)

            def normalise(i, q):
                dve.wait_ge(rstd_done, START + i + 1)
                dve.wait_ge(scaled_done, START + i)
                for p in range(R):
                    dve.tensor_scalar(centred[:, p, :], bank[R * q + p][0:IMG, 0:D], mv[q][:, p, 0:1],
                                      rstd[q][:, p:p + 1], ALU.subtract, ALU.mult).then_inc(centred_done, 1)
                dve.wait_ge(centred_done, START + R * (i + 1))
                dve.wait_ge(y_done, START + i)
                dve.tensor_tensor(scaled[:, :, :], centred[:, :, :], gamma[:, :].unsqueeze(1).broadcast_to([IMG, R, D]),
                                  ALU.mult).then_inc(scaled_done, 1)
                dve.wait_ge(stored, START + 16 * i)
                dve.wait_ge(scaled_done, START + i + 1)
                dve.tensor_tensor(y[:, :, :], scaled[:, :, :], beta[:, :].unsqueeze(1).broadcast_to([IMG, R, D]),
                                  ALU.add).then_inc(y_done, 1)

            measure(0, 0)
            for i in range(ROUNDS - 1):
                measure(i + 1, (i + 1) % 2)
                normalise(i, i % 2)
            dve.wait_ge(prep_step, START + 2)
            dve.wait_ge(prep_in, START + 16 * PREP_LOADS)
            dve.tensor_scalar(latent_b[:, :], latent_b[:, :], latent_gb[:, 1:2], None, ALU.mult).then_inc(wide_done, 1)
            dve.tensor_scalar(wk[0:RANK, :], up_k[:, :], latent_gb[0:RANK, 0:1], None, ALU.mult).then_inc(wk_done, 1)
            normalise(ROUNDS - 1, (ROUNDS - 1) % 2)
            dve.wait_ge(bias_ps, START + 1)
            for i in range(2):
                dve.tensor_copy(wk[RANK:RANK + 1, 2 * D * i:2 * D * (i + 1)], bank[R + i][0:1, 0:2 * D]
                                ).then_inc(wk_done, 1)
            dve.wait_ge(raw_done, START + 3)
            for i in range(3):
                dve.tensor_scalar(wvo[:, 2 * i:2 * i + 2, :], wvo_raw[:, 2 * i:2 * i + 2, :], latent_gb[:, 0:1], None,
                                  ALU.mult).then_inc(wvo_done, 1)
            dve.wait_ge(out_bias_ps, START + 1)
            dve.tensor_tensor(causal["bias"][:, :], bank[3][0:HB, 0:D], bo[:, :], ALU.add).then_inc(bias_done, 1)


def attend_squared(nc, used, w, dram, const):
    with ExitStack() as ctx:
        def sb(name, shape, dt=F32):
            return ctx.enter_context(nc.sbuf_tensor(name, shape, dt))

        sem = primed_semaphores(nc, used)

        bank = [ctx.enter_context(nc.psum_tensor(f"a_bank{i}", [128, 512], F32)) for i in range(8)]
        w_raw = sb("w_raw", [DC, 2, 4 * D])
        w_all = sb("w_all", [DC + 1, 2, 4 * D])
        b_all = sb("b_all", [1, 4 * D])
        ln_gb = sb("ln_gb", [DC, 2, 2])
        wo = sb("wo0", [DC + 1, 2, D])
        minus_half = sb("a_minus_half", [HB, 2])
        empty_rows = sb("empty_rows", [128, FILL, RW])
        h_norm = [sb(f"h_norm{i}", [HB, 2, D]) for i in range(2)]
        h_res = [sb(f"h_res{i}", [HB, 2, D]) for i in range(2)]
        stats = [sb(f"a_stats{i}", [HB, 2, 6]) for i in range(2)]
        mv = [sb(f"a_mv{i}", [HB, 2, 2]) for i in range(2)]
        ve = [sb(f"a_ve{i}", [HB, 2]) for i in range(2)]
        rstd = [sb(f"a_rstd{i}", [HB, 2]) for i in range(2)]
        z = [sb(f"a_z{i}", [HB, 2, D]) for i in range(2)]
        zT = [sb(f"a_zT{i}", [DC + 1, 2, SEQ]) for i in range(2)]
        uT = [sb(f"a_uT{i}", [DC, 2, SEQ]) for i in range(4)]
        qT = [sb(f"a_qT{i}", [DC, 2, SEQ]) for i in range(2)]
        kT = [sb(f"a_kT{i}", [DC, 2, SEQ]) for i in range(2)]
        v = [sb(f"a_v{i}", [HB, 2, D]) for i in range(4)]
        relu = [sb(f"a_relu{i}", [HB, 2, SEQ]) for i in range(2)]
        aT = [sb(f"a_aT{i}", [HB, 2, SEQ]) for i in range(2)]
        gT = [sb(f"a_gT{i}", [DC + 1, 2, SEQ]) for i in range(2)]
        h1 = [sb(f"a_h1_{i}", [HB, 2, D]) for i in range(2)]
        ident = const["ident"]
        U, Q, K, V = range(4)

        weights_in = sem("a_weights_in")
        norm_in = [sem(f"h_norm_in{i}") for i in range(2)]
        res_in = [sem(f"h_res_in{i}") for i in range(2)]
        bias_ps = sem("bias_ps")
        w_ready = sem("a_w_ready")
        consts = sem("a_consts")
        fill_ready = sem("a_fill_ready")
        filled = sem("a_filled")
        stats_done = sem("a_stats_done")
        mv_done = sem("a_mv_done")
        ve_done = sem("a_ve_done")
        rstd_done = sem("a_rstd_done")
        z_done = sem("a_z_done")
        zT_ps = sem("a_zT_ps")
        zT_done = sem("a_zT_done")
        proj_ps = sem("a_proj_ps")
        silu_done = sem("a_silu_done")
        sim_ps = sem("a_sim_ps")
        relu_done = sem("a_relu_done")
        aT_done = sem("a_aT_done")
        av_ps = sem("a_av_ps")
        gT_done = sem("a_gT_done")
        wo_ps = sem("a_wo_ps")
        h1_done = sem("a_h1_done")
        stored = [sem(f"a_stored{i}") for i in range(2)]
        vector_step = sem("a_vector_step")
        block = ctx.enter_context(nc.Block())
        PAIRS = B // 2

        def run(engine, pair):
            for m in range(2):
                pair(m, m, m == 0, False)
            with engine.Fori(1, PAIRS // 2 - 1) as j:
                for m in range(2):
                    pair(2 * j + m, m, False, False)
            for m in range(2):
                pair(PAIRS - 2 + m, m, False, m == 1)

        @block.sync
        def _(sp):
            sp.dma_start(w_raw[:, :, :], w["attn0_w"].rearrange("(c p) n -> p c n", c=2)).then_inc(weights_in, 16)
            sp.dma_start(b_all[:, :], w["attn0_b"]).then_inc(weights_in, 16)
            sp.dma_start(ln_gb[:, :, :], w["attn0_ln"].rearrange("(c p) n -> p c n", c=2)).then_inc(weights_in, 16)
            sp.dma_start(wo[0:DC, :, :], w["attn0_wo"].rearrange("(c p) n -> p c n", c=2)).then_inc(weights_in, 16)
            sp.dma_start(wo[DC:DC + 1, 0, :], w["attn0_bo"]).then_inc(weights_in, 16)

            def load(i):
                for p in range(2):
                    sp.wait_ge(z_done, START + 4 * i)
                    sp.dma_start(h_norm[p][:, :, :], rows_of(dram["h0"], 2 * i + p)).then_inc(norm_in[p], 16)

            def load_residual(i):
                for p in range(2):
                    sp.wait_ge(h1_done, START + 2 * i)
                    sp.dma_start(h_res[p][:, :, :], rows_of(dram["h0"], 2 * i + p)).then_inc(res_in[p], 16)

            def store(i):
                for p in range(2):
                    b = 2 * i + p
                    sp.wait_ge(h1_done, START + b + 1)
                    sp.dma_start(dram["h1"][bass.ds(b * T, HB), :], h1[p][:, 0, :]).then_inc(stored[p], 16)
                    sp.dma_start(dram["h1"][bass.ds(b * T + HB, T - HB), :], h1[p][0:T - HB, 1, :]
                                 ).then_inc(stored[p], 16)

            load(0)
            load(1)
            load_residual(0)
            with sp.Fori(1, PAIRS - 1) as i:
                load(i + 1)
                store(i - 1)
                load_residual(i)
            store(PAIRS - 2)
            load_residual(PAIRS - 1)
            store(PAIRS - 1)
            for p in range(2):
                sp.wait_ge(stored[p], START + 32 * PAIRS)

        @block.gpsimd
        def _(pool):
            pool.memset(minus_half[:, :], -0.5).then_inc(consts, 1)
            pool.memset(empty_rows[:, :, 0:D + 2], 0.0).then_inc(fill_ready, 1)
            pool.memset(empty_rows[:, :, D + 2:RW].bitcast(I32), NOWHERE).then_inc(fill_ready, 1)
            pool.wait_ge(fill_ready, START + 2)
            for p in range(2):
                pool.memset(zT[p][DC:DC + 1, :, :], 1.0).then_inc(consts, 1)
                pool.memset(gT[p][DC:DC + 1, :, :], 1.0).then_inc(consts, 1)
            pool.wait_ge(consts, START + 5)

            def scales(i):
                for p in range(2):
                    pool.wait_ge(ve_done, START + 2 * i + p + 1)
                    pool.tensor_tensor(rstd[p][:, :], ve[p][:, :], minus_half[:, :], ALU.pow).then_inc(rstd_done, 1)

            def squares(i):
                for p in range(2):
                    b = 2 * i + p
                    pool.wait_ge(av_ps, START + 2 * i)
                    pool.wait_ge(relu_done, START + b + 1)
                    pool.tensor_tensor(aT[p][:, :, :], relu[p][:, :, :], relu[p][:, :, :], ALU.mult
                                       ).then_inc(aT_done, 1)

            scales(0)
            with pool.Fori(0, PAIRS - 1) as i:
                scales(i + 1)
                squares(i)
            squares(PAIRS - 1)

        @block.scalar
        def _(act):
            def copy_zT(b, p):
                act.wait_ge(proj_ps, START + 4 * (b - p))
                act.wait_ge(zT_ps, START + b + 1)
                act.activation(zT[p][0:DC, :, :], bank[0][0:DC, 0:2 * SEQ].rearrange("p (c n) -> p c n", c=2),
                               ACT.Copy).then_inc(zT_done, 1)

            def pair(i, m, first, last):
                for p in range(2):
                    b = 2 * i + p
                    act.wait_ge(sim_ps, START + 2 * i)
                    act.wait_ge(av_ps, START + 2 * (i - 1))
                    act.wait_ge(gT_done, START + 2 * (i - 1))
                    for n, (bk, tile) in enumerate(((1, qT[p]), (2, kT[p]), (3, v[2 * m + p]), (4, uT[2 * m + p]))):
                        act.wait_ge(proj_ps, START + 4 * b + n + 1)
                        rows, width = (HB, D) if n == 2 else (DC, SEQ)
                        act.activation(tile[:, :, :],
                                       bank[bk][0:rows, 0:2 * width].rearrange("p (c n) -> p c n", c=2),
                                       ACT.Silu).then_inc(silu_done, 1)
                for p in range(2):
                    b = 2 * i + p
                    act.wait_ge(aT_done, START + 2 * i)
                    act.wait_ge(sim_ps, START + b + 1)
                    act.activation(relu[p][:, :, :], bank[5][0:HB, 0:2 * SEQ].rearrange("p (c n) -> p c n", c=2),
                                   ACT.Relu, scale=float(T) ** -0.5).then_inc(relu_done, 1)
                    if not last:
                        copy_zT(b + 2, p)

            for p in range(2):
                copy_zT(p, p)
            act.wait_ge(fill_ready, START + 2)
            for r in range(0, ROWS0, FILL * 128):
                act.dma_start(dram["slots0"][r:r + FILL * 128, :].rearrange("(p j) c -> p j c", j=FILL),
                              empty_rows[:, :, :]).then_inc(filled, 16)
            run(act, pair)
            act.wait_ge(filled, START + 16 * (ROWS0 // (FILL * 128)))

        @block.tensor
        def _(pe):
            pe.wait_ge(weights_in, START + 80)
            for half in range(2):
                for c in range(2):
                    mm = pe.matmul(bank[1 + half][0:1, 0:2 * D], ln_gb[:, c, 1:2],
                                   w_raw[:, c, half * 2 * D:(half + 1) * 2 * D], start=(c == 0), stop=(c == 1))
            mm.then_inc(bias_ps, 1)
            pe.wait_ge(consts, START + 5)

            def transposes(b, p):
                pe.wait_ge(zT_done, START + b)
                pe.wait_ge(z_done, START + 2 * b + 2)
                for t in range(2):
                    for c in range(2):
                        mm = pe.transpose(bank[0][0:DC, c * SEQ + t * HB:c * SEQ + (t + 1) * HB],
                                          z[p][:, t, c * DC:(c + 1) * DC], ident[0:HB, 0:HB])
                mm.then_inc(zT_ps, 1)

            def project(b, p, n):
                kind, bk = (Q, K, V, U)[n], n + 1
                pe.wait_ge(silu_done, START + 4 * (b - 1) + n + 1)
                pe.wait_ge(zT_done, START + b + 1)
                for half in range(2):
                    for c in range(2):
                        rows = DC + 1 if c == 0 else DC
                        if kind == V:
                            mm = pe.matmul(bank[bk][0:HB, half * D:(half + 1) * D],
                                           zT[p][0:rows, c, half * HB:(half + 1) * HB],
                                           w_all[0:rows, c, V * D:(V + 1) * D], start=(c == 0), stop=(c == 1))
                        else:
                            at = kind * D + half * DC
                            mm = pe.matmul(bank[bk][0:DC, half * SEQ:(half + 1) * SEQ],
                                           w_all[0:rows, c, at:at + DC], zT[p][0:rows, c, :],
                                           start=(c == 0), stop=(c == 1))
                mm.then_inc(proj_ps, 1)

            def scores(b, p):
                pe.wait_ge(relu_done, START + b)
                pe.wait_ge(silu_done, START + 4 * b + 2)
                for t in range(2):
                    for c in range(2):
                        mm = pe.matmul(bank[5][0:HB, t * SEQ:(t + 1) * SEQ], kT[p][:, c, t * HB:(t + 1) * HB],
                                       qT[p][:, c, :], start=(c == 0), stop=(c == 1))
                mm.then_inc(sim_ps, 1)

            def values(b, p, m):
                pe.wait_ge(gT_done, START + b)
                pe.wait_ge(silu_done, START + 4 * b + 3)
                pe.wait_ge(aT_done, START + b + 1)
                for c in range(2):
                    for t in range(2):
                        rows = HB if t == 0 else T - HB
                        mm = pe.matmul(bank[6][0:DC, c * SEQ:(c + 1) * SEQ],
                                       v[2 * m + p][0:rows, t, c * DC:(c + 1) * DC], aT[p][0:rows, t, :],
                                       start=(t == 0), stop=(t == 1))
                mm.then_inc(av_ps, 1)

            def outputs(b, p):
                pe.wait_ge(h1_done, START + b)
                pe.wait_ge(gT_done, START + b + 1)
                for t in range(2):
                    for c in range(2):
                        rows = DC + 1 if c == 0 else DC
                        mm = pe.matmul(bank[7][0:HB, t * D:(t + 1) * D], gT[p][0:rows, c, t * HB:(t + 1) * HB],
                                       wo[0:rows, c, :], start=(c == 0), stop=(c == 1))
                mm.then_inc(wo_ps, 1)

            def pair(i, m, first, last):
                for p in range(2):
                    b = 2 * i + p
                    for n in range(4):
                        project(b, p, n)
                        if p == 0 and n in (0, 2) and not first:
                            values(b - 2 + n // 2, n // 2, m ^ 1)
                        if (p, n) == (0, 3) and not first:
                            outputs(b - 2, 0)
                        if (p, n) == (1, 1) and not first:
                            outputs(b - 2, 1)
                for p in range(2):
                    scores(2 * i + p, p)
                    if not last:
                        transposes(2 * i + 2 + p, p)

            for p in range(2):
                transposes(p, p)
            pe.wait_ge(w_ready, START + 2 + 2)
            run(pe, pair)
            for p in range(2):
                values(B - 2 + p, p, 1)
            for p in range(2):
                outputs(B - 2 + p, p)

        @block.vector
        def _(dve):
            dve.wait_ge(weights_in, START + 80)
            for c in range(2):
                dve.tensor_scalar(w_all[0:DC, c, :], w_raw[:, c, :], ln_gb[:, c, 0:1], None, ALU.mult
                                  ).then_inc(w_ready, 1)

            def normalise(i):
                for p in range(2):
                    dve.wait_ge(norm_in[p], START + 16 * (i + 1))
                    for t in range(2):
                        dve.bn_stats(stats[p][:, t, :], h_norm[p][:, t, :]).then_inc(stats_done, 1)
                for p in range(2):
                    b = 2 * i + p
                    dve.wait_ge(stats_done, START + 2 * b + 2)
                    dve.sem_inc(vector_step, 1)
                    for t in range(2):
                        dve.bn_aggr(mv[p][:, t, :], stats[p][:, t, :]).then_inc(mv_done, 1)
                for p in range(2):
                    b = 2 * i + p
                    dve.wait_ge(mv_done, START + 2 * b + 2)
                    dve.tensor_scalar(ve[p][:, :], mv[p][:, :, 1], 1.0 + EPS, EPS * EPS, ALU.mult, ALU.add
                                      ).then_inc(ve_done, 1)
                for p in range(2):
                    b = 2 * i + p
                    dve.wait_ge(zT_ps, START + 2 * i)
                    dve.wait_ge(rstd_done, START + b + 1)
                    for t in range(2):
                        dve.tensor_scalar(z[p][:, t, :], h_norm[p][:, t, :], mv[p][:, t, 0:1], rstd[p][:, t:t + 1],
                                          ALU.subtract, ALU.mult).then_inc(z_done, 1)

            def gate_and_add(i, m):
                for p in range(2):
                    b = 2 * i + p
                    dve.wait_ge(wo_ps, START + 2 * i)
                    dve.wait_ge(silu_done, START + 4 * b + 4)
                    dve.wait_ge(av_ps, START + b + 1)
                    dve.tensor_tensor(gT[p][0:DC, :, :], bank[6][0:DC, 0:2 * SEQ].rearrange("p (c n) -> p c n", c=2),
                                      uT[2 * m + p][:, :, :], ALU.mult).then_inc(gT_done, 1)
                for p in range(2):
                    b = 2 * i + p
                    dve.wait_ge(stored[p], START + 32 * i)
                    dve.wait_ge(res_in[p], START + 16 * (i + 1))
                    dve.wait_ge(wo_ps, START + b + 1)
                    dve.tensor_tensor(h1[p][:, :, :], bank[7][0:HB, 0:2 * D].rearrange("p (t n) -> p t n", t=2),
                                      h_res[p][:, :, :], ALU.add).then_inc(h1_done, 1)

            def pair(i, m, first, last):
                if not first:
                    gate_and_add(i - 1, m ^ 1)
                if not last:
                    normalise(i + 1)

            normalise(0)
            dve.wait_ge(bias_ps, START + 1)
            for half in range(2):
                dve.tensor_tensor(w_all[DC:DC + 1, 0, half * 2 * D:(half + 1) * 2 * D], bank[1 + half][0:1, 0:2 * D],
                                  b_all[:, half * 2 * D:(half + 1) * 2 * D], ALU.add).then_inc(w_ready, 1)
            run(dve, pair)
            gate_and_add(PAIRS - 1, 1)


def dispatch(nc, used, w, dram, const, layer, load_ahead, split_high=None, split_low=None):
    experts, top = (E0, 1) if layer == 0 else (E1, 2)
    region = NP if layer == 0 else CAPR
    h, slots = dram["h1" if layer == 0 else "h3"], dram[f"slots{layer}"]
    GT = 5
    GROUPS = TILES // GT
    M = top * experts
    with ExitStack() as ctx:
        def sb(name, shape, dt=F32):
            return ctx.enter_context(nc.sbuf_tensor(f"r{layer}_{name}", shape, dt))

        primed = primed_semaphores(nc, used)

        def sem(name):
            return primed(f"r{layer}_{name}")

        bank = [ctx.enter_context(nc.psum_tensor(f"r{layer}_bank{i}", [128, 512], F32)) for i in range(8)]
        gate = sb("gate", [DC, 2, experts])
        bias = sb("bias", [128, experts])
        centre = sb("centre", [128, experts])
        minus_half = sb("minus_half", [128, GT])
        hg = [sb(f"h{i}", [128, GT, D]) for i in range(GROUPS)]
        rows = [sb(f"rows{i}", [128, GT, RW]) for i in range(GROUPS)]
        stats = [sb(f"stats{i}", [128, GT, 6]) for i in range(GROUPS)]
        mv = [sb(f"mv{i}", [128, GT, 2]) for i in range(GROUPS)]
        ve = [sb(f"ve{i}", [128, GT]) for i in range(GROUPS)]
        rstd = [sb(f"rstd{i}", [128, GT]) for i in range(GROUPS)]
        zT = [sb(f"zT{i}", [DC, GT, 2, 128]) for i in range(GROUPS)]
        logits = [sb(f"logits{i}", [128, GT, 8]) for i in range(GROUPS)]
        best = [sb(f"best{i}", [128, GT, 8]) for i in range(GROUPS)]
        best_at = [sb(f"best_at{i}", [128, GT, 8], U32) for i in range(GROUPS)]
        chosen = [sb(f"chosen{i}", [128, GT, top, experts], BF16) for i in range(GROUPS)]
        rank = [sb(f"rank{i}", [128, GT, M]) for i in range(GROUPS)]
        mine = [sb(f"mine{i}", [128, GT, M]) for i in range(GROUPS)]
        place = [sb(f"place{i}", [128, GT, top]) for i in range(GROUPS)]
        over = [sb(f"over{i}", [128, GT, top]) for i in range(GROUPS)]
        base = [sb(f"base{i}", [128, GT, top]) for i in range(GROUPS)]
        kept = [sb(f"kept{i}", [128, GT, top]) for i in range(GROUPS)]
        slot = [sb(f"slot{i}", [128, GT * top], I32) for i in range(GROUPS)]
        gap = [sb(f"gap{i}", [128, GT]) for i in range(GROUPS)]
        ex = [sb(f"ex{i}", [128, GT]) for i in range(GROUPS)]
        den = [sb(f"den{i}", [128, GT]) for i in range(GROUPS)]
        seen = sb("seen", [128, M])
        full = sb("full", [1, E0, TILES])
        in_use = sb("in_use", [1, E0])
        ends = sb("ends", [1, E0])
        past = sb("past", [1, TILES0, E0 - 1])
        expert_f = sb("expert_f", [1, TILES0])
        skipped = sb("skipped", [1, TILES0, E0 - 1])
        skip = sb("skip", [1, TILES0])
        own = sb("own", [1, TILES0])
        first = sb("first", [1, TILES0])
        expert_no, before, ones = const["expert_no"], const["before"], const["ones"]
        ident = const["ident"]

        gate_in = sem("gate_in")
        bias_in = sem("bias_in")
        h_in = [sem(f"h_in{i}") for i in range(GROUPS)]
        consts = sem("consts")
        rowno = sem("rowno")
        bias_done = sem("bias_done")
        stats_done = sem("stats_done")
        mv_done = sem("mv_done")
        ve_done = sem("ve_done")
        rstd_done = sem("rstd_done")
        z_done = sem("z_done")
        zT_ps = sem("zT_ps")
        zT_done = sem("zT_done")
        logits_ps = sem("logits_ps")
        logits_done = sem("logits_done")
        best_done = sem("best_done")
        at_done = sem("at_done")
        chosen_done = sem("chosen_done")
        rank_ps = sem("rank_ps")
        rank_done = sem("rank_done")
        seen_done = sem("seen_done")
        base_done = sem("base_done")
        den_done = sem("den_done")
        first_done = sem("first_done")
        mine_done = sem("mine_done")
        place_done = sem("place_done")
        over_done = sem("over_done")
        kept_done = sem("kept_done")
        table = sem("table")
        gap_done = sem("gap_done")
        ex_done = sem("ex_done")
        weights_done = sem("weights_done")
        slot_done = sem("slot_done")
        scattered = unprimed_semaphore(nc, used, f"r{layer}_scattered")
        block = ctx.enter_context(nc.Block())

        @block.sync
        def _(sp):
            def load_h(g):
                sp.dma_start(hg[g][:, :, :], h[g * GT * 128:(g + 1) * GT * 128, :]
                             .rearrange("(j p) c -> p j c", p=128)).then_inc(h_in[g], 16)

            load_h(0)
            sp.dma_start(gate[:, :, :], w[f"gate{layer}_w"].rearrange("(c p) n -> p c n", c=2)).then_inc(gate_in, 16)
            if layer == 0:
                sp.dma_start(bias[:, :], w["gate0_b"].broadcast_to([128, experts])).then_inc(bias_in, 16)
                sp.dma_start(centre[:, :], w["gate0_centre"].broadcast_to([128, experts])).then_inc(bias_in, 16)
            for g in range(1, GROUPS):
                load_h(g)
            load_ahead(sp)

        @block.gpsimd
        def _(pool):
            pool.memset(minus_half[:, :], -0.5).then_inc(consts, 1)
            for g in range(GROUPS):
                pool.memset(rows[g][:, :, D:D + 2], 1.0).then_inc(rowno, 1)
                for k in range(2):
                    pool.iota(rows[g][:, :, D + 2 + k:D + 3 + k].bitcast(I32), pattern=[[128, GT], [0, 1]],
                              base=k * NP + g * GT * 128, channel_multiplier=1).then_inc(rowno, 1)
            pool.wait_ge(consts, START + 1)
            pool.wait_ge(rowno, START + 3 * GROUPS)

            for g in range(GROUPS):
                pool.wait_ge(ve_done, START + g + 1)
                pool.tensor_tensor(rstd[g][:, :], ve[g][:, :], minus_half[:, :], ALU.pow).then_inc(rstd_done, 1)
            for g in range(GROUPS):
                pool.wait_ge(z_done, START + GT * (g + 1))
                if layer:
                    pool.wait_ge(weights_done, START + g + 1)
                pool.wait_ge(slot_done, START + g + 1)
                for j in range(GT):
                    for k in range(top):
                        pool.indirect_dma_start(
                            slots, bass.IndirectOffsetOnAxis(ap=slot[g][:, j * top + k:j * top + k + 1], axis=0),
                            rows[g][:, j, :], None, bounds_check=slots.shape[0] - 1, oob_is_err=False
                        ).then_inc(scattered, 16)
            pool.wait_ge(scattered, 16 * TILES * top)

        @block.scalar
        def _(act):
            def copy_zT(g):
                for n in range(GT):
                    act.wait_ge(zT_ps, START + GT * g + n + 1)
                    act.activation(zT[g][:, n, :, :], bank[n][0:DC, 0:256].rearrange("p (c n) -> p c n", c=2),
                                   ACT.Copy).then_inc(zT_done, 1)

            def exps(g):
                act.wait_ge(gap_done, START + g + 1)
                act.activation(ex[g][:, :], gap[g][:, :], ACT.Exp).then_inc(ex_done, 1)

            copy_zT(0)
            copy_zT(1)
            if layer:
                exps(0)
                exps(1)
            if split_high:
                split_high(act)
            copy_zT(2)
            copy_zT(3)
            if layer:
                exps(2)
                exps(3)

        @block.tensor
        def _(pe):
            def transposes(g):
                for j in range(GT):
                    pe.wait_ge(zT_done, START + GT * (g - 1) + j + 1)
                    pe.wait_ge(z_done, START + GT * g + j + 1)
                    for c in range(2):
                        mm = pe.transpose(bank[j][0:DC, c * 128:(c + 1) * 128],
                                          rows[g][:, j, c * DC:(c + 1) * DC], ident)
                    mm.then_inc(zT_ps, 1)

            def gates(g):
                pe.wait_ge(logits_done, START + g)
                pe.wait_ge(zT_done, START + GT * (g + 1))
                for j in range(GT):
                    for c in range(2):
                        mm = pe.matmul(bank[5][:, 8 * j:8 * j + experts], zT[g][:, j, c, :], gate[:, c, :],
                                       start=(c == 0), stop=(c == 1))
                mm.then_inc(logits_ps, 1)

            def ranks(g):
                out = bank[6 + g % 2]
                pe.wait_ge(seen_done, START + g)
                pe.wait_ge(chosen_done, START + top * (g + 1))
                for j in range(GT):
                    for earlier in range(j + 1):
                        pe.matmul(out[:, M * j:M * (j + 1)], before if earlier == j else ones,
                                  chosen[g][:, earlier, :, :].rearrange("p k e -> p (k e)"),
                                  start=(earlier == 0), stop=(earlier == j))
                for j in range(GT):
                    mm = pe.matmul(out[:, 128:128 + M], ones, chosen[g][:, j, :, :].rearrange("p k e -> p (k e)"),
                                   start=(j == 0), stop=(j == GT - 1))
                mm.then_inc(rank_ps, 1)

            transposes(0)
            pe.wait_ge(gate_in, START + 16)
            for g in (0, 2):
                gates(g)
                transposes(g + 1)
                ranks(g)
                gates(g + 1)
                ranks(g + 1)
                if g == 0:
                    transposes(2)

        @block.vector
        def _(dve):
            dve.memset(seen[:, :], 0.0).then_inc(seen_done, 1)
            for g in range(GROUPS):
                dve.memset(logits[g][:, :, :], -3e38).then_inc(consts, 1)
            dve.wait_ge(consts, START + GROUPS + 1)
            dve.wait_ge(seen_done, START + 1)
            dve.wait_ge(rowno, START + 3 * GROUPS)
            numbers = expert_no[:, 0:experts].unsqueeze(1).broadcast_to([128, GT, experts])

            def measure(g):
                dve.wait_ge(h_in[g], START + 16)
                for j in range(GT):
                    dve.bn_stats(stats[g][:, j, :], hg[g][:, j, :]).then_inc(stats_done, 1)
                dve.wait_ge(stats_done, START + GT * (g + 1))
                for j in range(GT):
                    dve.bn_aggr(mv[g][:, j, :], stats[g][:, j, :]).then_inc(mv_done, 1)
                dve.wait_ge(mv_done, START + GT * (g + 1))
                dve.tensor_scalar(ve[g][:, :], mv[g][:, :, 1], EPS, None, ALU.add).then_inc(ve_done, 1)

            def normalise(g):
                dve.wait_ge(rstd_done, START + g + 1)
                for j in range(GT):
                    dve.tensor_scalar(rows[g][:, j, 0:D], hg[g][:, j, :], mv[g][:, j, 0:1], rstd[g][:, j:j + 1],
                                      ALU.subtract, ALU.mult).then_inc(z_done, 1)

            def choose(g):
                dve.wait_ge(logits_ps, START + g + 1)
                raw = bank[5][:, 0:8 * GT].rearrange("p (j e) -> p j e", e=8)[:, :, 0:experts]
                if layer == 0:
                    dve.wait_ge(bias_done, START + 1)
                    dve.tensor_tensor(logits[g][:, :, 0:experts], raw,
                                      bias[:, :].unsqueeze(1).broadcast_to([128, GT, experts]), ALU.add
                                      ).then_inc(logits_done, 1)
                else:
                    dve.tensor_copy(logits[g][:, :, 0:experts], raw).then_inc(logits_done, 1)
                dve.wait_ge(logits_done, START + g + 1)
                for j in range(GT):
                    dve.max(best[g][:, j, :], logits[g][:, j, :]).then_inc(best_done, 1)
                dve.wait_ge(best_done, START + GT * (g + 1))
                for j in range(GT):
                    dve.max_index(best_at[g][:, j, :], best[g][:, j, :], logits[g][:, j, :]).then_inc(at_done, 1)
                dve.wait_ge(at_done, START + GT * (g + 1))
                for k in range(top):
                    dve.tensor_tensor(chosen[g][:, :, k, :], numbers,
                                      best_at[g][:, :, k:k + 1].broadcast_to([128, GT, experts]),
                                      ALU.is_equal).then_inc(chosen_done, 1)
                if layer:
                    dve.tensor_tensor(gap[g][:, :], best[g][:, :, 1], best[g][:, :, 0], ALU.subtract
                                      ).then_inc(gap_done, 1)
                for k in range(top):
                    dve.tensor_scalar(base[g][:, :, k], best_at[g][:, :, k], float(region * top),
                                      float(k * region), ALU.mult, ALU.add).then_inc(base_done, 1)

            def weights(g):
                dve.wait_ge(ex_done, START + g + 1)
                dve.tensor_scalar(den[g][:, :], ex[g][:, :], 1.0, None, ALU.add).then_inc(den_done, 1)
                dve.wait_ge(den_done, START + g + 1)
                dve.reciprocal(rows[g][:, :, D], den[g][:, :]).then_inc(first_done, 1)
                dve.wait_ge(first_done, START + g + 1)
                dve.tensor_tensor(rows[g][:, :, D + 1], ex[g][:, :], rows[g][:, :, D], ALU.mult
                                  ).then_inc(weights_done, 1)

            def slots_of(g):
                dve.wait_ge(rank_ps, START + g + 1)
                dve.wait_ge(seen_done, START + g + 1)
                out = bank[6 + g % 2]
                dve.tensor_tensor(rank[g][:, :, :], out[:, 0:M * GT].rearrange("p (j m) -> p j m", m=M),
                                  seen[:, :].unsqueeze(1).broadcast_to([128, GT, M]), ALU.add).then_inc(rank_done, 1)
                dve.wait_ge(rank_done, START + g + 1)
                dve.tensor_tensor(seen[:, :], out[:, 128:128 + M], seen[:, :], ALU.add).then_inc(seen_done, 1)
                dve.tensor_tensor(mine[g][:, :, :], rank[g][:, :, :],
                                  chosen[g][:, :, :, :].rearrange("p j k e -> p j (k e)"), ALU.mult
                                  ).then_inc(mine_done, 1)
                dve.wait_ge(mine_done, START + g + 1)
                dve.tensor_reduce(place[g][:, :, :].rearrange("p j k -> p (j k)"),
                                  mine[g][:, :, :].rearrange("p j (k e) -> p (j k) e", k=top), AX.X, ALU.add
                                  ).then_inc(place_done, 1)
                dve.wait_ge(place_done, START + g + 1)
                dve.tensor_scalar(over[g][:, :, :], place[g][:, :, :], float(CAP if layer else NP),
                                  float(NOWHERE), ALU.is_ge, ALU.mult).then_inc(over_done, 1)
                dve.wait_ge(base_done, START + top * (g + 1))
                dve.tensor_tensor(kept[g][:, :, :], place[g][:, :, :], base[g][:, :, :], ALU.add
                                  ).then_inc(kept_done, 1)
                dve.wait_ge(over_done, START + g + 1)
                dve.wait_ge(kept_done, START + g + 1)
                dve.tensor_tensor(slot[g][:, :].rearrange("p (j k) -> p j k", k=top), kept[g][:, :, :],
                                  over[g][:, :, :], ALU.add).then_inc(slot_done, 1)

            measure(0)
            measure(1)
            normalise(0)
            normalise(1)
            measure(2)
            measure(3)
            if layer == 0:
                dve.wait_ge(bias_in, START + 32)
                dve.tensor_tensor(bias[:, :], bias[:, :], centre[:, :], ALU.subtract).then_inc(bias_done, 1)
            for g in range(GROUPS):
                choose(g)
                if layer:
                    weights(g)
                slots_of(g)
                if g == 0:
                    normalise(2)
                    normalise(3)
                if split_low:
                    split_low(dve, g)
            if layer == 0:
                counted = seen[0:1, :]
                dve.wait_ge(seen_done, START + GROUPS + 1)
                dve.tensor_tensor(full[:, :, :], counted.unsqueeze(2).broadcast_to([1, E0, TILES]),
                                  const["tile_rows"][:, 0:TILES].unsqueeze(1).broadcast_to([1, E0, TILES]), ALU.is_gt
                                  ).then_inc(table, 1)
                dve.wait_ge(table, START + 1)
                dve.tensor_reduce(in_use[:, :], full[:, :, :], AX.X, ALU.add).then_inc(table, 1)
                dve.wait_ge(table, START + 2)
                dve.tensor_copy(ends[:, 0:1], in_use[:, 0:1]).then_inc(table, 1)
                for e in range(1, E0):
                    dve.wait_ge(table, START + 2 + e)
                    dve.tensor_tensor(ends[:, e:e + 1], ends[:, e - 1:e], in_use[:, e:e + 1], ALU.add
                                      ).then_inc(table, 1)
                dve.wait_ge(table, START + 2 + E0)
                dve.tensor_tensor(past[:, :, :], const["tile_no"].unsqueeze(2).broadcast_to([1, TILES0, E0 - 1]),
                                  ends[:, 0:E0 - 1].unsqueeze(1).broadcast_to([1, TILES0, E0 - 1]), ALU.is_ge
                                  ).then_inc(table, 1)
                dve.wait_ge(table, START + 3 + E0)
                dve.tensor_reduce(expert_f[:, :], past[:, :, :], AX.X, ALU.add).then_inc(table, 1)
                dve.tensor_tensor(skipped[:, :, :], past[:, :, :],
                                  in_use[:, 0:E0 - 1].unsqueeze(1).broadcast_to([1, TILES0, E0 - 1]), ALU.mult
                                  ).then_inc(table, 1)
                dve.wait_ge(table, START + 5 + E0)
                dve.tensor_reduce(skip[:, :], skipped[:, :, :], AX.X, ALU.add).then_inc(table, 1)
                dve.wait_ge(table, START + 6 + E0)
                dve.tensor_tensor(own[:, :], const["tile_no"], skip[:, :], ALU.subtract).then_inc(table, 1)
                dve.tensor_scalar(first[:, :], expert_f[:, :], float(NP), None, ALU.mult).then_inc(table, 1)
                dve.wait_ge(table, START + 8 + E0)
                dve.scalar_tensor_tensor(const["tile_row"], own[:, :], 128.0, first[:, :], ALU.mult, ALU.add
                                         ).then_inc(table, 1)
                dve.tensor_scalar(const["tile_expert"], expert_f[:, :], 1.0, None, ALU.mult).then_inc(table, 1)


def gelu_weights(nc, used, ctx):
    sem = primed_semaphores(nc, used)
    return {"w1": ctx.enter_context(nc.sbuf_tensor("e0_w1", [DC + 1, 2, E0, H0], F32)),
            "w2": ctx.enter_context(nc.sbuf_tensor("e0_w2", [128, H0 // 128, E0, D], F32)),
            "w1_parts": [ctx.enter_context(nc.sbuf_tensor(f"e0_w1_{part}", [DC + 1, 2, E0, H0], F32R))
                         for part in ("high", "low")],
            "w1_in": sem("e0_w1_in"), "w1_high": sem("e0_w1_high"), "w1_low": sem("e0_w1_low"),
            "in": sem("e0_w2_in")}


def load_gelu(sp, w, weights):
    w1, w2, w1_in, w_in = weights["w1"], weights["w2"], weights["w1_in"], weights["in"]
    for c in range(2):
        sp.dma_start(w1[0:DC, c, :, :], w["e0_w1"][c * DC:(c + 1) * DC, :]
                     .rearrange("p (e n) -> p e n", e=E0)).then_inc(w1_in, 16)
    sp.dma_start(w1[DC:DC + 1, 0, :, :], w["e0_b1"].rearrange("p (e n) -> p e n", e=E0)).then_inc(w1_in, 16)
    for e in range(E0):
        sp.dma_start(w2[:, :, e, :], w["e0_w2"][e].rearrange("(k p) n -> p k n", p=128)).then_inc(w_in, 16)


def high_gelu(act, weights):
    act.wait_ge(weights["w1_in"], START + 48)
    for e in range(E0):
        for c, rows in enumerate((DC + 1, DC)):
            act.activation(weights["w1_parts"][0][0:rows, c, e, :], weights["w1"][0:rows, c, e, :], ACT.Copy
                           ).then_inc(weights["w1_high"], 1)


def low_gelu(dve, weights, g):
    high, low = weights["w1_parts"]
    for e in ((), range(E0 - 1), (E0 - 1,), ())[g]:
        for c, rows in enumerate((DC + 1, DC)):
            dve.wait_ge(weights["w1_high"], START + 2 * e + c + 1)
            dve.tensor_tensor(low[0:rows, c, e, :], weights["w1"][0:rows, c, e, :],
                              high[0:rows, c, e, :].bitcast(F32), ALU.subtract).then_inc(weights["w1_low"], 1)


def experts_gelu(nc, used, w, dram, const, weights):
    w1_parts, w2 = weights["w1_parts"], weights["w2"]
    TURN, DOWN = 1, 2
    BODY = 4
    with ExitStack() as ctx:
        def sb(name, shape, dt=F32):
            return ctx.enter_context(nc.sbuf_tensor(f"e0_{name}", shape, dt))

        primed = primed_semaphores(nc, used)

        def sem(name):
            return primed(f"e0_{name}")

        bank = [ctx.enter_context(nc.psum_tensor(f"e0_bank{i}", [128, n, 512], F32))
                for i, n in enumerate((1, 2, 2, 2, 1))]
        T_PS, Y_PS = bank[0], bank[4]
        UP_PS, HT_PS = (bank[1], bank[2]), bank[3]
        HC = H0 // 128
        x = [sb(f"x{i}", [128, RW]) for i in range(BODY)]
        to = [sb(f"to{i}", [128, 1], I32) for i in range(BODY)]
        b2 = [sb(f"b2_{i}", [128, D]) for i in range(BODY)]
        xT = [[sb(f"xT_{part}{i}", [DC + 1, 2, 128], F32R) for part in ("high", "low")] for i in range(2)]
        hid = [sb(f"hid{i}", [128, H0]) for i in range(2)]
        hT = [sb(f"hT{i}", [128, HC, 128]) for i in range(2)]
        y = [sb(f"y{i}", [128, D]) for i in range(2)]
        empty_rows = sb("empty_rows", [128, 2 * CAPT, RW])
        zeros = sb("zeros", [128, 2 * D * NP // 128 // 4])
        ident = const["ident"]

        x_in = [sem(f"x_in{i}") for i in range(BODY)]
        b2_in = [sem(f"b2_in{i}") for i in range(BODY)]
        consts = sem("consts")
        xT_ps = sem("xT_ps")
        xT_high = sem("xT_high")
        xT_low = sem("xT_low")
        up_ps = sem("up_ps")
        hid_done = sem("hid_done")
        hT_ps = sem("hT_ps")
        hT_done = sem("hT_done")
        y_ps = sem("y_ps")
        y_done = sem("y_done")
        to_done = sem("to_done")
        y_free = sem("y_free")
        fill_ready = sem("fill_ready")
        filled = sem("filled")
        pool_step = sem("pool_step")
        scattered = [unprimed_semaphore(nc, used, f"e0_scattered{i}") for i in range(2)]
        block = ctx.enter_context(nc.Block())

        def run(engine, tile):
            for n in range(BODY):
                tile(0, n, True, False)
            with engine.Fori(1, TILES0 // BODY - 1) as i:
                for n in range(BODY):
                    tile(i, n, False, False)
            for n in range(BODY):
                tile(TILES0 // BODY - 1, n, False, n == BODY - 1)

        @block.sync
        def _(sp):
            with sp.Fori(0, TILES0 // BODY) as i:
                for n in range(BODY):
                    t = BODY * i + n
                    row = sp.value_load(const["tile_row"][0:1, bass.ds(t, 1)], min_val=0, max_val=ROWS0 - 128)
                    expert = sp.value_load(const["tile_expert"][0:1, bass.ds(t, 1)], min_val=0, max_val=E0 - 1)
                    sp.wait_ge(xT_ps, START + t - BODY + 1)
                    sp.wait_ge(to_done, START + t - BODY + 1)
                    sp.dma_start(x[n][:, :], dram["slots0"][bass.ds(row, 128), :]).then_inc(x_in[n], 16)
                    sp.wait_ge(y_done, START + t - BODY + 1)
                    sp.dma_start(b2[n][:, :], w["e0_b2"][bass.ds(expert, 1), :].broadcast_to([128, D])
                                 ).then_inc(b2_in[n], 16)

        @block.gpsimd
        def _(pool):
            pool.memset(empty_rows[:, :, 0:D + 2], 0.0).then_inc(fill_ready, 1)
            pool.memset(empty_rows[:, :, D + 2:RW].bitcast(I32), NOWHERE).then_inc(fill_ready, 1)
            pool.memset(zeros[:, :], 0.0).then_inc(fill_ready, 1)
            with pool.Fori(0, TILES0 // BODY) as i:
                for n in range(BODY):
                    t, p = BODY * i + n, n % 2
                    pool.wait_ge(to_done, START + t + 1)
                    pool.wait_ge(y_done, START + t + 1)
                    pool.sem_inc(pool_step, 1)
                    pool.indirect_dma_start(dram["y0"], bass.IndirectOffsetOnAxis(ap=to[n][:, 0:1], axis=0), y[p][:, :],
                                            None, bounds_check=NP - 1, oob_is_err=False).then_inc(scattered[p], 16)
                    pool.wait_ge(scattered[p], 16 * (BODY // 2 * i + n // 2 + 1))
                    pool.sem_inc(y_free, 1)

        @block.scalar
        def _(act):
            def units(t, p):
                act.wait_ge(hT_ps, START + t - 1)
                act.wait_ge(up_ps, START + t + 1)
                act.activation(hid[p][:, :].rearrange("p (n f) -> p n f", n=2), UP_PS[p][:, :, 0:H0 // 2],
                               ACT.Gelu).then_inc(hid_done, 1)

            def high_xT(t, p):
                act.wait_ge(up_ps, START + t - 1)
                act.wait_ge(xT_ps, START + t + 1)
                act.activation(xT[p][0][0:DC, :, :], T_PS[0:DC, 0, 0:256].rearrange("p (c n) -> p c n", c=2), ACT.Copy
                               ).then_inc(xT_high, 1)

            high_xT(0, 0)
            for p in range(2):
                high_xT(p + 1, 1 - p)
                units(p, p)
            act.wait_ge(fill_ready, START + 3)
            for e in range(E1):
                rows = 2 * CAPR
                act.dma_start(dram["slots1"][e * rows:(e + 1) * rows, :].rearrange("(p j) c -> p j c", p=128),
                              empty_rows[:, :, :]).then_inc(filled, 16)
            for r in range(0, 2 * NP, NP // 2):
                act.dma_start(dram["y1"][r:r + NP // 2, :].rearrange("(p j) c -> p (j c)", p=128), zeros[:, :]
                              ).then_inc(filled, 16)
            with act.Fori(1, TILES0 // 2 - 1) as i:
                for p in range(2):
                    high_xT(2 * i + p + 1, 1 - p)
                    units(2 * i + p, p)
            high_xT(TILES0 - 1, 1)
            units(TILES0 - 2, 0)
            units(TILES0 - 1, 1)
            act.wait_ge(filled, START + 16 * (E1 + 4))

        @block.tensor
        def _(pe):
            def transposes(t, n, loaded):
                pe.wait_ge(xT_low, START + t)
                pe.wait_ge(x_in[n], loaded)
                for c in range(2):
                    mm = pe.transpose(T_PS[0:DC, 0, c * 128:(c + 1) * 128], x[n][:, c * DC:(c + 1) * DC], ident)
                mm.then_inc(xT_ps, 1)

            def expert_of(t):
                return pe.value_load(const["tile_expert"][0:1, bass.ds(t, 1)], min_val=0, max_val=E0 - 1)

            def up(t, p):
                expert = expert_of(t)
                pe.wait_ge(hid_done, START + t - 1)
                pe.wait_ge(xT_low, START + t + 1)
                for half in range(2):
                    for c in range(2):
                        k = DC + 1 if c == 0 else DC
                        for a, b in PARTS:
                            mm = pe.matmul(UP_PS[p][:, half, 0:H0 // 2], xT[p][b][0:k, c, :],
                                           w1_parts[a][0:k, c, bass.ds(expert, 1), half * H0 // 2:(half + 1) * H0 // 2]
                                           .rearrange("p a n -> p (a n)"), start=(c == 0 and (a, b) == PARTS[0]),
                                           stop=(c == 1 and (a, b) == PARTS[-1]))
                mm.then_inc(up_ps, 1)

            def turn(t, p):
                pe.wait_ge(hT_done, START + 2 * t)
                pe.wait_ge(hid_done, START + t + 1)
                for k in range(HC):
                    mm = pe.transpose(HT_PS[:, k // 3, k % 3 * 128:(k % 3 + 1) * 128],
                                      hid[p][:, k * 128:(k + 1) * 128], ident)
                mm.then_inc(hT_ps, 1)

            def down(t, p):
                expert = expert_of(t)
                pe.wait_ge(y_done, START + t)
                pe.wait_ge(hT_done, START + 2 * t + 2)
                for k in range(HC):
                    mm = pe.matmul(Y_PS[:, 0, 0:D], hT[p][:, k, :],
                                   w2[:, k, bass.ds(expert, 1), :].rearrange("p a n -> p (a n)"),
                                   start=(k == 0), stop=(k == HC - 1))
                mm.then_inc(y_ps, 1)

            def tile(i, n, first, last):
                t = BODY * i + n
                up(t, n % 2)
                if not last:
                    transposes(t + 1, (n + 1) % BODY, START + 16 * (i + (2 if n == BODY - 1 else 1)))
                if n >= TURN or not first:
                    turn(t - TURN, (n - TURN) % 2)
                if n >= DOWN or not first:
                    down(t - DOWN, n % 2)

            pe.wait_ge(consts, START + 4)
            transposes(0, 0, START + 16)
            pe.wait_ge(weights["w1_low"], START + 2 * E0)
            pe.wait_ge(weights["in"], START + 16 * E0)
            run(pe, tile)
            turn(TILES0 - 1, 1)
            down(TILES0 - 2, 0)
            down(TILES0 - 1, 1)

        @block.vector
        def _(dve):
            for high, low in xT:
                dve.memset(high[DC:DC + 1, :, :].bitcast(F32), 1.0).then_inc(consts, 1)
                dve.memset(low[DC:DC + 1, :, :].bitcast(F32), 0.0).then_inc(consts, 1)

            def low_xT(t, p):
                dve.wait_ge(up_ps, START + t - 1)
                dve.wait_ge(xT_high, START + t + 1)
                high, low = xT[p]
                dve.tensor_tensor(low[0:DC, :, :], T_PS[0:DC, 0, 0:256].rearrange("p (c n) -> p c n", c=2),
                                  high[0:DC, :, :].bitcast(F32), ALU.subtract).then_inc(xT_low, 1)

            def copy_to(t, n):
                dve.wait_ge(y_free, START + t - BODY + 1)
                dve.tensor_copy(to[n][:, :], x[n][:, D + 2:D + 3].bitcast(I32)).then_inc(to_done, 1)

            def copy_hT(t, p):
                dve.wait_ge(y_ps, START + t - 1)
                dve.wait_ge(hT_ps, START + t + 1)
                for half in range(2):
                    dve.tensor_copy(hT[p][:, 3 * half:3 * half + 3, :],
                                    HT_PS[:, half, 0:384].rearrange("p (k n) -> p k n", k=3)).then_inc(hT_done, 1)

            def result(t, p, n, loaded):
                dve.wait_ge(y_free, START + t - 1)
                dve.wait_ge(b2_in[n], loaded)
                dve.wait_ge(y_ps, START + t + 1)
                dve.tensor_tensor(y[p][:, :], Y_PS[:, 0, 0:D], b2[n][:, :], ALU.add).then_inc(y_done, 1)

            def tile(i, n, first, last):
                t = BODY * i + n
                if not last:
                    low_xT(t + 1, (n + 1) % 2)
                    copy_to(t + 1, (n + 1) % BODY)
                if n >= TURN or not first:
                    copy_hT(t - TURN, (n - TURN) % 2)
                if n >= DOWN or not first:
                    result(t - DOWN, n % 2, (n - DOWN) % BODY, START + 16 * (i + (1 if n >= DOWN else 0)))

            low_xT(0, 0)
            copy_to(0, 0)
            run(dve, tile)
            copy_hT(TILES0 - 1, 1)
            result(TILES0 - 2, 0, BODY - 2, START + 16 * (TILES0 // BODY))
            result(TILES0 - 1, 1, BODY - 1, START + 16 * (TILES0 // BODY))


def attend_causal(nc, used, w, dram, const, causal):
    SCORE, SHARE, TURN, VALUE, OUT = 2, 3, 4, 5, 6
    PAIRS = HEADS // 2
    A, BT = slice(0, HB), slice(HB, SEQ)
    AK = slice(0, 2 * HB)
    BK = slice(2 * HB, 2 * HB + 2 * SEQ)
    KB = DC
    with ExitStack() as ctx:
        def sb(name, shape, dt=F32):
            return ctx.enter_context(nc.sbuf_tensor(f"c_{name}", shape, dt))

        primed = primed_semaphores(nc, used)

        def sem(name):
            return primed(f"c_{name}")

        def psum(name):
            return ctx.enter_context(nc.psum_tensor(f"c_{name}", [128, 512], F32))

        QK_PS = [psum(f"qk_ps{i}") for i in range(2)]
        S_PS = [psum(f"s_ps{i}") for i in range(2)]
        PT_PS = [psum(f"pT_ps{i}") for i in range(2)]
        X_PS, W_PS = psum("x_ps"), psum("w_ps")
        O_PS = X_PS[:, 0:SEQ]
        Z_PS = X_PS[:, SEQ:3 * SEQ]
        OUT_PS = W_PS[0:HB, 0:2 * D]
        wq, wk, wvo, wdown, bias, cos, sin, mask, ident_b = (
            causal[name] for name in ("wq", "wk", "wvo", "wdown", "bias", "cos", "sin", "mask", "ident_b"))
        minus_half = sb("minus_half", [HB, 2])
        h1 = sb("h1", [HB, 2, D])
        y0 = sb("y0", [HB, 2, D])
        h2 = [sb(f"h2_{i}", [HB, 2, D]) for i in range(2)]
        res = [sb(f"res{i}", [HB, 2, D]) for i in range(2)]
        h3 = sb("h3", [HB, 2, D])
        stats = sb("stats", [HB, 2, 6])
        mv = sb("mv", [HB, 2, 2])
        ve = sb("ve", [HB, 2])
        rstd = sb("rstd", [HB, 2])
        z = sb("z", [HB, 2, D])
        zT = [sb(f"zT{i}", [DC, 2, SEQ]) for i in range(2)]
        c = sb("c", [HB, 2, RANK])
        c_stats = sb("c_stats", [HB, 2, 6])
        c_mv = sb("c_mv", [HB, 2, 2])
        c_ve = sb("c_ve", [HB, 2])
        c_rstd = sb("c_rstd", [HB, 2])
        cz = sb("cz", [HB, 2, RANK])
        latent = [sb(f"latent{i}", [KB, 2, RANK]) for i in range(2)]
        cT = [sb(f"cT{i}", [KB, SEQ]) for i in range(2)]
        turn_cos = [sb(f"turn_cos{i}", [128, 2, SEQ]) for i in range(2)]
        turn_sin = [sb(f"turn_sin{i}", [128, 2, SEQ]) for i in range(2)]
        qT = [sb(f"qT{i}", [128, SEQ]) for i in range(3)]
        kT = [sb(f"kT{i}", [128, 2, SEQ]) for i in range(3)]
        top = [sb(f"top{i}", [HB, 4]) for i in range(3)]
        minus_top = [sb(f"minus_top{i}", [HB, 4]) for i in range(3)]
        total = [sb(f"total{i}", [HB, 4]) for i in range(3)]
        share = [sb(f"share{i}", [HB, 4]) for i in range(3)]
        prob = [sb(f"prob{i}", [HB, 2 * HB + 2 * SEQ]) for i in range(3)]
        pT = [sb(f"pT{i}", [KB, 2 * SEQ + 2 * HB]) for i in range(2)]
        oT = [sb(f"oT{i}", [128, SEQ]) for i in range(2)]
        ident = const["ident"]

        h_in = sem("h_in")
        y_in = sem("y_in")
        consts = sem("consts")
        cleared = sem("cleared")
        h2_done = sem("h2_done")
        stats_done = sem("stats_done")
        mv_done = sem("mv_done")
        ve_done = sem("ve_done")
        rstd_done = sem("rstd_done")
        z_done = sem("z_done")
        zT_ps = sem("zT_ps")
        zT_done = sem("zT_done")
        c_ps = sem("c_ps")
        c_done = sem("c_done")
        c_stats_done = sem("c_stats_done")
        c_mv_done = sem("c_mv_done")
        c_ve_done = sem("c_ve_done")
        c_rstd_done = sem("c_rstd_done")
        cz_done = sem("cz_done")
        latent_done = sem("latent_done")
        cT_ps = sem("cT_ps")
        cT_done = sem("cT_done")
        qk_ps = sem("qk_ps")
        turned = sem("turned")
        q_done = sem("q_done")
        k_done = sem("k_done")
        s_ps = sem("s_ps")
        top_done = sem("top_done")
        minus_done = sem("minus_done")
        exp_done = sem("exp_done")
        share_done = sem("share_done")
        prob_a_done = sem("prob_a_done")
        prob_b_done = sem("prob_b_done")
        pT_ps = sem("pT_ps")
        pT_done = sem("pT_done")
        o_ps = sem("o_ps")
        oT_done = sem("oT_done")
        out_ps = sem("out_ps")
        res_done = sem("res_done")
        h3_done = sem("h3_done")
        stored = sem("stored")
        step = sem("step")
        block = ctx.enter_context(nc.Block())

        def done(i):
            return START + 1 + i

        def run(engine, sequence):
            for q in range(2):
                sequence(q, q, q == 0, False)
            with engine.Fori(1, B // 2 - 1) as i:
                for q in range(2):
                    sequence(2 * i + q, q, False, False)
            for q in range(2):
                sequence(B - 2 + q, q, False, q == 1)

        @block.sync
        def _(sp):
            def load(b):
                sp.wait_ge(h2_done, START + b)
                sp.dma_start(h1[:, :, :], rows_of(dram["h1"], b)).then_inc(h_in, 16)
                sp.dma_start(y0[:, :, :], rows_of(dram["y0"], b)).then_inc(y_in, 16)

            def store(b):
                sp.wait_ge(h3_done, done(b))
                sp.dma_start(dram["h3"][bass.ds(b * T, HB), :], h3[:, 0, :]).then_inc(stored, 16)
                sp.dma_start(dram["h3"][bass.ds(b * T + HB, T - HB), :], h3[0:T - HB, 1, :]).then_inc(stored, 16)

            for b in range(3):
                load(b)
            with sp.Fori(1, B - 2) as b:
                load(b + 2)
                store(b - 1)
            for b in range(B - 3, B):
                store(b)
            sp.wait_ge(stored, START + 32 * B)

        @block.gpsimd
        def _(pool):
            pool.memset(minus_half[:, :], -0.5).then_inc(consts, 1)
            for tile in [*kT, *latent]:
                pool.memset(tile[:, :, :], 0.0).then_inc(cleared, 1)
            for tile in pT:
                pool.memset(tile[:, :], 0.0).then_inc(cleared, 1)
            pool.wait_ge(consts, START + 3)
            pool.wait_ge(cleared, START + 7)

            def scale_z(b):
                pool.wait_ge(ve_done, done(b))
                pool.tensor_tensor(rstd[:, :], ve[:, :], minus_half[:, :], ALU.pow).then_inc(rstd_done, 1)

            def scale_c(b):
                pool.wait_ge(c_ve_done, done(b))
                pool.tensor_tensor(c_rstd[:, :], c_ve[:, :], minus_half[:, :], ALU.pow).then_inc(c_rstd_done, 1)

            def rotate_keys(s, n):
                pool.wait_ge(s_ps, done(s - 3))
                pool.wait_ge(turned, done(s))
                for quarter in range(4):
                    if quarter:
                        pool.wait_ge(k_done, START + 4 * s + quarter)
                    rows = slice(32 * quarter, 32 * quarter + 32)
                    pool.tensor_tensor(kT[n % 3][rows, quarter % 2, :], turn_cos[n % 2][rows, 1, :],
                                       turn_sin[n % 2][rows, 1, :], ALU.add).then_inc(k_done, 1)
                pool.wait_ge(k_done, START + 4 * s + 4)

            def normalise(s, n):
                pool.wait_ge(exp_done, START + 4 * s + 4)
                pool.wait_ge(share_done, done(s))
                view = prob[n % 3][:, BK].rearrange("p (o n) -> p o n", o=2)
                pool.tensor_tensor(view, view, share[n % 3][:, 2:4].unsqueeze(2).broadcast_to([HB, 2, SEQ]),
                                   ALU.mult).then_inc(prob_b_done, 1)

            def sequence(b, q, first, last):
                for p in range(PAIRS):
                    s, n = PAIRS * b + p, PAIRS * q + p
                    if p >= SHARE or not first:
                        normalise(s - SHARE, n - SHARE)
                    if p >= SHARE or not first:
                        pool.wait_ge(prob_b_done, done(s - SHARE))
                    if p == 1 and not last:
                        scale_z(b + 1)
                        pool.wait_ge(rstd_done, done(b + 1))
                    rotate_keys(s, n)
                    if p == 3 and not last:
                        scale_c(b + 1)

            scale_z(0)
            scale_c(0)
            run(pool, sequence)
            for p in range(SHARE):
                normalise(PAIRS * B + p - SHARE, p - SHARE)

        @block.scalar
        def _(act):
            def copy_zT(b, q):
                act.wait_ge(qk_ps, START + PAIRS * (b - 1))
                act.wait_ge(zT_ps, done(b))
                act.activation(zT[q][:, :, :], Z_PS[0:DC, :].rearrange("p (c n) -> p c n", c=2), ACT.Copy
                               ).then_inc(zT_done, 1)

            def copy_c(b):
                act.wait_ge(cz_done, START + 2 * b)
                act.wait_ge(c_ps, done(b))
                act.activation(c[:, :, :], Z_PS[0:HB, 0:2 * RANK].rearrange("p (t n) -> p t n", t=2), ACT.Copy
                               ).then_inc(c_done, 1)

            def copy_cT(b, q):
                act.wait_ge(qk_ps, START + PAIRS * (b - 1))
                act.wait_ge(cT_ps, done(b))
                act.activation(cT[q][0:RANK, :], Z_PS[0:RANK, 0:SEQ], ACT.Copy).then_inc(cT_done, 1)

            def keep_latent(b, q):
                act.wait_ge(o_ps, START + PAIRS * (b - 1))
                act.wait_ge(cz_done, START + 2 * b + 2)
                act.activation(latent[q][0:HB, :, :], cz[:, :, :], ACT.Copy).then_inc(latent_done, 1)

            def exps(s, n):
                act.wait_ge(pT_ps, done(s - 3))
                act.wait_ge(minus_done, done(s))
                for tile in range(2):
                    for o in range(2):
                        at, width = 2 * tile + o, HB * (tile + 1)
                        cols = slice(2 * HB * tile + o * width, 2 * HB * tile + (o + 1) * width)
                        act.activation(prob[n % 3][:, cols], S_PS[n % 2][0:HB, cols], ACT.Exp,
                                       bias=minus_top[n % 3][:, at:at + 1], scale=HD ** -0.5,
                                       accum_out=total[n % 3][:, at:at + 1]).then_inc(exp_done, 1)

            def normalise(s, n):
                act.wait_ge(exp_done, START + 4 * s + 4)
                act.wait_ge(share_done, done(s))
                for o in range(2):
                    cols = slice(o * HB, (o + 1) * HB)
                    act.activation(prob[n % 3][:, cols], prob[n % 3][:, cols], ACT.Copy,
                                   scale=share[n % 3][:, o:o + 1]).then_inc(prob_a_done, 1)

            def copy_pT(s, n):
                act.wait_ge(o_ps, done(s - 2))
                act.wait_ge(pT_ps, done(s))
                act.activation(pT[n % 2][0:HB, :], PT_PS[n % 2][0:HB, 0:2 * SEQ + 2 * HB], ACT.Copy
                               ).then_inc(pT_done, 1)

            def copy_oT(s, n):
                act.wait_ge(out_ps, done(s - 2))
                act.wait_ge(o_ps, done(s))
                act.activation(oT[n % 2][:, :], O_PS, ACT.Copy).then_inc(oT_done, 1)

            def sequence(b, q, first, last):
                for p in range(PAIRS):
                    s, n = PAIRS * b + p, PAIRS * q + p
                    if p >= TURN or not first:
                        copy_pT(s - TURN, n - TURN)
                    if p >= VALUE or not first:
                        copy_oT(s - VALUE, n - VALUE)
                    if p == 2 and not last:
                        copy_zT(b + 1, q ^ 1)
                    if p == 3 and not last:
                        copy_c(b + 1)
                    if p == 5 and not last:
                        copy_cT(b + 1, q ^ 1)
                    if p == 1:
                        keep_latent(b, q)
                    if p >= SHARE or not first:
                        normalise(s - SHARE, n - SHARE)
                    if p >= SCORE or not first:
                        exps(s - SCORE, n - SCORE)

            copy_zT(0, 0)
            copy_c(0)
            copy_cT(0, 0)
            run(act, sequence)
            for p in range(VALUE):
                s, n = PAIRS * B + p, p
                if p < TURN:
                    copy_pT(s - TURN, n - TURN)
                copy_oT(s - VALUE, n - VALUE)
                if p < SHARE:
                    normalise(s - SHARE, n - SHARE)
                if p < SCORE:
                    exps(s - SCORE, n - SCORE)

        @block.tensor
        def _(pe):
            pe.wait_ge(consts, START + 3)
            pe.wait_ge(cleared, START + 7)

            def transpose_z(b, values_out):
                pe.wait_ge(oT_done, values_out)
                pe.wait_ge(z_done, START + 2 * b + 2)
                for half in range(2):
                    for t in range(2):
                        mm = pe.transpose(Z_PS[0:DC, half * SEQ + t * HB:half * SEQ + (t + 1) * HB],
                                          z[:, t, half * DC:(half + 1) * DC], ident[0:HB, 0:HB])
                mm.then_inc(zT_ps, 1)

            def make_latent(b, q, values_out):
                pe.wait_ge(oT_done, values_out)
                pe.wait_ge(zT_done, done(b))
                for t in range(2):
                    for c in range(2):
                        mm = pe.matmul(Z_PS[0:HB, t * RANK:(t + 1) * RANK], zT[q][:, c, t * HB:(t + 1) * HB],
                                       wdown[:, c, :], start=(c == 0), stop=(c == 1))
                mm.then_inc(c_ps, 1)

            def transpose_c(b, values_out):
                pe.wait_ge(oT_done, values_out)
                pe.wait_ge(cz_done, START + 2 * b + 2)
                pe.sem_inc(step, 1)
                for t in range(2):
                    mm = pe.transpose(Z_PS[0:RANK, t * HB:(t + 1) * HB], cz[:, t, :], ident[0:HB, 0:HB])
                mm.then_inc(cT_ps, 1)

            def project(b, q, s, n, p):
                pe.wait_ge(turned, done(s - 2))
                pe.wait_ge(zT_done, done(b))
                for c in range(2):
                    pe.matmul(QK_PS[n % 2][:, 0:SEQ], wq[:, c, 128 * p:128 * (p + 1)], zT[q][:, c, :],
                              start=(c == 0), stop=(c == 1))
                pe.wait_ge(cT_done, done(b))
                pe.matmul(QK_PS[n % 2][:, SEQ:2 * SEQ], wk[:, 128 * p:128 * (p + 1)], cT[q][:, :],
                          start=True, stop=True).then_inc(qk_ps, 1)

            def scores(s, n):
                bank, keys = S_PS[n % 2][0:HB, :], kT[n % 3]
                pe.wait_ge(exp_done, START + 4 * (s - 1))
                pe.matmul(bank[:, 0:2 * HB + 2 * SEQ], ident_b[:, :], mask[:, :], start=True, stop=False)
                pe.wait_ge(q_done, done(s))
                pe.wait_ge(k_done, START + 4 * s + 4)
                pe.matmul(bank[:, AK].rearrange("p (o n) -> p o n", o=2), qT[n % 3][:, A], keys[:, :, A],
                          start=False, stop=False)
                pe.matmul(bank[:, BK].rearrange("p (o n) -> p o n", o=2), qT[n % 3][:, BT], keys[:, :, :],
                          start=False, stop=True).then_inc(s_ps, 1)

            def transpose_p(s, n):
                pe.wait_ge(pT_done, done(s - 2))
                pe.wait_ge(prob_a_done, START + 2 * s + 2)
                pe.wait_ge(prob_b_done, done(s))
                for o in range(2):
                    second = 2 * HB + o * SEQ
                    for src, to in ((o * HB, o * SEQ), (second, o * SEQ + HB), (second + HB, 2 * SEQ + o * HB)):
                        mm = pe.transpose(PT_PS[n % 2][0:HB, to:to + HB], prob[n % 3][:, src:src + HB],
                                          ident[0:HB, 0:HB])
                mm.then_inc(pT_ps, 1)

            def values(b, q, s, n):
                pe.wait_ge(oT_done, START + s)
                pe.wait_ge(latent_done, done(b))
                pe.wait_ge(pT_done, done(s))
                for o in range(2):
                    out = O_PS[o * RANK:(o + 1) * RANK, :]
                    pe.matmul(out, latent[q][:, 0, :], pT[n % 2][:, o * SEQ:(o + 1) * SEQ], start=True, stop=False)
                    mm = pe.matmul(out[:, BT], latent[q][:, 1, :],
                                   pT[n % 2][:, 2 * SEQ + o * HB:2 * SEQ + (o + 1) * HB], start=False, stop=True)
                mm.then_inc(o_ps, 1)

            def output(b, s, n, p):
                if p == 0:
                    pe.wait_ge(h3_done, START + b)
                pe.wait_ge(oT_done, done(s))
                for t in range(2):
                    mm = pe.matmul(OUT_PS[:, t * D:(t + 1) * D], oT[n % 2][:, t * HB:(t + 1) * HB], wvo[:, p, :],
                                   start=(p == 0 and t == 0), stop=(p == PAIRS - 1 and t == 1))
                mm.then_inc(out_ps, 1)

            def sequence(b, q, first, last):
                for p in range(PAIRS):
                    s, n = PAIRS * b + p, PAIRS * q + p
                    project(b, q, s, n, p)
                    if p >= SCORE or not first:
                        scores(s - SCORE, n - SCORE)
                    if not first:
                        output(b - 1, s - OUT, n - OUT, p)
                    if p >= TURN or not first:
                        transpose_p(s - TURN, n - TURN)
                    if p in (2, 3, 5) and not last:
                        values_out = START + max(s - VALUE, 0) if first else START + s - VALUE
                        if p == 2:
                            transpose_z(b + 1, values_out)
                        if p == 3:
                            make_latent(b + 1, q ^ 1, values_out)
                        if p == 5:
                            transpose_c(b + 1, values_out)
                    if p == 4 and not last:
                        pe.wait_ge(c_done, done(b + 1))
                    if p == 0:
                        pe.wait_ge(cT_done, done(b))
                    if p >= VALUE:
                        values(b, q, s - VALUE, n - VALUE)
                    elif not first:
                        values(b - 1, q ^ 1, s - VALUE, n - VALUE)

            transpose_z(0, START)
            make_latent(0, 0, START)
            transpose_c(0, START)
            run(pe, sequence)
            for p in range(OUT):
                s, n = PAIRS * B + p, p
                output(B - 1, s - OUT, n - OUT, p)
                if p < SCORE:
                    scores(s - SCORE, n - SCORE)
                if p < TURN:
                    transpose_p(s - TURN, n - TURN)
                if p < VALUE:
                    values(B - 1, 1, s - VALUE, n - VALUE)

        @block.vector
        def _(dve):
            for i in range(2):
                dve.memset(cT[i][RANK:KB, :], 0.0).then_inc(step, 1)
            dve.wait_ge(step, START + 2)
            for i in range(2):
                dve.memset(cT[i][RANK:RANK + 1, :], 1.0).then_inc(consts, 1)

            def measure(b, q):
                dve.wait_ge(h_in, START + 16 * (b + 1))
                dve.wait_ge(y_in, START + 16 * (b + 1))
                dve.wait_ge(res_done, START + b - 1)
                dve.tensor_tensor(h2[q][:, :, :], h1[:, :, :], y0[:, :, :], ALU.add).then_inc(h2_done, 1)
                dve.wait_ge(h2_done, done(b))
                for t in range(2):
                    dve.bn_stats(stats[:, t, :], h2[q][:, t, :]).then_inc(stats_done, 1)
                dve.wait_ge(stats_done, START + 2 * b + 2)
                dve.sem_inc(step, 1)
                for t in range(2):
                    dve.bn_aggr(mv[:, t, :], stats[:, t, :]).then_inc(mv_done, 1)
                dve.wait_ge(mv_done, START + 2 * b + 2)
                dve.tensor_scalar(ve[:, :], mv[:, :, 1], EPS, None, ALU.add).then_inc(ve_done, 1)

            def normalise(b, q):
                dve.wait_ge(zT_ps, START + b)
                dve.wait_ge(rstd_done, done(b))
                for t in range(2):
                    dve.tensor_scalar(z[:, t, :], h2[q][:, t, :], mv[:, t, 0:1], rstd[:, t:t + 1],
                                      ALU.subtract, ALU.mult).then_inc(z_done, 1)

            def measure_latent(b):
                dve.wait_ge(c_done, done(b))
                for t in range(2):
                    dve.bn_stats(c_stats[:, t, :], c[:, t, :]).then_inc(c_stats_done, 1)
                dve.wait_ge(c_stats_done, START + 2 * b + 2)
                dve.sem_inc(step, 1)
                for t in range(2):
                    dve.bn_aggr(c_mv[:, t, :], c_stats[:, t, :]).then_inc(c_mv_done, 1)
                dve.wait_ge(c_mv_done, START + 2 * b + 2)
                dve.tensor_scalar(c_ve[:, :], c_mv[:, :, 1], EPS, None, ALU.add).then_inc(c_ve_done, 1)

            def normalise_latent(b):
                dve.wait_ge(cT_ps, START + b)
                dve.wait_ge(latent_done, START + b)
                dve.wait_ge(c_rstd_done, done(b))
                for t in range(2):
                    dve.tensor_scalar(cz[:, t, :], c[:, t, :], c_mv[:, t, 0:1],
                                      c_rstd[:, t:t + 1], ALU.subtract, ALU.mult).then_inc(cz_done, 1)

            def residual(b, q):
                dve.wait_ge(h3_done, START + b - 1)
                dve.tensor_tensor(res[q][:, :, :], h2[q][:, :, :], bias[:, :].unsqueeze(1).broadcast_to([HB, 2, D]),
                                  ALU.add).then_inc(res_done, 1)

            def turn(s, n):
                dve.wait_ge(q_done, done(s - 2))
                dve.wait_ge(k_done, START + 4 * (s - 1))
                dve.wait_ge(qk_ps, done(s))
                src = QK_PS[n % 2][:, 0:2 * SEQ].rearrange("p (r n) -> p r n", r=2)
                for half in range(2):
                    here, there = slice(64 * half, 64 * half + 64), slice(64 - 64 * half, 128 - 64 * half)
                    dve.tensor_tensor(turn_sin[n % 2][there, :, :], src[here],
                                      sin[here, :].unsqueeze(1).broadcast_to([64, 2, SEQ]), ALU.mult
                                      ).then_inc(step, 1)
                dve.tensor_tensor(turn_cos[n % 2][:, :, :], src, cos[:, :].unsqueeze(1).broadcast_to([128, 2, SEQ]),
                                  ALU.mult).then_inc(turned, 1)

            def rotate_queries(s, n):
                dve.wait_ge(s_ps, done(s - 3))
                dve.wait_ge(turned, done(s))
                dve.tensor_tensor(qT[n % 3][:, :], turn_cos[n % 2][:, 0, :], turn_sin[n % 2][:, 0, :], ALU.add
                                  ).then_inc(q_done, 1)

            def maxima(s, n):
                dve.wait_ge(s_ps, done(s))
                for tile, cols in ((0, AK), (1, BK)):
                    dve.tensor_reduce(top[n % 3][:, 2 * tile:2 * tile + 2],
                                      S_PS[n % 2][0:HB, cols].rearrange("p (o n) -> p o n", o=2), AX.X, ALU.max
                                      ).then_inc(top_done, 1)
                dve.wait_ge(top_done, START + 2 * s + 2)
                dve.tensor_scalar(minus_top[n % 3][:, :], top[n % 3][:, :], -HD ** -0.5, None, ALU.mult
                                  ).then_inc(minus_done, 1)

            def shares(s, n):
                dve.wait_ge(exp_done, START + 4 * s + 4)
                dve.reciprocal(share[n % 3][:, :], total[n % 3][:, :]).then_inc(share_done, 1)

            def add(b, q):
                dve.wait_ge(stored, START + 32 * b)
                dve.wait_ge(res_done, done(b))
                dve.wait_ge(out_ps, START + PAIRS * (b + 1))
                dve.tensor_tensor(h3[:, :, :], OUT_PS.rearrange("p (t n) -> p t n", t=2), res[q][:, :, :],
                                  ALU.add).then_inc(h3_done, 1)

            def sequence(b, q, first, last):
                for p in range(PAIRS):
                    s, n = PAIRS * b + p, PAIRS * q + p
                    if p == 4 and not last:
                        measure_latent(b + 1)
                    turn(s, n)
                    if p >= SHARE or not first:
                        shares(s - SHARE, n - SHARE)
                    if p >= SCORE or not first:
                        maxima(s - SCORE, n - SCORE)
                    rotate_queries(s, n)
                    if p == 0 and not last:
                        measure(b + 1, q ^ 1)
                    if p == 1 and not last:
                        normalise(b + 1, q ^ 1)
                    if p == 3:
                        residual(b, q)
                    if p == 4 and not last:
                        normalise_latent(b + 1)
                    if p == 5 and not first:
                        add(b - 1, q ^ 1)

            measure(0, 0)
            normalise(0, 0)
            measure_latent(0)
            normalise_latent(0)
            run(dve, sequence)
            for p in range(SHARE):
                s, n = PAIRS * B + p, p
                shares(s - SHARE, n - SHARE)
                if p < SCORE:
                    maxima(s - SCORE, n - SCORE)
            add(B - 1, 1)


CHUNKS = 6
CHUNK = N * D // 128 // CHUNKS


def swiglu_weights(nc, used, ctx):
    sem = primed_semaphores(nc, used)
    return {"w1": [ctx.enter_context(nc.sbuf_tensor(f"e1_w1_{i}", [DC, 2, 2 * H1], F32)) for i in range(2)],
            "w2": [ctx.enter_context(nc.sbuf_tensor(f"e1_w2_{i}", [128, H1 // 128, D], F32)) for i in range(2)],
            "in": [sem(f"e1_w_in{i}") for i in range(2)],
            "h3": [ctx.enter_context(nc.sbuf_tensor(f"s_h3{i}", [128, CHUNK], F32)) for i in range(CHUNKS)],
            "h3_in": sem("s_h3_in")}


def chunks(src):
    return src.rearrange("r c -> (r c)").rearrange("(q p n) -> q p n", p=128, q=CHUNKS)


def load_swiglu(sp, w, weights, e, j):
    sp.dma_start(weights["w1"][j][:, :, :], w["e1_w1"][bass.ds(e * D, D), :].rearrange("(c p) n -> p c n", c=2)
                 ).then_inc(weights["in"][j], 16)
    sp.dma_start(weights["w2"][j][:, :, :], w["e1_w2"][bass.ds(e * H1, H1), :].rearrange("(k p) n -> p k n", p=128)
                 ).then_inc(weights["in"][j], 16)


def experts_swiglu(nc, used, w, dram, const, weights):
    w1, w2, w_in = weights["w1"], weights["w2"], weights["in"]
    UNITS = 2 * E1
    BODY = 4
    HC = H1 // 128
    with ExitStack() as ctx:
        def sb(name, shape, dt=F32):
            return ctx.enter_context(nc.sbuf_tensor(f"e1_{name}", shape, dt))

        primed = primed_semaphores(nc, used)

        def sem(name):
            return primed(f"e1_{name}")

        bank = [ctx.enter_context(nc.psum_tensor(f"e1_bank{i}", [128, 512], F32)) for i in range(8)]
        T_PS, VALUE_PS, GATE_PS, Y_PS = bank[0:2], bank[2:4], bank[4:6], bank[6:8]

        def parts(name, shape):
            return [[sb(f"{name}_{part}{i}", shape, F32R) for part in ("high", "low")] for i in range(2)]

        w1_parts = parts("w1", [DC, 2, 2 * H1])
        x = [sb(f"x{i}", [128, CAPT, RW]) for i in range(BODY)]
        xT = parts("xT", [DC, 2, CAPR])
        silu = [sb(f"silu{i}", [128, CAPR]) for i in range(2)]
        gated = [sb(f"gated{i}", [128, HC, CAPR]) for i in range(2)]
        y = [sb(f"y{i}", [128, CAPT, D]) for i in range(2)]
        ident = const["ident"]

        x_in = [sem(f"x_in{i}") for i in range(BODY)]
        xT_ps = sem("xT_ps")
        w_high = sem("w_high")
        w_low = sem("w_low")
        xT_high = sem("xT_high")
        xT_low = sem("xT_low")
        up_ps = sem("up_ps")
        silu_done = sem("silu_done")
        gated_done = sem("gated_done")
        y_ps = sem("y_ps")
        y_done = sem("y_done")
        x_free = sem("x_free")
        step = sem("step")
        scattered = [unprimed_semaphore(nc, used, f"e1_scattered{i}") for i in range(2)]
        block = ctx.enter_context(nc.Block())

        def run(engine, unit):
            for n in range(BODY):
                unit(0, n, n == 0, False)
            with engine.Fori(1, UNITS // BODY - 1) as i:
                for n in range(BODY):
                    unit(i, n, False, False)
            for n in range(BODY):
                unit(UNITS // BODY - 1, n, False, n == BODY - 1)

        @block.sync
        def _(sp):
            def load_x(u, n):
                sp.wait_ge(x_free, START + u - BODY + 1)
                sp.dma_start(x[n][:, :, :], dram["slots1"][bass.ds(u * CAPR, CAPR), :]
                             .rearrange("(t p) c -> p t c", p=128)).then_inc(x_in[n], 16)

            def load_weights(e, j):
                sp.wait_ge(w_low, START + 2 * (e - 1))
                sp.wait_ge(y_ps, START + CAPT * 2 * (e - 1))
                load_swiglu(sp, w, weights, e, j)

            for n in range(BODY):
                load_x(n, n)
            with sp.Fori(1, UNITS // BODY) as i:
                for j in range(2):
                    load_weights(2 * i + j, j)
                    for n in (2 * j, 2 * j + 1):
                        load_x(BODY * i + n, n)
            for i in range(CHUNKS):
                sp.dma_start(weights["h3"][i][:, :], chunks(dram["h3"][0:N, :])[i]).then_inc(weights["h3_in"], 16)

        @block.gpsimd
        def _(pool):
            with pool.Fori(0, UNITS // BODY) as i:
                for n in range(BODY):
                    u, k = BODY * i + n, n % 2
                    for t in range(CAPT):
                        pool.wait_ge(y_done, START + CAPT * u + t + 1)
                        pool.sem_inc(step, 1)
                        pool.indirect_dma_start(
                            dram["y1"],
                            bass.IndirectOffsetOnAxis(ap=x[n][:, t, D + 2 + k:D + 3 + k].bitcast(I32), axis=0),
                            y[n % 2][:, t, :], None, bounds_check=2 * NP - 1, oob_is_err=False
                        ).then_inc(scattered[n % 2], 16)
                    if n:
                        pool.wait_ge(scattered[(n - 1) % 2], 16 * CAPT * (2 * i + (n - 1) // 2 + 1))
                        pool.sem_inc(x_free, 1)
                pool.wait_ge(scattered[1], 16 * CAPT * (2 * i + 2))
                pool.sem_inc(x_free, 1)

        @block.scalar
        def _(act):
            def high_xT(u, n):
                act.wait_ge(up_ps, START + HC * (u - 1))
                for c in range(2):
                    act.wait_ge(xT_ps, START + 2 * u + c + 1)
                    act.activation(xT[n % 2][0][:, c, :], T_PS[c][0:DC, 0:CAPR], ACT.Copy).then_inc(xT_high, 1)

            def high_weights(e, j, loaded, c):
                act.wait_ge(up_ps, START + HC * 2 * (e - 1))
                act.wait_ge(w_in[j], loaded)
                act.activation(w1_parts[j][0][:, c, :], w1[j][:, c, :], ACT.Copy).then_inc(w_high, 1)

            def unit(i, n, first, last):
                u = BODY * i + n
                for k in range(HC):
                    act.wait_ge(gated_done, START + HC * u + k - 1)
                    act.wait_ge(up_ps, START + HC * u + k + 1)
                    act.activation(silu[k % 2][:, :], GATE_PS[k % 2][:, 0:CAPR], ACT.Silu).then_inc(silu_done, 1)
                    if n % 2 and k < 2 and not last:
                        high_weights(2 * i + (n + 1) // 2, (n + 1) // 2 % 2, START + 32 * (i + 1 + n // 3), k)
                    if k == HC - 2 and not last:
                        high_xT(u + 1, n + 1)

            for c in range(2):
                high_weights(0, 0, START + 32, c)
            high_xT(0, 0)
            run(act, unit)

        @block.tensor
        def _(pe):
            def transposes(u, n, in_):
                pe.wait_ge(x_in[n % BODY], in_)
                for c in range(2):
                    pe.wait_ge(xT_low, START + 2 * u + c - 1)
                    for t in range(CAPT):
                        mm = pe.transpose(T_PS[c][0:DC, t * 128:(t + 1) * 128], x[n % BODY][:, t, c * DC:(c + 1) * DC],
                                          ident)
                    mm.then_inc(xT_ps, 1)

            def up(u, n, k):
                pe.wait_ge(gated_done, START + HC * u + k - 1)
                pe.wait_ge(xT_low, START + 2 * u + 2)
                for part, ps in enumerate((GATE_PS, VALUE_PS)):
                    at = H1 * (1 - part) + 128 * k
                    for c in range(2):
                        for a, b in PARTS:
                            mm = pe.matmul(ps[k % 2][:, 0:CAPR], w1_parts[n // 2][a][:, c, at:at + 128],
                                           xT[n % 2][b][:, c, :], start=(c == 0 and (a, b) == PARTS[0]),
                                           stop=(c == 1 and (a, b) == PARTS[-1]))
                mm.then_inc(up_ps, 1)

            def down(u, n, t):
                pe.wait_ge(y_done, START + CAPT * u + t - 1)
                pe.wait_ge(gated_done, START + HC * (u + 1))
                bank_ = Y_PS[(CAPT * n + t) % 2]
                for k in range(HC):
                    mm = pe.matmul(bank_[:, 0:D], gated[n % 2][:, k, t * 128:(t + 1) * 128], w2[n // 2][:, k, :],
                                   start=(k == 0), stop=(k == HC - 1))
                mm.then_inc(y_ps, 1)

            def unit(i, n, first, last):
                u = BODY * i + n
                if n % 2 == 0:
                    pe.wait_ge(w_low, START + 2 * (2 * i + n // 2 + 1))
                for k in range(HC):
                    up(u, n, k)
                    if k == HC - 2 and not last:
                        transposes(u + 1, n + 1, START + 16 * (i + (2 if n == BODY - 1 else 1)))
                    if k and not first:
                        down(u - 1, (n - 1) % BODY, k - 1)

            transposes(0, 0, START + 16)
            run(pe, unit)
            for t in range(CAPT):
                down(UNITS - 1, BODY - 1, t)

        @block.vector
        def _(dve):
            def scale_y(u, n, t):
                dve.wait_ge(x_free, START + u - 1)
                dve.wait_ge(y_ps, START + CAPT * u + t + 1)
                dve.tensor_scalar(y[n % 2][:, t, :], Y_PS[(CAPT * n + t) % 2][:, 0:D],
                                  x[n][:, t, D + n % 2:D + n % 2 + 1], None, ALU.mult).then_inc(y_done, 1)

            def low_xT(u, n):
                dve.wait_ge(up_ps, START + HC * (u - 1))
                for c in range(2):
                    high, low = xT[n % 2]
                    dve.wait_ge(xT_high, START + 2 * u + c + 1)
                    dve.tensor_tensor(low[:, c, :], T_PS[c][0:DC, 0:CAPR], high[:, c, :].bitcast(F32), ALU.subtract
                                      ).then_inc(xT_low, 1)

            def low_weights(e, j, c):
                high, low = w1_parts[j]
                dve.wait_ge(up_ps, START + HC * 2 * (e - 1))
                dve.wait_ge(w_high, START + 2 * e + c + 1)
                dve.tensor_tensor(low[:, c, :], w1[j][:, c, :], high[:, c, :].bitcast(F32), ALU.subtract
                                  ).then_inc(w_low, 1)

            def unit(i, n, first, last):
                u = BODY * i + n
                for k in range(HC):
                    dve.wait_ge(y_ps, START + CAPT * (u - 1))
                    dve.wait_ge(silu_done, START + HC * u + k + 1)
                    dve.tensor_tensor(gated[n % 2][:, k, :], VALUE_PS[k % 2][:, 0:CAPR], silu[k % 2][:, :], ALU.mult
                                      ).then_inc(gated_done, 1)
                    if k and not first:
                        scale_y(u - 1, (n - 1) % BODY, k - 1)
                    if n % 2 and k < 2 and not last:
                        low_weights(2 * i + (n + 1) // 2, (n + 1) // 2 % 2, k)
                    if k == HC - 2 and not last:
                        low_xT(u + 1, n + 1)

            for c in range(2):
                low_weights(0, 0, c)
            low_xT(0, 0)
            run(dve, unit)
            for t in range(CAPT):
                scale_y(UNITS - 1, BODY - 1, t)


def combine(nc, used, w, dram, weights, out):
    with ExitStack() as ctx:
        primed = primed_semaphores(nc, used)
        first, second = ([ctx.enter_context(nc.sbuf_tensor(f"s_{n}{i}", [128, CHUNK], F32)) for i in range(CHUNKS)]
                         for n in ("first", "second"))
        h3 = weights["h3"]
        loaded = [primed(f"s_loaded{i}") for i in range(CHUNKS)]
        summed = primed("s_summed")
        final = primed("s_final")
        stored = primed("s_stored")
        block = ctx.enter_context(nc.Block())

        @block.sync
        def _(sp):
            for i in range(CHUNKS):
                for tiles, src in ((first, dram["y1"][0:N, :]), (second, dram["y1"][NP:NP + N, :])):
                    sp.dma_start(tiles[i][:, :], chunks(src)[i]).then_inc(loaded[i], 16)
            for i in range(CHUNKS):
                sp.wait_ge(final, START + i + 1)
                sp.dma_start(chunks(out.rearrange("b t c -> (b t) c"))[i], first[i][:, :]).then_inc(stored, 16)
            sp.wait_ge(stored, START + 16 * CHUNKS)

        @block.vector
        def _(dve):
            dve.wait_ge(weights["h3_in"], START + 16 * CHUNKS)
            for i in range(CHUNKS):
                dve.wait_ge(loaded[i], START + 32)
                dve.tensor_tensor(first[i][:, :], first[i][:, :], second[i][:, :], ALU.add).then_inc(summed, 1)
                dve.wait_ge(summed, START + i + 1)
                dve.tensor_tensor(first[i][:, :], first[i][:, :], h3[i][:, :], ALU.add).then_inc(final, 1)


def build(nc, w, out):
    with ExitStack() as ctx:
        def scratch(name, rows, width=D):
            return nc.dram_tensor(name, [rows, width], F32).ap()

        dram = {"h0": scratch("h0", N + 1), "h1": scratch("h1", NP), "h3": scratch("h3", NP),
                "slots0": scratch("slots0", ROWS0, RW), "slots1": scratch("slots1", ROWS1, RW),
                "y0": scratch("y0", NP), "y1": scratch("y1", 2 * NP)}
        const = {}
        for name, shape, dt in (("ident", [128, 128], F32), ("ones", [128, 128], BF16), ("before", [128, 128], BF16),
                                ("expert_no", [128, 8], F32), ("tile_rows", [1, TILES], F32),
                                ("tile_no", [1, TILES0], F32)):
            const[name] = ctx.enter_context(nc.sbuf_tensor(name, shape, dt))[:, :]
        made = {name: ctx.enter_context(nc.sbuf_tensor(name, [1, TILES0], I32))[:, :]
                for name in ("tile_row", "tile_expert")}
        used = []
        causal = causal_weights(ctx, nc)
        embed_patches(nc, used, w, dram, const, causal)
        const.update(made)
        attend_squared(nc, used, w, dram, const)
        with ExitStack() as layer:
            weights = gelu_weights(nc, used, layer)
            dispatch(nc, used, w, dram, const, 0, lambda sp: load_gelu(sp, w, weights),
                     lambda act: high_gelu(act, weights), lambda dve, g: low_gelu(dve, weights, g))
            experts_gelu(nc, used, w, dram, const, weights)
        clear_semaphores(nc, used)
        attend_causal(nc, used, w, dram, const, causal)
        weights = swiglu_weights(nc, used, ctx)
        dispatch(nc, used, w, dram, const, 1, lambda sp: [load_swiglu(sp, w, weights, e, e) for e in range(2)])
        experts_swiglu(nc, used, w, dram, const, weights)
        combine(nc, used, w, dram, weights, out)


def _layouts(a):
    BF = mybir.dt.np(BF16)

    def f(name):
        return np.asarray(a[name])

    x = f("x")[:, :, :GRID * PATCH, :GRID * PATCH].reshape(B, 3, GRID, PATCH, GRID, PATCH)
    rows = np.zeros((B, 3 * KP, IMG), np.float32)
    rows[:, :300, 1:] = x.transpose(0, 1, 3, 5, 2, 4).reshape(B, 300, IMG - 1)
    rows[:, 300, 1:] = 1
    rows[:, 301, 0] = 1
    tok_w = np.zeros((3 * KP, D), np.float32)
    tok_w[:300] = f("L0_tok_W").T
    tok_w[300] = f("L0_tok_b")
    tok_w[301] = f("L0_tok_cls").reshape(-1)

    def halves_first(m):
        return m.reshape(-1, HEADS // 2, 2, 2, HD // 2).swapaxes(2, 3).reshape(m.shape)

    inv = np.float32(1) / np.float32(10000) ** (np.arange(0, HD, 2, dtype=np.float32) / np.float32(HD))
    angle = np.tile(inv[:, None] * np.arange(SEQ, dtype=np.float32)[None], (4, 1)).astype(np.float32)
    sign = np.repeat(np.array([1, -1], np.float32), HD)[:, None]
    rows80 = np.arange(HB)[:, None]
    mask = np.concatenate([np.where(np.arange(HB)[None] <= rows80, 0, -1e30)] * 2
                          + [np.where(np.arange(SEQ)[None] <= rows80 + HB, 0, -1e30)] * 2, 1)
    out = {
        "patches": rows.reshape(B, 3, KP, IMG).transpose(0, 2, 1, 3).reshape(B, KP, 3 * IMG),
        "tok_w": tok_w.reshape(3, KP, D).transpose(1, 0, 2).reshape(KP, 3 * D),
        "tok_gamma": np.broadcast_to(f("L0_tok_gamma"), (IMG, D)),
        "tok_beta": np.broadcast_to(f("L0_tok_beta"), (IMG, D)),
        "txt": f("txt"),
        "ident": np.eye(128, dtype=np.float32),
        "attn0_w": np.concatenate([f(f"L0_attn_W{n}_w").T for n in "uqkv"], 1),
        "attn0_b": np.concatenate([f(f"L0_attn_W{n}_b") for n in "uqkv"])[None],
        "attn0_ln": np.stack([f("L0_attn_ln_gamma"), f("L0_attn_ln_beta")], 1),
        "attn0_wo": f("L0_attn_Wo_w").T,
        "attn0_bo": f("L0_attn_Wo_b")[None],
        "ones": np.ones((128, 128), BF),
        "before": np.triu(np.ones((128, 128), BF), 1),
        "expert_no": np.broadcast_to(np.arange(8, dtype=np.float32), (128, 8)),
        "tile_rows": np.arange(TILES, dtype=np.float32)[None] * 128,
        "tile_no": np.arange(TILES0, dtype=np.float32)[None],
        "gate0_w": f("L0_ffn_gate_w"),
        "gate0_b": f("L0_ffn_gate_b")[None],
        "gate0_centre": f("L0_ffn_gate_center")[None],
        "e0_w1": f("L0_ffn_w1").transpose(1, 0, 2).reshape(D, E0 * H0),
        "e0_b1": f("L0_ffn_b1").reshape(1, E0 * H0),
        "e0_w2": f("L0_ffn_w2"),
        "e0_b2": f("L0_ffn_b2"),
        "wq": halves_first(f("L1_attn_Wq")),
        "wdown": f("L1_attn_Wdown"),
        "up_k": halves_first(f("L1_attn_Wup")[:, :HEADS * HD]),
        "up_vT": f("L1_attn_Wup")[:, HEADS * HD:].T,
        "attn1_ln": np.tile(np.stack([f("L1_attn_ln_g"), f("L1_attn_ln_b")], 1), (2, 1)),
        "wo1": f("L1_attn_Wo"),
        "bo": np.broadcast_to(f("L1_attn_bo"), (HB, D)),
        "cos": np.cos(angle),
        "sin": np.sin(angle) * sign,
        "mask": mask.astype(BF),
        "ident_b": np.eye(HB, dtype=BF),
        "gate1_w": f("L1_ffn_Wg"),
        "e1_w1": f("L1_ffn_W1").reshape(E1 * D, 2 * H1),
        "e1_w2": f("L1_ffn_W2").reshape(E1 * H1, D),
    }
    return {k: np.ascontiguousarray(v) for k, v in out.items()}


def kernel(**inputs):
    import concourse.bacc as _bacc
    from concourse.bass_utils import run_bass_kernel_spmd as _run

    nc = _bacc.Bacc("TRN2", target_bir_lowering=False, num_devices=1)
    arrays = {f"in_{k}": v for k, v in _layouts(inputs).items()}
    w = {k[3:]: nc.dram_tensor(k, v.shape, mybir.dt.from_np(v.dtype), kind="ExternalInput").ap()
         for k, v in arrays.items()}
    out = nc.dram_tensor("out_0", (B, T, D), F32, kind="ExternalOutput").ap()
    build(nc, w, out)
    r = _run(nc, [arrays], core_ids=[0])
    return r.results[0]["out_0"]
```
